# Optimizing a Trainium2 kernel written in Bass

```python
import numpy as np
import jax
import jax.numpy as jnp

def _softmax(x, axis=-1):
    return jax.nn.softmax(x, axis=axis)

def _gelu(x):
    return jax.nn.gelu(x, approximate=True)

def _silu(x):
    return jax.nn.silu(x)

def _sigmoid(x):
    return jax.nn.sigmoid(x)

def _layernorm(x, axis=-1, eps=1e-05):
    m = jnp.mean(x, axis=axis, keepdims=True)
    v = jnp.var(x, axis=axis, keepdims=True)
    return (x - m) / jnp.sqrt(v + eps)

def _scatter_add(tgt, idx, src, axis=0):
    return tgt.at[idx].add(src)

def _segment_sum(src, seg, n):
    return jax.ops.segment_sum(src, seg, n)
kernel_name = 'mk_adaln_ffn_d2_seqx_r2_24ee36'

def setup_inputs(seed: int=0):
    np.random.seed(seed)
    _w = jnp.asarray

    def _rec_inputs():
        import jax
        import jax.numpy as jnp
        _rk = jax.random.key(seed)
        x = -1.528e-05 + 0.9999 * jax.random.normal(jax.random.fold_in(_rk, 1), (8, 1024, 512), jnp.float32)
        _lenS = 1024 - jax.random.randint(jax.random.fold_in(_rk, 7), (8,), 0, max(1, 1024 // 4) + 1, jnp.int32)
        _lenS2 = 1024 - jax.random.randint(jax.random.fold_in(_rk, 8), (8,), 0, max(1, 1024 // 4) + 1, jnp.int32)
        cond_1024 = -0.00608245 + 1.00131 * jax.random.normal(jax.random.fold_in(_rk, 11), (8, 512), jnp.float32)
        return (x, cond_1024)
    x, cond_1024 = _rec_inputs()

    def _L0_cond_setup():
        import jax, jax.numpy as jnp
        import numpy as np
        LATENT = 512
        key = jax.random.key(seed)
        k1, k2, k3, k4 = jax.random.split(key, 4)
        B, T, D = (64, 256, LATENT)
        h_t = jax.random.normal(k1, (B, D), dtype=jnp.float32)
        z = jax.random.normal(k2, (B, T, D), dtype=jnp.float32)
        bound = 1.0 / np.sqrt(2 * D)
        W = jax.random.uniform(k3, (D, 2 * D), minval=-bound, maxval=bound, dtype=jnp.float32)
        b = jax.random.uniform(k4, (D,), minval=-bound, maxval=bound, dtype=jnp.float32)
        alpha = jnp.full((D,), 0.1, dtype=jnp.float32)
        return {'h_t': h_t, 'z': z, 'W': W, 'b': b, 'alpha': alpha}
    _L0_cond_all = _L0_cond_setup()
    _L0_cond_in = {k: v for k, v in _L0_cond_all.items() if k in ('W', 'b', 'alpha')}
    del _L0_cond_all

    def _L0_ffn_setup():
        import jax, jax.numpy as jnp
        import numpy as np
        EPS = 1e-05
        key = jax.random.key(seed)
        kx, kw, kb = jax.random.split(key, 3)
        B, S, K, N = (8, 4096, 512, 512)
        x = jax.random.normal(kx, (B, S, K), dtype=jnp.float32)
        W = jax.random.normal(kw, (N, K), dtype=jnp.float32) * 0.02
        weight_scale = jnp.maximum(jnp.max(jnp.abs(W), axis=1, keepdims=True) / 127.0, EPS)
        weight_int8 = jnp.clip(jnp.round(W / weight_scale), -128, 127).astype(jnp.int8)
        bias = jax.random.normal(kb, (N,), dtype=jnp.float32) * 0.01
        return {'x': x, 'weight_int8': weight_int8, 'weight_scale': weight_scale, 'bias': bias}
    _L0_ffn_all = _L0_ffn_setup()
    _L0_ffn_in = {k: v for k, v in _L0_ffn_all.items() if k in ('weight_int8', 'weight_scale', 'bias')}
    del _L0_ffn_all

    def _L1_cond_setup():
        import jax, jax.numpy as jnp
        import numpy as np
        IN_FEATURES = 512
        OUT_FEATURES = 512
        BATCH = 32
        SEQ = 512
        EPS = 1e-08
        key = jax.random.key(seed)
        k1, k2, k3 = jax.random.split(key, 3)
        Efou = jax.random.normal(k1, (BATCH, SEQ, IN_FEATURES), dtype=jnp.float32)
        y = jax.random.normal(k2, (BATCH, IN_FEATURES), dtype=jnp.float32)
        weight = jax.random.normal(k3, (IN_FEATURES, OUT_FEATURES), dtype=jnp.float32)
        return {'Efou': Efou, 'y': y, 'weight': weight}
    _L1_cond_all = _L1_cond_setup()
    _L1_cond_in = {k: v for k, v in _L1_cond_all.items() if k in ('weight',)}
    del _L1_cond_all

    def _L1_ffn_setup():
        import jax, jax.numpy as jnp
        import numpy as np
        B, S, H, FF, E = (4, 2048, 512, 2048, 8)
        EPS = 1e-05
        key = jax.random.key(seed)
        ks = jax.random.split(key, 8)
        std = 0.02
        return {'x': jax.random.normal(ks[0], (B, S, H), jnp.float32), 'norm_weight': jnp.ones((H,), jnp.float32), 'router_w': jax.random.normal(ks[1], (E, H), jnp.float32) * std, 'router_b': jnp.zeros((E,), jnp.float32), 'fc1_w': jax.random.normal(ks[2], (E, FF, H), jnp.float32) * std, 'fc1_b': jnp.zeros((E, FF), jnp.float32), 'fc2_w': jax.random.normal(ks[3], (E, H, FF), jnp.float32) * std, 'fc2_b': jnp.zeros((E, H), jnp.float32)}
    _L1_ffn_all = _L1_ffn_setup()
    _L1_ffn_in = {k: v for k, v in _L1_ffn_all.items() if k in ('norm_weight', 'router_w', 'router_b', 'fc1_w', 'fc1_b', 'fc2_w', 'fc2_b')}
    del _L1_ffn_all
    return {'x': x, 'cond_1024': cond_1024, 'L0_cond_W': _L0_cond_in['W'], 'L0_cond_b': _L0_cond_in['b'], 'L0_cond_alpha': _L0_cond_in['alpha'], 'L0_ffn_weight_int8': _L0_ffn_in['weight_int8'], 'L0_ffn_weight_scale': _L0_ffn_in['weight_scale'], 'L0_ffn_bias': _L0_ffn_in['bias'], 'L1_cond_weight': _L1_cond_in['weight'], 'L1_ffn_norm_weight': _L1_ffn_in['norm_weight'], 'L1_ffn_router_w': _L1_ffn_in['router_w'], 'L1_ffn_router_b': _L1_ffn_in['router_b'], 'L1_ffn_fc1_w': _L1_ffn_in['fc1_w'], 'L1_ffn_fc1_b': _L1_ffn_in['fc1_b'], 'L1_ffn_fc2_w': _L1_ffn_in['fc2_w'], 'L1_ffn_fc2_b': _L1_ffn_in['fc2_b']}

def reference(x, cond_1024, L0_cond_W, L0_cond_b, L0_cond_alpha, L0_ffn_weight_int8, L0_ffn_weight_scale, L0_ffn_bias, L1_cond_weight, L1_ffn_norm_weight, L1_ffn_router_w, L1_ffn_router_b, L1_ffn_fc1_w, L1_ffn_fc1_b, L1_ffn_fc2_w, L1_ffn_fc2_b):
    import jax
    import jax.numpy as jnp

    def _L0_cond_ref(h_t, z, W, b, alpha):
        import jax, jax.numpy as jnp
        import numpy as np
        LATENT = 512
        D = h_t.shape[-1]
        Wh = W[:, :D]
        Wz = W[:, D:]
        leak = 1.0 - alpha

        def step(h, z_t):
            gate = jax.nn.sigmoid(h @ Wh.T + z_t @ Wz.T + b)
            h_new = jnp.tanh(h * leak + gate * z_t)
            return (h_new, h_new)
        _, hs = jax.lax.scan(step, h_t, jnp.swapaxes(z, 0, 1))
        return jnp.swapaxes(hs, 0, 1)

    def _L0_ffn_ref(x, weight_int8, weight_scale, bias):
        import jax, jax.numpy as jnp
        import numpy as np
        EPS = 1e-05
        B, S, K = x.shape
        x2 = x.reshape(-1, K)
        x_scale = jnp.maximum(jnp.abs(x2).max() / 127.0, EPS)
        x_int8 = jnp.clip(jnp.round(x2 / x_scale), -128, 127).astype(jnp.int8)
        acc_i32 = jax.lax.dot_general(x_int8, weight_int8.T, dimension_numbers=(((1,), (0,)), ((), ())), preferred_element_type=jnp.int32)
        out = acc_i32.astype(jnp.float32) * x_scale * weight_scale.T
        out = out + bias
        return out.reshape(B, S, -1)

    def _L1_cond_ref(Efou, y, weight):
        import jax, jax.numpy as jnp
        import numpy as np
        IN_FEATURES = 512
        OUT_FEATURES = 512
        BATCH = 32
        SEQ = 512
        EPS = 1e-08
        scale = 1.0 / np.sqrt(np.float32(weight.shape[0]))
        ys = y * scale
        d = jax.lax.rsqrt(jnp.einsum('bi,io->bo', ys * ys, weight * weight) + EPS)
        out = jnp.einsum('bsi,io->bso', Efou * ys[:, None, :], weight) * d[:, None, :]
        return out

    def _L1_ffn_ref(x, norm_weight, router_w, router_b, fc1_w, fc1_b, fc2_w, fc2_b):
        import jax, jax.numpy as jnp
        import numpy as np
        B, S, H, FF, E = (4, 2048, 512, 2048, 8)
        EPS = 1e-05
        b, s, h = x.shape
        T = b * s
        e = router_w.shape[0]
        cap = T // e
        x_flat = x.reshape(T, h)
        xn = x_flat * jax.lax.rsqrt(jnp.mean(x_flat * x_flat, axis=-1, keepdims=True) + EPS) * norm_weight
        logits = xn @ router_w.T + router_b
        probs = jax.nn.softmax(logits, axis=-1)
        gates, idx = jax.lax.top_k(probs.T, cap)
        xe = xn[idx]
        hmid = jnp.einsum('ech,efh->ecf', xe, fc1_w) + fc1_b[:, None, :]
        hmid = jax.nn.gelu(hmid, approximate=False)
        ye = jnp.einsum('ecf,ehf->ech', hmid, fc2_w) + fc2_b[:, None, :]
        flat_idx = idx.reshape(-1)
        weighted = (ye * gates[..., None]).reshape(-1, h)
        out = jnp.zeros((T, h), x.dtype).at[flat_idx].add(weighted)
        gate_sums = jnp.zeros((T, 1), x.dtype).at[flat_idx].add(gates.reshape(-1, 1))
        out = out / jnp.maximum(gate_sums, 1e-09)
        return out.reshape(b, s, h)
    x = x + _L0_ffn_ref(_L0_cond_ref(cond_1024, x, L0_cond_W, L0_cond_b, L0_cond_alpha), L0_ffn_weight_int8, L0_ffn_weight_scale, L0_ffn_bias)
    x = x + _L1_ffn_ref(_L1_cond_ref(x, cond_1024, L1_cond_weight), L1_ffn_norm_weight, L1_ffn_router_w, L1_ffn_router_b, L1_ffn_fc1_w, L1_ffn_fc1_b, L1_ffn_fc2_w, L1_ffn_fc2_b)
    return x

_drawn_inputs = setup_inputs


def setup_inputs(seed=0):
    import zlib

    import numpy as np

    out = dict(_drawn_inputs(seed))
    spreads = {'L0_cond_alpha': (0.10000000149011612, 0.6),
     'L1_ffn_norm_weight': (1.0, 0.2),
     'L1_ffn_router_b': (0.0, 0.1),
     'L1_ffn_fc1_b': (0.0, 0.1),
     'L1_ffn_fc2_b': (0.0, 0.1)}
    factors = {'L0_cond_b': 8.0}
    for name, (base, spread) in spreads.items():
        noise = np.random.default_rng([zlib.crc32(name.encode()), seed]).standard_normal(out[name].shape)
        drawn = base * np.exp(spread * noise) if base else spread * noise
        out[name] = jnp.asarray(drawn.astype(out[name].dtype))
    for name, factor in factors.items():
        out[name] = (out[name] * factor).astype(out[name].dtype)
    return out
```

```python
import concourse.bass as bass
from concourse import mybir
from contextlib import ExitStack


def adaln_ffn_kernel(nc, x_scan, x_feat, cond_t, wh_t, wz_t, gate_bias, alpha, q_weight_t, q_vecs,
                     mod_w, mod_w_t, norm_w_t, norm_w_row, router_t, router_b, fc1_t, fc1_b,
                     fc2_t, fc2_b, out):
    f32, f16, bf16 = mybir.dt.float32, mybir.dt.float16, mybir.dt.bfloat16
    i32, u32 = mybir.dt.int32, mybir.dt.uint32
    ALU = mybir.AluOpType
    ACT = mybir.ActivationFunctionType
    AX = mybir.AxisListType

    P = 128
    B, S, H = 8, 1024, 512
    K = H // P
    T = B * S
    NT = T // P
    E, FF = 8, 2048
    F = FF // P
    CAP = T // E
    CT = CAP // P
    SB = 16
    NBLK = S // SB
    TT = 512
    SUB = TT // P
    ROUND = 1.5 * 2.0 ** 23
    EXP_ONE = 1 << 23
    BITS = 30
    GATHER = 5

    ABSMAX = bass.bass_isa.ReduceOp.absmax

    def bc(ap, shape):
        return ap.to_broadcast(shape)

    with ExitStack() as ctx:
        def sem(name):
            return ctx.enter_context(nc.semaphore(name))

        ARENA = 53200
        arena = ctx.enter_context(nc.sbuf_tensor("arena", [P, ARENA], f32))
        banks = [ctx.enter_context(nc.psum_tensor(f"bank{n}", [P, 512], f32)) for n in range(8)]

        class Region:

            def __init__(self, at):
                self.at = at

            def take(self, words, dt=f32):
                lo, self.at = self.at, self.at + words
                assert self.at <= ARENA, self.at
                view = arena[:, lo:self.at]
                return view if dt == f32 else view.bitcast(dt)

        keep = Region(0)
        ident = keep.take(P)
        small = keep.take(64)
        ones_f = keep.take(P)
        ones_b = keep.take(P // 2, bf16)
        idx_all = keep.take(E * CT, i32).rearrange("p (e c) -> p e c", e=E)
        w_all = keep.take(E * CT).rearrange("p (e c) -> p e c", e=E)
        EXPERTS_AT = keep.at
        d_rows = keep.take(B * H)
        d_rows = d_rows.rearrange("p (b o) -> p b o", b=B)
        mod_sb = keep.take(K * H).rearrange("p (k o) -> p k o", k=K)
        route_sb = keep.take(K * P).rearrange("p (k n) -> p k n", k=K)
        qw_sb = keep.take(K * H // 2, bf16).rearrange("p (k o) -> p k o", k=K)
        ys = keep.take(K * B).rearrange("p (k b) -> p k b", k=K)
        probs = keep.take(NT * E)
        rstd = keep.take(NT)
        rb_sb = keep.take(E)
        vecs = keep.take(4 * K)
        keep_nw = keep.take(H)
        AFTER_KEEP = keep.at

        scan = Region(AFTER_KEEP)
        hs = scan.take(B * K * S).rearrange("p (b k t) -> p b k t", b=B, k=K)
        AFTER_HS = scan.at
        wh_hi = scan.take(K * H // 2, f16).rearrange("p (k o) -> p k o", k=K)
        wh_lo = scan.take(K * H // 2, f16).rearrange("p (k o) -> p k o", k=K)
        wz = scan.take(K * H).rearrange("p (k o) -> p k o", k=K)
        xblk = [scan.take(SB * K * B).rearrange("p (t k b) -> p t k b", t=SB, k=K) for _ in range(2)]
        hring = [scan.take(SB * K * B).rearrange("p (t k b) -> p t k b", t=SB, k=K) for _ in range(2)]
        h_hi = scan.take(K * B // 2, f16).rearrange("p (k b) -> p k b", k=K)
        h_lo = scan.take(K * B // 2, f16).rearrange("p (k b) -> p k b", k=K)
        gate = scan.take(K * B)
        gz = scan.take(K * B)
        hv = scan.take(K * B)
        lh = scan.take(K * B)
        leak = scan.take(K * B)
        h0 = scan.take(K * B).rearrange("p (k b) -> p k b", k=K)
        gb_row = scan.take(H)
        hmax = scan.take(NBLK)
        nw_bc = keep_nw
        pro = Region(AFTER_KEEP)
        wh = pro.take(K * H).rearrange("p (k o) -> p k o", k=K)
        mod_sq = pro.take(K * H).rearrange("p (k o) -> p k o", k=K)
        mod_t = pro.take(K * H).rearrange("p (k o) -> p k o", k=K)
        ysq = pro.take(K * B).rearrange("p (k b) -> p k b", k=K)
        ysq_wide = pro.take(K * B * P).rearrange("p (k b n) -> p k b n", k=K, b=B)
        d_t = pro.take(K * B).rearrange("p (k b) -> p k b", k=K)
        nw_t = pro.take(K)
        rt_t = pro.take(K * E).rearrange("p (k e) -> p k e", k=K)
        rnw = pro.take(K * E).rearrange("p (k e) -> p k e", k=K)
        g_t = pro.take(K * B * E).rearrange("p (k b e) -> p k b e", k=K, b=B)
        qw_words = pro.take(K * H // 4, i32)
        qw_i8 = qw_words.bitcast(mybir.dt.int8).rearrange("p (k o) -> p k o", k=K)
        alpha_sb = pro.take(K)

        dense = Region(AFTER_HS)
        xt = [dense.take(K * TT).rearrange("p (k t) -> p k t", k=K) for _ in range(2)]
        q_sb = dense.take(K * TT // 2, bf16).rearrange("p (k t) -> p k t", k=K)
        ffn = [dense.take(TT) for _ in range(2)]
        wb = dense.take(K * H).rearrange("p (k o) -> p k o", k=K)
        yrow = [dense.take(H) for _ in range(2)]
        orow = [dense.take(H) for _ in range(2)]
        sq_out = dense.take(H)
        ss = dense.take(8)

        pick = Region(AFTER_KEEP)
        p_et = pick.take(E * NT).rearrange("p (e t) -> p e t", e=E)
        flags = pick.take(E * NT // 2, bf16).rearrange("p (e t) -> p e t", e=E)
        flags2 = pick.take(E * NT // 2, bf16).rearrange("p (e t) -> p e t", e=E)
        above = pick.take(E * NT).rearrange("p (e t) -> p e t", e=E)
        rank = pick.take(E * NT).rearrange("p (e t) -> p e t", e=E)
        cum = pick.take(E * NT).rearrange("p (e t) -> p e t", e=E)
        tot = pick.take(E * NT).rearrange("p (e t) -> p e t", e=E)
        wsel = pick.take(E * NT).rearrange("p (e t) -> p e t", e=E)
        wres = pick.take(E * NT).rearrange("p (e t) -> p e t", e=E)
        slot_i = pick.take(E * NT, i32).rearrange("p (e t) -> p e t", e=E)
        part_i = pick.take(E * NT, i32).rearrange("p (e t) -> p e t", e=E)
        slot_lo = pick.take(E * NT // 2, bf16).rearrange("p (e t) -> p e t", e=E)
        slot_hi = pick.take(E * NT // 2, bf16).rearrange("p (e t) -> p e t", e=E)
        vals = pick.take(E * NT * GATHER // 2 + E, bf16)[:, 0:E * NT * GATHER].rearrange(
            "p (e t v) -> p e t v", e=E, v=GATHER)
        ones64 = pick.take(NT)
        tri = pick.take(P // 2, bf16)
        onehot = [pick.take(NT * P // 2, bf16).rearrange("p (t n) -> p t n", t=NT) for _ in range(2)]
        hi_hot = pick.take(NT * CT // 2, bf16).rearrange("p (t c) -> p t c", t=NT)
        carried = [pick.take(NT * CT * GATHER // 2, bf16).rearrange(
            "p (t v c) -> p t v c", t=NT, v=GATHER) for _ in range(2)]
        iota_p = pick.take(P // 2, bf16)
        iota_c = pick.take(CT // 2, bf16)
        iota_i = pick.take(P, i32)
        row_i = pick.take(NT, i32)
        tile_i = pick.take(NT, i32)
        thr = pick.take(E, i32)
        cand = pick.take(E, i32)
        bit = pick.take(1, i32)
        hit = pick.take(E, i32)
        cnt = pick.take(E // 2, bf16)
        gsum = pick.take(NT)
        need = pick.take(E)
        got = pick.take(GATHER * CT)

        moe = Region(EXPERTS_AT)
        fc1_sb = moe.take(K * FF).rearrange("p (k f) -> p k f", k=K)
        fc2_sb = moe.take(F * H).rearrange("p (f o) -> p f o", f=F)
        mid = moe.take(F * CAP).rearrange("p (f c) -> p f c", f=F)
        xe_row = moe.take(CT * H).rearrange("p (c o) -> p c o", c=CT)
        xe_t = moe.take(K * CAP).rearrange("p (k c) -> p k c", k=K)
        ye = [moe.take(H) for _ in range(4)]
        idx_cur = [moe.take(CT, i32) for _ in range(2)]
        w_cur = [moe.take(CT) for _ in range(2)]
        fc1_bias = [moe.take(F) for _ in range(2)]
        fc2_bias = [moe.take(H) for _ in range(2)]

        xn_rows = nc.dram_tensor("xn_rows", [T, H], f32, kind="Internal").ap()

        loaded = sem("loaded")
        dve_step = sem("dve_step")
        pool_step = sem("pool_step")
        wmax_in = sem("wmax_in")
        wmax_out = sem("wmax_out")
        consts = sem("consts")
        xblk_in = [sem(f"xblk_in{p}") for p in range(2)]
        pre_ready = sem("pre_ready")
        gate_ready = sem("gate_ready")
        v_ready = sem("v_ready")
        hi_ready = sem("hi_ready")
        h_ready = sem("h_ready")
        lo_ready = sem("lo_ready")
        lh_ready = sem("lh_ready")
        max_taken = sem("max_taken")
        split_ready = sem("split_ready")
        states_moved = sem("states_moved")
        gz_ready = sem("gz_ready")

        aux_in = sem("aux_in")
        aux_ready = sem("aux_ready")
        aux_done = sem("aux_done")
        aux_root = sem("aux_root")
        aux_free = sem("aux_free")
        hmax_in = sem("hmax_in")
        hmax_out = sem("hmax_out")
        xt_in = [sem(f"xt_in{p}") for p in range(2)]
        q_ready = sem("q_ready")
        acc_ready = sem("acc_ready")
        ffn_ready = sem("ffn_ready")
        xp_ready = sem("xp_ready")
        wb_ready = sem("wb_ready")
        tr_ready = sem("tr_ready")
        orow_ready = sem("orow_ready")
        xc_ready = sem("xc_ready")
        y_ready = sem("y_ready")
        lg_ready = sem("lg_ready")
        lg_used = sem("lg_used")
        root_ready = sem("root_ready")
        rstd_ready = sem("rstd_ready")
        xn_ready = sem("xn_ready")
        out_stored = [sem(f"out_stored{p}") for p in range(2)]
        xn_stored = [sem(f"xn_stored{p}") for p in range(2)]
        logit_ready = sem("logit_ready")
        exp_ready = sem("exp_ready")
        iota_ready = sem("iota_ready")
        cnt_ready = sem("cnt_ready")
        count_done = sem("count_done")
        flag_ready = sem("flag_ready")
        rank_done = sem("rank_done")
        hot_ready = sem("hot_ready")
        hot_used = sem("hot_used")
        idx_ready = sem("idx_ready")
        bias_in = [sem(f"bias_in{p}") for p in range(2)]
        fc1_in = sem("fc1_in")
        fc2_in = sem("fc2_in")
        fc1_done = sem("fc1_done")
        fc2_done = sem("fc2_done")
        cur_ready = sem("cur_ready")
        xe_in = sem("xe_in")
        xtr_ready = sem("xtr_ready")
        xtr_moved = sem("xtr_moved")
        mid_pre = sem("mid_pre")
        mid_ready = sem("mid_ready")
        y_pre = sem("y_pre")
        y_sum = sem("y_sum")
        ye_ready = sem("ye_ready")
        ye_stored = [sem(f"ye_stored{p}") for p in range(4)]
        dve_loop = sem("dve_loop")

        def chain(ins):
            chain.n += 1
            ins.then_inc(dve_step, 1)
            nc.vector.wait_ge(dve_step, chain.n)

        chain.n = 0

        def pchain(ins):
            pchain.n += 1
            ins.then_inc(pool_step, 1)
            nc.gpsimd.wait_ge(pool_step, pchain.n)

        pchain.n = 0

        sq_ready = sem("sq_ready")
        eps_ready = sem("eps_ready")
        load_turn = sem("load_turn")
        row_turn = sem("row_turn")
        hmax_ready = sem("hmax_ready")
        q_raw = sem("q_raw")
        hi_hot_ready = sem("hi_hot_ready")
        got_ready = sem("got_ready")
        ident_ready = sem("ident_ready")
        d_flat = d_rows.rearrange("p b o -> p (b o)")
        ys_flat = ys.rearrange("p k b -> p (k b)")
        vals_flat = vals.rearrange("p e t v -> p (e t v)")
        w_flat = w_all.rearrange("p e c -> p (e c)")
        idx_flat = idx_all.rearrange("p e c -> p (e c)")
        flags_row = flags.rearrange("p e t -> p (e t)")
        x_feat3 = x_feat.rearrange("p (k t) -> p k t", k=K)

        block = ctx.enter_context(nc.Block())

        EPS_D, EPS_N = 1e-8, 1e-5
        LOADS = 5
        AUX_LOADS = 8
        ACC = banks[0:2]
        TRB = banks[2:4]
        XCB = banks[4:6]
        LGB = banks[6:8]

        @block.sync
        def _(sp):
            for dst, src in ((wh, wh_t), (wz, wz_t), (gb_row[0:1, :], gate_bias), (h0, cond_t),
                             (alpha_sb, alpha)):
                sp.dma_start(dst, src).then_inc(loaded, 16)
            for dst, src in ((mod_sb, mod_w), (mod_t, mod_w_t), (nw_t, norm_w_t), (rt_t, router_t),
                             (qw_words, q_weight_t), (vecs[:, 0:2 * K], q_vecs),
                             (nw_bc, norm_w_row.broadcast_to([P, H])), (rb_sb, router_b.broadcast_to([P, E]))):
                sp.dma_start(dst, src).then_inc(aux_in, 16)

            def load_block(n, par):
                if not (isinstance(n, int) and n < 2):
                    sp.wait_ge(lh_ready, (n - 1) * SB + 1)
                sp.dma_start(xblk[par].rearrange("p t k b -> p (t k b)"),
                             x_scan[:, bass.ds(n * (SB * K * B), SB * K * B)]).then_inc(xblk_in[par], 16)

            load_block(0, 0)
            load_block(1, 1)
            with sp.Fori(1, NBLK // 2) as i:
                for par in range(2):
                    load_block(2 * i + par, par)

            with sp.Fori(0, B) as b:
                for s in range(2 * SUB):
                    u, par = b * (2 * SUB) + s, s % 2
                    sp.wait_ge(orow_ready, u + 1)
                    sp.dma_start(out[bass.ds(u * P, P), :], orow[par]).then_inc(out_stored[par], 16)
                    sp.wait_ge(xn_ready, u + 1)
                    sp.dma_start(xn_rows[bass.ds(u * P, P), :], yrow[par]).then_inc(xn_stored[par], 16)

            sp.wait_ge(idx_ready, E)

            def load_expert(e, par, first=False):
                rows = e * P if isinstance(e, int) else sp.snap(e * P)
                if not isinstance(e, int):
                    sp.wait_ge(mid_ready, (e - 1) * (2 * F))
                    sp.sem_inc(load_turn, 1)
                    sp.wait_ge(y_sum, (e - 1) * CT)
                    sp.sem_inc(load_turn, 1)
                sp.dma_start(fc1_bias[par], fc1_b[bass.ds(rows, P), :]).then_inc(bias_in[par], 16)
                sp.dma_start(fc2_bias[par], fc2_b[bass.ds(e, 1), :].broadcast_to([P, H])).then_inc(bias_in[par], 16)
                if not first:
                    sp.wait_ge(fc1_done, e)
                sp.dma_start(fc1_sb.rearrange("p k f -> p (k f)"), fc1_t[bass.ds(rows, P), :]).then_inc(fc1_in, 16)
                if not first:
                    sp.wait_ge(fc2_done, e)
                sp.dma_start(fc2_sb.rearrange("p f o -> p (f o)"), fc2_t[bass.ds(rows, P), :]).then_inc(fc2_in, 16)

            load_expert(0, 0, first=True)
            load_expert(1, 1)
            with sp.Fori(1, E // 2) as i:
                load_expert(2 * i, 0)
                load_expert(2 * i + 1, 1)
            sp.wait_ge(out_stored[0], 16 * NT // 2)
            sp.wait_ge(out_stored[1], 16 * NT // 2)
            for c in range(4):
                sp.wait_ge(ye_stored[c], 16 * E * CT // 4)

        def pe_block(n, par, more=True):
            pz = banks[par][:, :].rearrange("p (t m b) -> p t m b", t=SB, m=K)
            nxt = banks[1 - par][:, :].rearrange("p (t m b) -> p t m b", t=SB, m=K)
            queue = zw_products(nxt, xblk[1 - par]) if more else []
            for s in range(SB):
                def product(w, h):
                    for m in range(K):
                        for k in range(K):
                            ins = nc.tensor.matmul(pz[:, s, m, :], w[:, k, m * P:(m + 1) * P], h[:, k, :],
                                                   start=False, stop=False, skip_group_check=True)
                    return ins
                nc.tensor.wait_ge(hi_ready, n * SB + s + 1)
                product(wh_hi, h_hi)
                product(wh_lo, h_hi)
                nc.tensor.wait_ge(lo_ready, n * SB + s + 1)
                product(wh_hi, h_lo).then_inc(pre_ready, 1)
                if more and s == 3:
                    nc.tensor.wait_ge(xblk_in[1 - par], zw_in_value(n, par))
                if s >= 3:
                    for _ in range(2):
                        if queue:
                            queue.pop(0)()

        def zw_in_value(n, par):
            if isinstance(n, int):
                return 16 * ((n + 1) // 2 + 1)
            return 8 * (n - par) + 16 * (par + 1)

        def zw_products(bank, x):
            todo = []
            for m in range(K):
                def bias(m=m):
                    nc.tensor.matmul(bank[:, :, m, :], gb_row[0:1, m * P:(m + 1) * P], ones_f[0:1, :],
                                     start=(m == 0), stop=False, skip_group_check=True)
                todo.append(bias)
                for k in range(K):
                    def prod(m=m, k=k):
                        nc.tensor.matmul(bank[:, :, m, :], wz[:, k, m * P:(m + 1) * P], x[:, :, k, :],
                                         start=False, stop=False, skip_group_check=True)
                    todo.append(prod)
            return todo

        def pe_quant(t):
            nc.tensor.wait_ge(q_ready, t + 1)
            for m in range(K):
                if not (isinstance(t, int) and t == 0 and m < 2):
                    nc.tensor.wait_ge(ffn_ready, t * K + m - 1)
                for k in range(K):
                    ins = nc.tensor.matmul(ACC[m % 2][:, :], qw_sb[:, k, m * P:(m + 1) * P], q_sb[:, k, :],
                                           start=(k == 0), stop=(k == K - 1))
                ins.then_inc(acc_ready, 1)

        def pe_tile(b, half, more=True):
            t = b * 2 + half
            if more:
                pe_quant(t + 1)
            nc.tensor.wait_ge(xp_ready, (t + 1) * K)
            nc.tensor.wait_ge(wb_ready, b + 1)
            x = xt[half]
            for s in range(SUB):
                u, par = t * SUB + s, s % 2
                first = isinstance(t, int) and t == 0 and s < 2
                if not first:
                    nc.tensor.wait_ge(y_ready, u - 1)
                for k in range(K):
                    ins = nc.tensor.matmul(XCB[par][:, :], x[:, k, s * P:(s + 1) * P], wb[:, k, :],
                                           start=(k == 0), stop=(k == K - 1))
                ins.then_inc(xc_ready, 1)
                if not first:
                    nc.tensor.wait_ge(lg_used, u - 1)
                for k in range(K):
                    ins = nc.tensor.matmul(LGB[par][:, 0:P], x[:, k, s * P:(s + 1) * P], route_sb[:, k, :],
                                           start=(k == 0), stop=(k == K - 1))
                ins.then_inc(lg_ready, 1)
                if not first:
                    nc.tensor.wait_ge(orow_ready, u - 1)
                for k in range(K):
                    ins = nc.tensor.transpose(TRB[par][:, k * P:(k + 1) * P], x[:, k, s * P:(s + 1) * P], ident)
                ins.then_inc(tr_ready, 1)

        def pe_xe_t(e):
            nc.tensor.wait_ge(xe_in, (e + 1) * (16 * CT))
            for c in range(CT):
                if not (isinstance(e, int) and e == 0 and c < 2):
                    nc.tensor.wait_ge(xtr_moved, e * CT + c - 1)
                for k in range(K):
                    ins = nc.tensor.transpose(banks[c % 2][:, k * P:(k + 1) * P],
                                              xe_row[:, c, k * P:(k + 1) * P], ident)
                ins.then_inc(xtr_ready, 1)

        def pe_expert(e, more=True):
            nc.tensor.wait_ge(fc1_in, (e + 1) * 16)
            nc.tensor.wait_ge(xtr_moved, (e + 1) * CT)
            for f in range(F):
                for half in range(2):
                    j = 2 * f + half
                    if not (isinstance(e, int) and e == 0 and j < 4):
                        nc.tensor.wait_ge(mid_ready, e * (2 * F) + j - 3)
                    for k in range(K):
                        ins = nc.tensor.matmul(banks[4 + j % 4][:, :], fc1_sb[:, k, f * P:(f + 1) * P],
                                               xe_t[:, k, half * 512:(half + 1) * 512],
                                               start=(k == 0), stop=(k == K - 1))
                    ins.then_inc(mid_pre, 1)
            nc.tensor.wait_ge(mid_pre, (e + 1) * (2 * F))
            pe_sem_inc(fc1_done)
            if more:
                pe_xe_t(e + 1)
            nc.tensor.wait_ge(fc2_in, (e + 1) * 16)
            nc.tensor.wait_ge(mid_ready, (e + 1) * (2 * F))
            for c in range(CT):
                if not (isinstance(e, int) and e == 0 and c < 2):
                    nc.tensor.wait_ge(y_sum, e * CT + c - 1)
                for f in range(F):
                    ins = nc.tensor.matmul(banks[2 + c % 2][:, :], mid[:, f, c * P:(c + 1) * P], fc2_sb[:, f, :],
                                           start=(f == 0), stop=(f == F - 1))
                ins.then_inc(y_pre, 1)
            nc.tensor.wait_ge(y_pre, (e + 1) * CT)
            pe_sem_inc(fc2_done)

        def pe_sem_inc(x):
            nc.tensor.sem_inc(x, 1)

        def pe_prefix(n):
            nc.tensor.wait_ge(flag_ready, n + 1)
            nc.tensor.matmul(banks[2][:, :], tri, flags_row, start=True, stop=True)
            nc.tensor.matmul(banks[3][:, :], ones_b, flags_row, start=True, stop=True).then_inc(rank_done, 1)

        @block.tensor
        def _(pe):
            pe.wait_ge(aux_ready, 1)
            for m in range(K):
                for k in range(K):
                    ins = nc.tensor.matmul(banks[2][:, m * B:(m + 1) * B], mod_sq[:, k, m * P:(m + 1) * P],
                                           ysq[:, k, :], start=(m == 0 and k == 0), stop=(m == K - 1 and k == K - 1),
                                           skip_group_check=True)
            ins.then_inc(aux_done, 1)
            for b in range(B):
                if b >= 2:
                    pe.wait_ge(aux_root, b)
                for k in range(K):
                    ins = nc.tensor.matmul(banks[3 + b % 2][:, :], ysq_wide[:, k, b, :], mod_sq[:, k, :],
                                           start=(k == 0), stop=(k == K - 1))
                ins.then_inc(aux_done, 1)
            pe.wait_ge(aux_ready, 2)
            for ic in range(K):
                for k in range(K):
                    ins = nc.tensor.matmul(banks[5][:, ic * B * E:(ic + 1) * B * E],
                                           mod_t[:, k, ic * P:(ic + 1) * P], g_t[:, k, :, :],
                                           start=(ic == 0 and k == 0), stop=(ic == K - 1 and k == K - 1),
                                           skip_group_check=True)
            ins.then_inc(aux_done, 1)

            pe.wait_ge(split_ready, 1)
            pe.wait_ge(xblk_in[0], 16)
            for f in zw_products(banks[0][:, :].rearrange("p (t m b) -> p t m b", t=SB, m=K), xblk[0]):
                f()
            for m in range(K):
                for k in range(K):
                    nc.tensor.matmul(banks[0][:, m * B:(m + 1) * B], wh[:, k, m * P:(m + 1) * P],
                                     h0[:, k, :], start=False, stop=False, skip_group_check=True)
            with pe.Fori(0, NBLK // 2 - 1) as i:
                pe_block(2 * i, 0)
                pe_block(2 * i + 1, 1)
            pe_block(NBLK - 2, 0)
            pe_block(NBLK - 1, 1, more=False)

            pe.wait_ge(gate_ready, S)
            pe.wait_ge(ident_ready, 1)
            pe_quant(0)
            pe_tile(0, 0)
            pe_tile(0, 1)
            with pe.Fori(1, B - 1) as b:
                pe_tile(b, 0)
                pe_tile(b, 1)
            pe_tile(B - 1, 0)
            pe_tile(B - 1, 1, more=False)

            with pe.Fori(0, BITS) as i:
                pe.wait_ge(cnt_ready, i + 1)
                nc.tensor.matmul(banks[0][:, 0:E], ones_b, cnt, start=True, stop=True).then_inc(count_done, 1)
            pe.wait_ge(cnt_ready, BITS + 1)
            nc.tensor.matmul(banks[0][:, 0:E], ones_b, cnt, start=True, stop=True).then_inc(count_done, 1)
            pe_prefix(0)
            pe_prefix(1)
            with pe.Fori(0, E // 2) as i:
                for par in range(2):
                    pe.wait_ge(hot_ready, 2 * i + par + 1)
                    for t in range(NT):
                        ins = nc.tensor.matmul(banks[4 + par][:, 0:GATHER * CT], onehot[par][:, t, :],
                                               carried[par][:, t, :, :], start=(t == 0), stop=(t == NT - 1))
                    ins.then_inc(hot_used, 1)

            pe_xe_t(0)
            pe_expert(0)
            with pe.Fori(1, E - 1) as e:
                pe_expert(e)
            pe_expert(E - 1, more=False)

        def act_block(n, par):
            for s in range(SB):
                pz = banks[par][:, s * K * B:(s + 1) * K * B]
                nc.scalar.wait_ge(pre_ready, n * SB + s + 1)
                nc.scalar.activation(gate, pz, ACT.Sigmoid, scale=small[:, 1:2]).then_inc(gate_ready, 1)
                nc.scalar.wait_ge(v_ready, n * SB + s + 1)
                nc.scalar.activation(h_hi.rearrange("p k b -> p (k b)"), hv, ACT.Tanh).then_inc(hi_ready, 1)
                if s == 0 and not (isinstance(n, int) and n < 2):
                    nc.scalar.wait_ge(states_moved, n - 1)
                    nc.scalar.wait_ge(max_taken, n - 1)
                nc.scalar.activation(hring[par][:, s].rearrange("p k b -> p (k b)"), hv, ACT.Tanh).then_inc(h_ready, 1)

        def act_chunks(t):
            for m in range(K):
                nc.scalar.wait_ge(acc_ready, t * K + m + 1)
                if not (isinstance(t, int) and t == 0 and m < 2):
                    nc.scalar.wait_ge(xp_ready, t * K + m - 1)
                nc.scalar.activation(ffn[m % 2], ACC[m % 2][:, :], ACT.Identity, bias=vecs[:, K + m:K + m + 1],
                                     scale=vecs[:, 2 * K + m:2 * K + m + 1]).then_inc(ffn_ready, 1)

        def act_tile(b, half, more=True):
            t = b * 2 + half
            if more:
                act_chunks(t + 1)
            for s in range(SUB):
                u, par = t * SUB + s, s % 2
                nc.scalar.wait_ge(y_ready, u + 1)
                if not (isinstance(t, int) and t == 0 and s < 2):
                    nc.scalar.wait_ge(rstd_ready, u - 1)
                nc.scalar.activation(sq_out, yrow[par], ACT.Square, accum_out=ss[:, par:par + 1]).then_inc(sq_ready, 1)
                nc.scalar.wait_ge(sq_ready, u + 1)
                nc.scalar.activation(ss[:, 2 + par:3 + par], ss[:, par:par + 1], ACT.Sqrt, bias=small[:, 11:12],
                                     scale=1.0 / H).then_inc(root_ready, 1)
                nc.scalar.wait_ge(tr_ready, u + 1)
                if not (isinstance(t, int) and t == 0 and s < 2):
                    nc.scalar.wait_ge(out_stored[par], out_value(b, half, s))
                nc.scalar.activation(orow[par], TRB[par][:, :], ACT.Copy).then_inc(orow_ready, 1)

        def out_value(b, half, s):
            return b * (16 * SUB) + 16 * ((half * SUB + s) // 2)

        def bias_value(e, par):
            return (e - par) * 16 + 32

        @block.scalar
        def _(act):
            act.wait_ge(aux_done, 1)
            act.wait_ge(eps_ready, 1)
            nc.scalar.activation(d_t.rearrange("p k b -> p (k b)"), banks[2][:, 0:K * B], ACT.Sqrt,
                                 bias=small[:, 10:11]).then_inc(aux_root, 1)
            for b in range(B):
                act.wait_ge(aux_done, b + 2)
                nc.scalar.activation(d_rows[:, b, :], banks[3 + b % 2][:, :], ACT.Sqrt,
                                     bias=small[:, 10:11]).then_inc(aux_root, 1)
            act.wait_ge(split_ready, 1)
            act_block(0, 0)
            act_block(1, 1)
            with act.Fori(1, NBLK // 2) as i:
                act_block(2 * i, 0)
                act_block(2 * i + 1, 1)

            act.wait_ge(hmax_ready, 1)
            act_chunks(0)
            act_tile(0, 0)
            act_tile(0, 1)
            with act.Fori(1, B - 1) as b:
                act_tile(b, 0)
                act_tile(b, 1)
            act_tile(B - 1, 0)
            act_tile(B - 1, 1, more=False)

            act.wait_ge(logit_ready, 1)
            nc.scalar.activation(probs, probs, ACT.Exp).then_inc(exp_ready, 1)

            def mid_half(e, par):
                nc.scalar.wait_ge(bias_in[par], bias_value(e, par))
                for f in range(F):
                    for half in range(2):
                        j = 2 * f + half
                        nc.scalar.wait_ge(mid_pre, e * (2 * F) + j + 1)
                        nc.scalar.activation(mid[:, f, half * 512:(half + 1) * 512], banks[4 + j % 4][:, :],
                                             ACT.Gelu, bias=fc1_bias[par][:, f:f + 1]).then_inc(mid_ready, 1)

            with act.Fori(0, E // 2) as i:
                mid_half(2 * i, 0)
                mid_half(2 * i + 1, 1)

        def dve_block(n, par):
            v = nc.vector
            for s in range(SB):
                xs = xblk[par][:, s].rearrange("p k b -> p (k b)")
                hr = hring[par][:, s].rearrange("p k b -> p (k b)")
                v.wait_ge(gate_ready, n * SB + s + 1)
                if s == 0:
                    v.wait_ge(xblk_in[par], 8 * (n - par) + 16)
                v.tensor_tensor(gz, gate, xs, ALU.mult).then_inc(gz_ready, 1)
                v.wait_ge(gz_ready, n * SB + s + 1)
                v.wait_ge(lh_ready, n * SB + s + 1)
                v.tensor_tensor(hv, gz, lh, ALU.add).then_inc(v_ready, 1)
                v.wait_ge(h_ready, n * SB + s + 1)
                v.tensor_tensor(h_lo.rearrange("p k b -> p (k b)"), hr, h_hi.rearrange("p k b -> p (k b)"),
                                ALU.subtract).then_inc(lo_ready, 1)
                v.tensor_tensor(lh, hr, leak, ALU.mult).then_inc(lh_ready, 1)
            v.tensor_reduce(hmax[:, bass.ds(n, 1)], hring[par].rearrange("p t k b -> p (t k b)"), AX.X, ALU.max,
                            apply_absolute_value=True).then_inc(max_taken, 1)

        def dve_quant(b, half, t):
            v = nc.vector
            hb = hs[:, b, :, half * TT:(half + 1) * TT] if isinstance(b, int) else \
                hs[:, bass.ds(b, 1), :, half * TT:(half + 1) * TT].rearrange("p b k t -> p (b k) t")
            if not (isinstance(t, int) and t == 0):
                v.wait_ge(acc_ready, t * K)
            v.tensor_scalar(hb, hb, vecs[:, 3 * K:3 * K + 1], ROUND, ALU.mult, ALU.add).then_inc(q_raw, 1)
            v.wait_ge(q_raw, t + 1)
            v.tensor_scalar(q_sb, hb, ROUND, 127.0, ALU.subtract, ALU.min).then_inc(q_ready, 1)

        def dve_add(b, half, t):
            v = nc.vector
            v.wait_ge(xt_in[half], b * 16 + 16)
            for m in range(K):
                v.wait_ge(ffn_ready, t * K + m + 1)
                v.tensor_tensor(xt[half][:, m, :], xt[half][:, m, :], ffn[m % 2], ALU.add).then_inc(xp_ready, 1)

        def dve_finish(b, u, par):
            v = nc.vector
            v.wait_ge(root_ready, u + 1)
            v.reciprocal(rstd[:, bass.ds(u, 1)], ss[:, 2 + par:3 + par]).then_inc(rstd_ready, 1)
            v.wait_ge(rstd_ready, u + 1)
            v.scalar_tensor_tensor(yrow[par], yrow[par], rstd[:, bass.ds(u, 1)], nw_bc, ALU.mult,
                                   ALU.mult).then_inc(xn_ready, 1)
            v.wait_ge(lg_ready, u + 1)
            v.tensor_scalar(probs[:, bass.ds(u * E, E)], LGB[par][:, bass.ds(b * E, E)], rstd[:, bass.ds(u, 1)],
                            None, ALU.mult).then_inc(lg_used, 1)

        def dve_tile(b, half, quant=True, add=True):
            v = nc.vector
            t = b * 2 + half
            nb, nh = (b, 1) if half == 0 else (b + 1, 0)
            if half == 0:
                if not (isinstance(b, int) and b == 0):
                    v.wait_ge(xc_ready, b * (2 * SUB))
                for k in range(K):
                    ins = v.tensor_scalar(wb[:, k, :], mod_sb[:, k, :], ys_of(k, b), None, ALU.mult)
                ins.then_inc(wb_ready, 1)
            if add:
                dve_add(nb, nh, t + 1)
            if quant:
                dve_quant(b + 1, half, t + 2)
            for s in range(SUB):
                u, par = t * SUB + s, s % 2
                v.wait_ge(xc_ready, u + 1)
                if not (isinstance(t, int) and t == 0 and s < 2):
                    v.wait_ge(xn_stored[par], out_value(b, half, s))
                v.tensor_tensor(yrow[par], XCB[par][:, :], drow(b), ALU.mult).then_inc(y_ready, 1)
                dve_finish(b, u, par)

        def drow(b):
            return d_flat[:, bass.ds(b * H, H)]

        def ys_of(k, b):
            return ys_flat[:, bass.ds(b + k * B, 1)]

        def dve_count(c):
            v = nc.vector

        def dve_prefix(n):
            v = nc.vector
            v.wait_ge(rank_done, n + 1)
            chain(v.tensor_copy(tot.rearrange("p e t -> p (e t)"), banks[3][:, :]))
            for e in range(E):
                ins = v.tensor_tensor_scan(cum[:, e, :], ones64, tot[:, e, :], 0.0, ALU.mult, ALU.add)
            chain(ins)
            chain(v.tensor_tensor(cum, cum, tot, ALU.subtract))
            chain(v.tensor_tensor(rank.rearrange("p e t -> p (e t)"), banks[2][:, :],
                                  cum.rearrange("p e t -> p (e t)"), ALU.add))

        @block.vector
        def _(dve):
            v = nc.vector
            v.memset(ones_f, 1.0)
            v.memset(ones_b, 1.0)
            v.memset(small[:, 10:11], EPS_D)
            chain(v.memset(small[:, 11:12], EPS_N))
            dve.sem_inc(eps_ready, 1)
            v.wait_ge(loaded, 16 * LOADS)
            v.wait_ge(aux_in, 16 * AUX_LOADS)
            chain(v.tensor_scalar(ys_flat, h0.rearrange("p k b -> p (k b)"), float(H) ** -0.5, None, ALU.mult))
            chain(v.tensor_tensor(ysq, ys, ys, ALU.mult))
            v.tensor_copy(ysq_wide, bc(ysq[:, :, :, None], [P, K, B, P]))
            chain(v.tensor_tensor(mod_sq, mod_sb, mod_sb, ALU.mult))
            dve.sem_inc(aux_ready, 1)
            for k in range(K):
                ins = v.tensor_scalar(rnw[:, k, :], rt_t[:, k, :], nw_t[:, k:k + 1], None, ALU.mult)
            chain(ins)
            v.wait_ge(aux_root, 1)
            chain(v.reciprocal(d_t, d_t))
            for k in range(K):
                ins = v.tensor_tensor(g_t[:, k], bc(d_t[:, k, :, None], [P, B, E]),
                                      bc(rnw[:, k, None, :], [P, B, E]), ALU.mult)
            chain(ins)
            dve.sem_inc(aux_ready, 1)
            v.tensor_copy(qw_sb, qw_i8)
            v.memset(route_sb, 0.0)
            v.wait_ge(aux_root, B + 1)
            chain(v.reciprocal(d_flat, d_flat))
            v.wait_ge(aux_done, B + 2)
            for ic in range(K):
                ins = v.tensor_tensor(route_sb[:, ic, 0:B * E].rearrange("p (b e) -> p b e", b=B),
                                      banks[5][:, ic * B * E:(ic + 1) * B * E].rearrange("p (b e) -> p b e", b=B),
                                      bc(ys[:, ic, :, None], [P, B, E]), ALU.mult)
            chain(ins)

            v.tensor_reduce(small[:, 2:3], wh, AX.XY, ALU.max, apply_absolute_value=True)
            chain(v.tensor_reduce(small[:, 3:4], wz, AX.XY, ALU.max, apply_absolute_value=True))
            v.tensor_tensor(small[:, 4:5], small[:, 2:3], small[:, 3:4], ALU.max).then_inc(wmax_in, 1)
            v.wait_ge(wmax_out, 1)
            scale_bits = small[:, 6:7].bitcast(i32)
            chain(v.tensor_scalar(scale_bits, small[:, 5:6].bitcast(i32), 0x7F800000, None, ALU.bitwise_and))
            chain(v.tensor_scalar(scale_bits, scale_bits, float(20 * EXP_ONE), None, ALU.max))
            v.tensor_scalar(small[:, 0:1].bitcast(i32), scale_bits, -1.0, float(267 * EXP_ONE), ALU.mult, ALU.add)
            chain(v.tensor_scalar(small[:, 1:2].bitcast(i32), scale_bits, float(13 * EXP_ONE), None, ALU.subtract))
            v.tensor_scalar(wz, wz, small[:, 0:1], None, ALU.mult)
            v.tensor_scalar(gb_row[0:1, :], gb_row[0:1, :], small[0:1, 0:1], None, ALU.mult)
            chain(v.tensor_scalar(wh, wh, small[:, 0:1], None, ALU.mult))
            chain(v.tensor_copy(wh_hi, wh))
            chain(v.tensor_tensor(wh_lo, wh, wh_hi, ALU.subtract))
            chain(v.tensor_scalar(alpha_sb, alpha_sb, -1.0, 1.0, ALU.mult, ALU.add))
            chain(v.tensor_copy(leak.rearrange("p (k b) -> p k b", k=K), bc(alpha_sb[:, :, None], [P, K, B])))
            chain(v.tensor_tensor(lh, leak, h0.rearrange("p k b -> p (k b)"), ALU.mult))
            v.memset(h_lo, 0.0)
            chain(v.memset(h_hi, 0.0))
            for x in (hi_ready, lo_ready, lh_ready, split_ready):
                dve.sem_inc(x, 1)
            with dve.Fori(0, NBLK // 2) as i:
                dve_block(2 * i, 0)
                dve_block(2 * i + 1, 1)

            v.wait_ge(max_taken, NBLK)
            v.tensor_reduce(small[:, 12:13], hmax, AX.X, ALU.max).then_inc(hmax_in, 1)
            v.wait_ge(hmax_out, 1)
            chain(v.tensor_scalar(small[:, 14:15], small[:, 13:14], 1.0 / 127.0, 1e-5, ALU.mult, ALU.max))
            v.reciprocal(vecs[:, 3 * K:3 * K + 1], small[:, 14:15])
            chain(v.tensor_scalar(vecs[:, 2 * K:3 * K], vecs[:, 0:K], small[:, 14:15], None, ALU.mult))
            dve.sem_inc(hmax_ready, 1)
            v.wait_ge(states_moved, NBLK)
            dve_quant(0, 0, 0)
            dve_add(0, 0, 0)
            dve_quant(0, 1, 1)
            dve_tile(0, 0)
            dve_tile(0, 1)
            with dve.Fori(1, B - 1) as b:
                dve_tile(b, 0)
                dve_tile(b, 1)
            dve_tile(B - 1, 0, quant=False)
            dve_tile(B - 1, 1, quant=False, add=False)

            v.wait_ge(iota_ready, 6)
            v.wait_ge(lg_used, NT)
            pr = probs.rearrange("p (t e) -> p t e", t=NT)
            chain(v.tensor_tensor(pr, pr, bc(rb_sb[:, None, :], [P, NT, E]), ALU.add))
            chain(v.tensor_reduce(gsum, pr, AX.X, ALU.max))
            v.tensor_tensor(pr, pr, bc(gsum[:, :, None], [P, NT, E]), ALU.subtract).then_inc(logit_ready, 1)
            v.wait_ge(exp_ready, 1)
            chain(v.tensor_reduce(gsum, pr, AX.X, ALU.add))
            chain(v.reciprocal(gsum, gsum))
            pe_view = p_et.rearrange("p e t -> p t e")
            chain(v.tensor_tensor(pe_view, pr, bc(gsum[:, :, None], [P, NT, E]), ALU.mult))

            v.memset(thr, 0)
            chain(v.memset(bit, 1 << (BITS - 1)))

            def count(flag, n):
                with nc.allow_low_precision(reason="at most 64 flags, which bf16 holds exactly"):
                    nc.vector.tensor_reduce(cnt, flag, AX.X, ALU.add).then_inc(cnt_ready, 1)
                nc.vector.wait_ge(count_done, n + 1)

            STEPS = 6
            base = chain.n

            def link(ins, i, j):
                ins.then_inc(dve_loop, 1)
                nc.vector.wait_ge(dve_loop, i * STEPS + j)

            with dve.Fori(0, BITS) as i:
                link(v.tensor_scalar(cand, thr, bit[:, 0:1], None, ALU.bitwise_or), i, 1)
                link(v.tensor_tensor(flags, p_et, bc(cand.bitcast(f32)[:, :, None], [P, E, NT]), ALU.is_ge), i, 2)
                count(flags, i)
                link(v.tensor_scalar(hit, banks[0][:, 0:E], float(CAP), -1.0, ALU.is_ge, ALU.mult), i, 3)
                link(v.tensor_scalar(hit, hit, bit[:, 0:1], None, ALU.bitwise_and), i, 4)
                link(v.tensor_tensor(thr, thr, hit, ALU.bitwise_or), i, 5)
                link(v.tensor_scalar(bit, bit, 1, None, ALU.logical_shift_right), i, 6)

            thr_b = bc(thr.bitcast(f32)[:, :, None], [P, E, NT])
            chain(v.tensor_tensor(flags, p_et, thr_b, ALU.is_gt))
            count(flags, BITS)
            chain(v.tensor_scalar(need, banks[0][:, 0:E], -1.0, float(CAP), ALU.mult, ALU.add))
            chain(v.tensor_copy(flags2, flags))
            v.tensor_tensor(flags, p_et, thr_b, ALU.is_equal).then_inc(flag_ready, 1)
            dve_prefix(0)
            chain(v.tensor_tensor(rank, rank, bc(need[:, :, None], [P, E, NT]), ALU.is_lt))
            chain(v.tensor_tensor(rank, rank, flags, ALU.mult))
            v.tensor_tensor(flags, flags2, rank, ALU.add).then_inc(flag_ready, 1)
            dve_prefix(1)
            chain(v.tensor_tensor(wsel, flags, p_et, ALU.mult))
            chain(v.tensor_reduce(gsum, wsel.rearrange("p e t -> p t e"), AX.X, ALU.add))
            chain(v.tensor_scalar(gsum, gsum, 1e-9, None, ALU.max))
            chain(v.reciprocal(gsum, gsum))
            chain(v.tensor_tensor(wsel, wsel, bc(gsum[:, None, :], [P, E, NT]), ALU.mult))
            chain(v.tensor_scalar(cum, flags, -float(T), float(T), ALU.mult, ALU.add))
            chain(v.tensor_tensor(slot_i, rank, cum, ALU.add))
            chain(v.tensor_scalar(part_i, slot_i, P - 1, None, ALU.bitwise_and))
            chain(v.tensor_copy(slot_lo, part_i))
            chain(v.tensor_scalar(part_i, slot_i, 7, None, ALU.logical_shift_right))
            chain(v.tensor_copy(slot_hi, part_i))
            v.tensor_copy(vals[:, :, :, 0], bc(row_i[:, None, :], [P, E, NT]))
            v.tensor_copy(vals[:, :, :, 1], bc(tile_i[:, None, :], [P, E, NT]))
            chain(v.tensor_copy(vals[:, :, :, 2], wsel))
            chain(v.tensor_tensor(wres, wsel, vals[:, :, :, 2], ALU.subtract))
            chain(v.tensor_copy(vals[:, :, :, 3], wres))
            chain(v.tensor_tensor(vals[:, :, :, 4], wres, vals[:, :, :, 3], ALU.subtract))
            chain(v.tensor_copy(iota_p, iota_i))
            chain(v.tensor_copy(iota_c, iota_i[:, 0:CT]))

            def lists(e, par):
                lo = slot_lo.rearrange("p e t -> p (e t)")[:, bass.ds(e * NT, NT)]
                hi = slot_hi.rearrange("p e t -> p (e t)")[:, bass.ds(e * NT, NT)]
                va = vals_flat[:, bass.ds(e * (NT * GATHER), NT * GATHER)].rearrange("p (t v) -> p t v", v=GATHER)
                if not (isinstance(e, int) and e < 2):
                    v.wait_ge(hot_used, e - 1)
                v.tensor_tensor(onehot[par], bc(iota_p[:, None, :], [P, NT, P]), bc(lo[:, :, None], [P, NT, P]),
                                ALU.is_equal)
                if not (isinstance(e, int) and e == 0):
                    v.wait_ge(hot_ready, e)
                v.tensor_tensor(hi_hot, bc(iota_c[:, None, :], [P, NT, CT]), bc(hi[:, :, None], [P, NT, CT]),
                                ALU.is_equal).then_inc(hi_hot_ready, 1)
                v.wait_ge(hi_hot_ready, e + 1)
                v.tensor_tensor(carried[par], bc(hi_hot[:, :, None, :], [P, NT, GATHER, CT]),
                                bc(va[:, :, :, None], [P, NT, GATHER, CT]), ALU.mult).then_inc(hot_ready, 1)

            def take_list(e, par):
                v.wait_ge(hot_used, e + 1)
                if not isinstance(e, int):
                    v.wait_ge(idx_ready, e)
                v.tensor_copy(got, banks[4 + par][:, 0:GATHER * CT]).then_inc(got_ready, 1)
                v.wait_ge(got_ready, 3 * e + 1)
                g3 = got.rearrange("p (v c) -> p v c", v=GATHER)
                v.tensor_tensor(g3[:, 2, :], g3[:, 2, :], g3[:, 3, :], ALU.add).then_inc(got_ready, 1)
                v.wait_ge(got_ready, 3 * e + 2)
                v.tensor_tensor(w_flat[:, bass.ds(e * CT, CT)], g3[:, 2, :], g3[:, 4, :], ALU.add)
                v.scalar_tensor_tensor(idx_flat[:, bass.ds(e * CT, CT)], g3[:, 1, :], float(P), g3[:, 0, :],
                                       ALU.mult, ALU.add).then_inc(got_ready, 1)
                v.wait_ge(got_ready, 3 * e + 3)
                v.sem_inc(idx_ready, 1)

            lists(0, 0)
            lists(1, 1)
            take_list(0, 0)
            with dve.Fori(1, E // 2) as i:
                lists(2 * i, 0)
                take_list(2 * i - 1, 1)
                lists(2 * i + 1, 1)
                take_list(2 * i, 0)
            take_list(E - 1, 1)

            def move_xe(e):
                for c in range(CT):
                    v.wait_ge(xtr_ready, e * CT + c + 1)
                    v.tensor_copy(xe_t[:, :, c * P:(c + 1) * P],
                                  banks[c % 2][:, :].rearrange("p (k n) -> p k n", k=K)).then_inc(xtr_moved, 1)

            def current(e, par):
                v.tensor_copy(w_cur[par], w_flat[:, bass.ds(e * CT, CT)])
                v.tensor_copy(idx_cur[par], idx_flat[:, bass.ds(e * CT, CT)]).then_inc(cur_ready, 1)

            def finish_expert(e, par, more=True):
                if more:
                    if not (isinstance(e, int) and e == 0):
                        for c in range(4):
                            v.wait_ge(ye_stored[c], e * 32)
                    current(e + 1, 1 - par)
                    move_xe(e + 1)
                v.wait_ge(bias_in[par], bias_value(e, par))
                for c in range(CT):
                    v.wait_ge(y_pre, e * CT + c + 1)
                    if not (isinstance(e, int) and e == 0 and c < 4):
                        v.wait_ge(ye_stored[c % 4], e * 32 + 16 * (c // 4))
                    v.tensor_tensor(ye[c % 4], banks[2 + c % 2][:, :], fc2_bias[par], ALU.add).then_inc(y_sum, 1)
                    v.wait_ge(y_sum, e * CT + c + 1)
                    v.tensor_scalar(ye[c % 4], ye[c % 4], w_cur[par][:, c:c + 1], None, ALU.mult).then_inc(ye_ready, 1)

            v.wait_ge(idx_ready, E)
            current(0, 0)
            move_xe(0)
            finish_expert(0, 0)
            finish_expert(1, 1)
            with dve.Fori(1, E // 2 - 1) as i:
                finish_expert(2 * i, 0)
                finish_expert(2 * i + 1, 1)
            finish_expert(E - 2, 0)
            finish_expert(E - 1, 1, more=False)

        def pool_block(n, par):
            g = nc.gpsimd
            g.wait_ge(h_ready, (n + 1) * SB)
            g.tensor_copy(hs[:, :, :, bass.ds(n * SB, SB)],
                          hring[par].rearrange("p t k b -> p b k t")).then_inc(states_moved, 1)

        @block.gpsimd
        def _(pool):
            g = nc.gpsimd
            pchain(g.memset(ident, 0.0))
            g.affine_select(out=ident, in_=ident, compare_op=ALU.not_equal, fill=1.0, base=0,
                            pattern=[[-1, P]], channel_multiplier=1).then_inc(ident_ready, 1)
            g.wait_ge(wmax_in, 1)
            g.partition_all_reduce(small[:, 5:6], small[:, 4:5], P, ABSMAX).then_inc(wmax_out, 1)
            g.wait_ge(split_ready, 1)
            with pool.Fori(0, NBLK // 2) as i:
                pool_block(2 * i, 0)
                pool_block(2 * i + 1, 1)
            g.wait_ge(hmax_in, 1)
            g.partition_all_reduce(small[:, 13:14], small[:, 12:13], P, ABSMAX).then_inc(hmax_out, 1)

            def load_x(b, half):
                t = b * 2 + half
                g.dma_start(xt[half], x_feat3[:, :, bass.ds(t * TT, TT)]).then_inc(xt_in[half], 16)

            g.wait_ge(hmax_out, 1)
            load_x(0, 0)
            load_x(0, 1)
            with pool.Fori(1, B) as b:
                for half in range(2):
                    g.wait_ge(tr_ready, (b * 2 + half - 1) * SUB)
                    load_x(b, half)

            g.wait_ge(lg_used, NT)
            for par in range(2):
                g.wait_ge(xn_stored[par], 16 * NT // 2)
                g.wait_ge(out_stored[par], 16 * NT // 2)
            g.memset(ones64, 1.0).then_inc(iota_ready, 1)
            pchain(g.memset(tri, 1.0))
            g.affine_select(out=tri, in_=tri, compare_op=ALU.is_gt, fill=0.0, base=0, pattern=[[1, P]],
                            channel_multiplier=-1).then_inc(iota_ready, 1)
            g.iota(iota_i, pattern=[[1, P]], base=0, channel_multiplier=0).then_inc(iota_ready, 1)
            g.iota(row_i, pattern=[[0, NT]], base=0, channel_multiplier=1).then_inc(iota_ready, 1)
            g.iota(tile_i, pattern=[[1, NT]], base=0, channel_multiplier=0).then_inc(iota_ready, 1)
            g.wait_ge(iota_ready, 5)
            g.sem_inc(iota_ready, 1)

            def gather(e, par):
                g.wait_ge(cur_ready, e + 1)
                if not (isinstance(e, int) and e == 0):
                    g.wait_ge(xtr_ready, e * CT)
                g.sem_inc(row_turn, 1)
                for c in range(CT):
                    g.indirect_dma_start(xe_row[:, c, :], None, xn_rows[:, :],
                                         bass.IndirectOffsetOnAxis(idx_cur[par][:, c:c + 1].bitcast(u32), 0)
                                         ).then_inc(xe_in, 16)

            def scatter(e, par):
                if not (isinstance(e, int) and e == 0):
                    for c in range(4):
                        g.wait_ge(ye_stored[c], e * 32)
                for c in range(CT):
                    g.wait_ge(ye_ready, e * CT + c + 1)
                    g.sem_inc(row_turn, 1)
                    g.indirect_dma_start(out[:, :],
                                         bass.IndirectOffsetOnAxis(idx_cur[par][:, c:c + 1].bitcast(u32), 0),
                                         ye[c % 4], None, compute_op=ALU.add).then_inc(ye_stored[c % 4], 16)

            for par in range(2):
                g.wait_ge(xn_stored[par], 16 * NT // 2)
                g.wait_ge(out_stored[par], 16 * NT // 2)
            gather(0, 0)
            gather(1, 1)
            scatter(0, 0)
            with pool.Fori(1, E // 2) as i:
                gather(2 * i, 0)
                scatter(2 * i - 1, 1)
                gather(2 * i + 1, 1)
                scatter(2 * i, 0)
            scatter(E - 1, 1)


def kernel(x, cond_1024, L0_cond_W, L0_cond_b, L0_cond_alpha, L0_ffn_weight_int8, L0_ffn_weight_scale,
           L0_ffn_bias, L1_cond_weight, L1_ffn_norm_weight, L1_ffn_router_w, L1_ffn_router_b,
           L1_ffn_fc1_w, L1_ffn_fc1_b, L1_ffn_fc2_w, L1_ffn_fc2_b):
    import numpy as np
    import concourse.bacc as bacc
    from concourse import mybir as _mybir
    from concourse.bass_utils import run_bass_kernel_spmd

    B, S, H = x.shape
    P = 128
    K = H // P
    E, FF, _ = L1_ffn_fc1_w.shape
    x, W = np.asarray(x), np.asarray(L0_cond_W)

    def by_part(m):
        m = np.asarray(m)
        n = m.shape[1]
        return np.ascontiguousarray(m.reshape(-1, P, n).transpose(1, 0, 2).reshape(P, -1))

    def cols(v):
        return np.ascontiguousarray(np.asarray(v).reshape(-1, P).T)

    def row(v):
        return np.ascontiguousarray(np.asarray(v).reshape(1, -1))

    fc1 = np.asarray(L1_ffn_fc1_w).reshape(E, FF, K, P).transpose(0, 3, 2, 1).reshape(E * P, K * FF)
    fc2 = np.asarray(L1_ffn_fc2_w).reshape(E, H, FF // P, P).transpose(0, 3, 2, 1).reshape(E * P, FF // P * H)
    arrays = {
        "x_scan": x.reshape(B, S, K, P).transpose(3, 1, 2, 0).reshape(P, S * K * B),
        "x_feat": x.reshape(B * S, K, P).transpose(2, 1, 0).reshape(P, K * B * S),
        "cond_t": by_part(np.asarray(cond_1024).T),
        "wh_t": by_part(W[:, :H].T),
        "wz_t": by_part(W[:, H:].T),
        "gate_bias": row(L0_cond_b),
        "alpha": cols(L0_cond_alpha),
        "q_weight_t": by_part(np.asarray(L0_ffn_weight_int8).T).view(np.int32),
        "q_vecs": np.concatenate([cols(np.asarray(L0_ffn_weight_scale).reshape(-1)), cols(L0_ffn_bias)], axis=1),
        "mod_w": by_part(L1_cond_weight),
        "mod_w_t": by_part(np.asarray(L1_cond_weight).T),
        "norm_w_t": cols(L1_ffn_norm_weight),
        "norm_w_row": row(L1_ffn_norm_weight),
        "router_t": by_part(np.asarray(L1_ffn_router_w).T),
        "router_b": row(L1_ffn_router_b),
        "fc1_t": fc1,
        "fc1_b": np.asarray(L1_ffn_fc1_b).reshape(E, FF // P, P).transpose(0, 2, 1).reshape(E * P, FF // P),
        "fc2_t": fc2,
        "fc2_b": L1_ffn_fc2_b,
    }
    nc = bacc.Bacc("TRN2", target_bir_lowering=False, num_devices=1)
    arrays = {n: np.ascontiguousarray(a) for n, a in arrays.items()}
    aps = [nc.dram_tensor(f"{n}_dram", a.shape, _mybir.dt.from_np(a.dtype), kind="ExternalInput").ap()
           for n, a in arrays.items()]
    out = nc.dram_tensor("out_dram", (B * S, H), _mybir.dt.float32, kind="ExternalOutput").ap()
    adaln_ffn_kernel(nc, *aps, out)
    r = run_bass_kernel_spmd(nc, [{f"{n}_dram": a for n, a in arrays.items()}], core_ids=[0])
    return r.results[0]["out_dram"].reshape(B, S, H)
```

```python
import concourse.bass as bass
from concourse import mybir
from contextlib import ExitStack


def adaln_ffn_kernel(nc, x_scan, x_feat, cond_t, wh_t, wz_t, gate_bias, alpha, q_weight_t, q_vecs,
                     mod_w, mod_w_t, norm_w_t, norm_w_row, router_t, router_b, fc1_t, fc1_b,
                     fc2_t, fc2_b, out):
    f32, f16, bf16 = mybir.dt.float32, mybir.dt.float16, mybir.dt.bfloat16
    i32, u32 = mybir.dt.int32, mybir.dt.uint32
    ALU = mybir.AluOpType
    ACT = mybir.ActivationFunctionType
    AX = mybir.AxisListType

    P = 128
    B, S, H = 8, 1024, 512
    K = H // P
    T = B * S
    NT = T // P
    E, FF = 8, 2048
    F = FF // P
    CAP = T // E
    CT = CAP // P
    SB = 16
    NBLK = S // SB
    TT = 512
    SUB = TT // P
    ROUND = 1.5 * 2.0 ** 23
    EXP_ONE = 1 << 23
    BITS = 30
    GATHER = 5

    ABSMAX = bass.bass_isa.ReduceOp.absmax

    def bc(ap, shape):
        return ap.to_broadcast(shape)

    with ExitStack() as ctx:
        def sem(name):
            return ctx.enter_context(nc.semaphore(name))

        ARENA = 53200
        arena = ctx.enter_context(nc.sbuf_tensor("arena", [P, ARENA], f32))
        banks = [ctx.enter_context(nc.psum_tensor(f"bank{n}", [P, 512], f32)) for n in range(8)]

        class Region:

            def __init__(self, at):
                self.at = at

            def take(self, words, dt=f32):
                lo, self.at = self.at, self.at + words
                assert self.at <= ARENA, self.at
                view = arena[:, lo:self.at]
                return view if dt == f32 else view.bitcast(dt)

        keep = Region(0)
        ident = keep.take(P)
        small = keep.take(64)
        ones_f = keep.take(P)
        ones_b = keep.take(P // 2, bf16)
        idx_all = keep.take(E * CT, i32).rearrange("p (e c) -> p e c", e=E)
        w_all = keep.take(E * CT).rearrange("p (e c) -> p e c", e=E)
        EXPERTS_AT = keep.at
        d_rows = keep.take(B * H)
        d_rows = d_rows.rearrange("p (b o) -> p b o", b=B)
        mod_sb = keep.take(K * H).rearrange("p (k o) -> p k o", k=K)
        route_sb = keep.take(K * P).rearrange("p (k n) -> p k n", k=K)
        qw_sb = keep.take(K * H // 2, bf16).rearrange("p (k o) -> p k o", k=K)
        ys = keep.take(K * B).rearrange("p (k b) -> p k b", k=K)
        probs = keep.take(NT * E)
        rstd = keep.take(NT)
        rb_sb = keep.take(E)
        vecs = keep.take(4 * K)
        keep_nw = keep.take(H)
        AFTER_KEEP = keep.at

        scan = Region(AFTER_KEEP)
        hs = scan.take(B * K * S).rearrange("p (b k t) -> p b k t", b=B, k=K)
        AFTER_HS = scan.at
        wh_hi = scan.take(K * H // 2, f16).rearrange("p (k o) -> p k o", k=K)
        wh_lo = scan.take(K * H // 2, f16).rearrange("p (k o) -> p k o", k=K)
        wz = scan.take(K * H).rearrange("p (k o) -> p k o", k=K)
        xblk = [scan.take(SB * K * B).rearrange("p (k t b) -> p k t b", k=K, t=SB) for _ in range(2)]
        zl = [scan.take(SB * K * B * 2).rearrange("p (t c w) -> p t c w", t=SB, w=2) for _ in range(2)]
        hring = [scan.take(SB * K * B).rearrange("p (t k b) -> p t k b", t=SB, k=K) for _ in range(2)]
        h_hi = scan.take(K * B // 2, f16).rearrange("p (k b) -> p k b", k=K)
        h_lo = scan.take(K * B // 2, f16).rearrange("p (k b) -> p k b", k=K)
        gate = scan.take(K * B * 2).rearrange("p (c w) -> p c w", w=2)
        hv = scan.take(K * B * 2).rearrange("p (c w) -> p c w", w=2)
        leak = scan.take(K * B)
        h0 = scan.take(K * B).rearrange("p (k b) -> p k b", k=K)
        gb_row = scan.take(H)
        gb_part = [scan.take(H // 2, bf16) for _ in range(3)]
        gb_parts = scan.take(H // 2, bf16)
        hmax = scan.take(2 * NBLK)
        nw_bc = keep_nw
        pro = Region(AFTER_KEEP)
        wh = pro.take(K * H).rearrange("p (k o) -> p k o", k=K)
        mod_sq = pro.take(K * H).rearrange("p (k o) -> p k o", k=K)
        mod_t = pro.take(K * H).rearrange("p (k o) -> p k o", k=K)
        ysq = pro.take(K * B).rearrange("p (k b) -> p k b", k=K)
        ysq_wide = pro.take(K * B * P).rearrange("p (k b n) -> p k b n", k=K, b=B)
        d_t = pro.take(K * B).rearrange("p (k b) -> p k b", k=K)
        nw_t = pro.take(K)
        rt_t = pro.take(K * E).rearrange("p (k e) -> p k e", k=K)
        rnw = pro.take(K * E).rearrange("p (k e) -> p k e", k=K)
        g_t = pro.take(K * B * E).rearrange("p (k b e) -> p k b e", k=K, b=B)
        qw_words = pro.take(K * H // 4, i32)
        qw_i8 = qw_words.bitcast(mybir.dt.int8).rearrange("p (k o) -> p k o", k=K)
        alpha_sb = pro.take(K)

        dense = Region(AFTER_HS)
        xt = [dense.take(K * TT).rearrange("p (k t) -> p k t", k=K) for _ in range(2)]
        q_sb = dense.take(K * TT // 2, bf16).rearrange("p (k t) -> p k t", k=K)
        ffn = [dense.take(TT) for _ in range(2)]
        wb = dense.take(K * H).rearrange("p (k o) -> p k o", k=K)
        yrow = [dense.take(H) for _ in range(2)]
        orow = [dense.take(H) for _ in range(2)]
        sq_out = dense.take(H)
        ss = dense.take(8)

        pick = Region(AFTER_KEEP)
        p_et = pick.take(E * NT).rearrange("p (e t) -> p e t", e=E)
        flags = pick.take(E * NT // 2, bf16).rearrange("p (e t) -> p e t", e=E)
        flags2 = pick.take(E * NT // 2, bf16).rearrange("p (e t) -> p e t", e=E)
        above = pick.take(E * NT).rearrange("p (e t) -> p e t", e=E)
        rank = pick.take(E * NT).rearrange("p (e t) -> p e t", e=E)
        cum = pick.take(E * NT).rearrange("p (e t) -> p e t", e=E)
        tot = pick.take(E * NT).rearrange("p (e t) -> p e t", e=E)
        wsel = pick.take(E * NT).rearrange("p (e t) -> p e t", e=E)
        wres = pick.take(E * NT).rearrange("p (e t) -> p e t", e=E)
        slot_i = pick.take(E * NT, i32).rearrange("p (e t) -> p e t", e=E)
        part_i = pick.take(E * NT, i32).rearrange("p (e t) -> p e t", e=E)
        slot_lo = pick.take(E * NT // 2, bf16).rearrange("p (e t) -> p e t", e=E)
        slot_hi = pick.take(E * NT // 2, bf16).rearrange("p (e t) -> p e t", e=E)
        vals = pick.take(E * NT * GATHER // 2 + E, bf16)[:, 0:E * NT * GATHER].rearrange(
            "p (e t v) -> p e t v", e=E, v=GATHER)
        ones64 = pick.take(NT)
        tri = pick.take(P // 2, bf16)
        onehot = [pick.take(NT * P // 2, bf16).rearrange("p (t n) -> p t n", t=NT) for _ in range(2)]
        hi_hot = pick.take(NT * CT // 2, bf16).rearrange("p (t c) -> p t c", t=NT)
        carried = [pick.take(NT * CT * GATHER // 2, bf16).rearrange(
            "p (t v c) -> p t v c", t=NT, v=GATHER) for _ in range(2)]
        iota_p = pick.take(P // 2, bf16)
        iota_c = pick.take(CT // 2, bf16)
        iota_i = pick.take(P, i32)
        row_i = pick.take(NT, i32)
        tile_i = pick.take(NT, i32)
        thr = pick.take(E, i32)
        cand = pick.take(E, i32)
        bit = pick.take(1, i32)
        hit = pick.take(E, i32)
        cnt = pick.take(E // 2, bf16)
        gsum = pick.take(NT)
        need = pick.take(E)
        got = pick.take(GATHER * CT)

        moe = Region(EXPERTS_AT)
        fc1_sb = moe.take(K * FF).rearrange("p (k f) -> p k f", k=K)
        fc2_sb = moe.take(F * H).rearrange("p (f o) -> p f o", f=F)
        mid = moe.take(F * CAP).rearrange("p (f c) -> p f c", f=F)
        xe_row = moe.take(CT * H).rearrange("p (c o) -> p c o", c=CT)
        xe_t = moe.take(K * CAP).rearrange("p (k c) -> p k c", k=K)
        ye = [moe.take(H) for _ in range(4)]
        idx_cur = [moe.take(CT, i32) for _ in range(2)]
        w_cur = [moe.take(CT) for _ in range(2)]
        fc1_bias = [moe.take(F) for _ in range(2)]
        fc2_bias = [moe.take(H) for _ in range(2)]

        xn_rows = nc.dram_tensor("xn_rows", [T, H], f32, kind="Internal").ap()

        loaded = sem("loaded")
        dve_step = sem("dve_step")
        pool_step = sem("pool_step")
        wmax_in = sem("wmax_in")
        wmax_out = sem("wmax_out")
        consts = sem("consts")
        xblk_in = [sem(f"xblk_in{p}") for p in range(2)]
        pre_ready = sem("pre_ready")
        gate_ready = sem("gate_ready")
        v_ready = sem("v_ready")
        hi_ready = sem("hi_ready")
        h_ready = sem("h_ready")
        lo_ready = sem("lo_ready")
        lh_ready = sem("lh_ready")
        max_taken = sem("max_taken")
        split_ready = sem("split_ready")
        states_moved = sem("states_moved")
        zl_ready = sem("zl_ready")
        parts_ready = sem("parts_ready")
        parts_in = sem("parts_in")

        aux_in = sem("aux_in")
        aux_ready = sem("aux_ready")
        aux_done = sem("aux_done")
        aux_root = sem("aux_root")
        aux_free = sem("aux_free")
        hmax_in = sem("hmax_in")
        hmax_out = sem("hmax_out")
        xt_in = [sem(f"xt_in{p}") for p in range(2)]
        q_ready = sem("q_ready")
        acc_ready = sem("acc_ready")
        ffn_ready = sem("ffn_ready")
        xp_ready = sem("xp_ready")
        wb_ready = sem("wb_ready")
        tr_ready = sem("tr_ready")
        orow_ready = sem("orow_ready")
        xc_ready = sem("xc_ready")
        y_ready = sem("y_ready")
        lg_ready = sem("lg_ready")
        lg_used = sem("lg_used")
        root_ready = sem("root_ready")
        rstd_ready = sem("rstd_ready")
        xn_ready = sem("xn_ready")
        out_stored = [sem(f"out_stored{p}") for p in range(2)]
        xn_stored = [sem(f"xn_stored{p}") for p in range(2)]
        logit_ready = sem("logit_ready")
        exp_ready = sem("exp_ready")
        iota_ready = sem("iota_ready")
        cnt_ready = sem("cnt_ready")
        count_done = sem("count_done")
        flag_ready = sem("flag_ready")
        rank_done = sem("rank_done")
        hot_ready = sem("hot_ready")
        hot_used = sem("hot_used")
        idx_ready = sem("idx_ready")
        bias_in = [sem(f"bias_in{p}") for p in range(2)]
        fc1_in = sem("fc1_in")
        fc2_in = sem("fc2_in")
        fc1_done = sem("fc1_done")
        fc2_done = sem("fc2_done")
        cur_ready = sem("cur_ready")
        xe_in = sem("xe_in")
        xtr_ready = sem("xtr_ready")
        xtr_moved = sem("xtr_moved")
        mid_pre = sem("mid_pre")
        mid_ready = sem("mid_ready")
        y_pre = sem("y_pre")
        y_sum = sem("y_sum")
        ye_ready = sem("ye_ready")
        ye_stored = [sem(f"ye_stored{p}") for p in range(4)]
        dve_loop = sem("dve_loop")

        def chain(ins):
            chain.n += 1
            ins.then_inc(dve_step, 1)
            nc.vector.wait_ge(dve_step, chain.n)

        chain.n = 0

        def pchain(ins):
            pchain.n += 1
            ins.then_inc(pool_step, 1)
            nc.gpsimd.wait_ge(pool_step, pchain.n)

        pchain.n = 0

        sq_ready = sem("sq_ready")
        eps_ready = sem("eps_ready")
        load_turn = sem("load_turn")
        pool_turn = sem("pool_turn")
        hmax_ready = sem("hmax_ready")
        q_raw = sem("q_raw")
        hi_hot_ready = sem("hi_hot_ready")
        got_ready = sem("got_ready")
        ident_ready = sem("ident_ready")
        h_hi_flat = h_hi.rearrange("p k b -> p (k b)")
        h_lo_flat = h_lo.rearrange("p k b -> p (k b)")
        hring_flat = [h.rearrange("p t k b -> p t (k b)") for h in hring]
        d_flat = d_rows.rearrange("p b o -> p (b o)")
        ys_flat = ys.rearrange("p k b -> p (k b)")
        vals_flat = vals.rearrange("p e t v -> p (e t v)")
        w_flat = w_all.rearrange("p e c -> p (e c)")
        idx_flat = idx_all.rearrange("p e c -> p (e c)")
        flags_row = flags.rearrange("p e t -> p (e t)")
        x_feat3 = x_feat.rearrange("p (k t) -> p k t", k=K)

        block = ctx.enter_context(nc.Block())

        HALF = (range(0, K // 2), range(K // 2, K))
        HC = K * B // 2
        STEP2 = 2 * SB

        def sums(par, m, at, n):
            at += (m % 2) * SB * B
            return banks[2 * par + m // 2][:, at:at + n]

        def pre(par, j, s):
            return banks[2 * par + j][:, 0:2 * SB * B].rearrange("p (m t b) -> p m t b", m=2, t=SB)[:, :, s, :]

        EPS_D, EPS_N = 1e-8, 1e-5
        LOADS = 5
        AUX_LOADS = 8
        ACC = banks[0:2]
        TRB = banks[2:4]
        XCB = banks[4:6]
        LGB = banks[6:8]

        @block.sync
        def _(sp):
            for dst, src in ((wh, wh_t), (wz, wz_t), (gb_row[0:1, :], gate_bias), (h0, cond_t),
                             (alpha_sb, alpha)):
                sp.dma_start(dst, src).then_inc(loaded, 16)
            for dst, src in ((mod_sb, mod_w), (mod_t, mod_w_t), (nw_t, norm_w_t), (rt_t, router_t),
                             (qw_words, q_weight_t), (vecs[:, 0:2 * K], q_vecs),
                             (nw_bc, norm_w_row.broadcast_to([P, H])), (rb_sb, router_b.broadcast_to([P, E]))):
                sp.dma_start(dst, src).then_inc(aux_in, 16)

            def load_block(n, par):
                if not (isinstance(n, int) and n < 2):
                    sp.wait_ge(zl_ready, n - 1)
                    sp.wait_ge(gate_ready, (n - 2) * STEP2 + 1)
                sp.dma_start(xblk[par].rearrange("p k t b -> p (k t b)"),
                             x_scan[:, bass.ds(n * (SB * K * B), SB * K * B)]).then_inc(xblk_in[par], 16)

            load_block(0, 0)
            load_block(1, 1)
            sp.wait_ge(parts_ready, 1)
            for n, part in enumerate(gb_part):
                sp.dma_start(gb_parts[n:n + 1, :], part[0:1, :]).then_inc(parts_in, 16)
            with sp.Fori(1, NBLK // 2) as i:
                for par in range(2):
                    load_block(2 * i + par, par)

            with sp.Fori(0, B) as b:
                for s in range(2 * SUB):
                    u, par = b * (2 * SUB) + s, s % 2
                    sp.wait_ge(orow_ready, u + 1)
                    sp.dma_start(out[bass.ds(u * P, P), :], orow[par]).then_inc(out_stored[par], 16)
                    sp.wait_ge(xn_ready, u + 1)
                    sp.dma_start(xn_rows[bass.ds(u * P, P), :], yrow[par]).then_inc(xn_stored[par], 16)

            sp.wait_ge(idx_ready, E)

            def load_expert(e, par, first=False):
                rows = e * P if isinstance(e, int) else sp.snap(e * P)
                if not isinstance(e, int):
                    sp.wait_ge(mid_ready, (e - 1) * (2 * F))
                    sp.sem_inc(load_turn, 1)
                    sp.wait_ge(y_sum, (e - 1) * CT)
                    sp.sem_inc(load_turn, 1)
                sp.dma_start(fc1_bias[par], fc1_b[bass.ds(rows, P), :]).then_inc(bias_in[par], 16)
                sp.dma_start(fc2_bias[par], fc2_b[bass.ds(e, 1), :].broadcast_to([P, H])).then_inc(bias_in[par], 16)
                if not first:
                    sp.wait_ge(fc1_done, e)
                sp.dma_start(fc1_sb.rearrange("p k f -> p (k f)"), fc1_t[bass.ds(rows, P), :]).then_inc(fc1_in, 16)
                if not first:
                    sp.wait_ge(fc2_done, e)
                sp.dma_start(fc2_sb.rearrange("p f o -> p (f o)"), fc2_t[bass.ds(rows, P), :]).then_inc(fc2_in, 16)

            load_expert(0, 0, first=True)
            load_expert(1, 1)
            with sp.Fori(1, E // 2) as i:
                load_expert(2 * i, 0)
                load_expert(2 * i + 1, 1)
            sp.wait_ge(out_stored[0], 16 * NT // 2)
            sp.wait_ge(out_stored[1], 16 * NT // 2)
            for c in range(4):
                sp.wait_ge(ye_stored[c], 16 * E * CT // 4)

        def pe_block(n, par, more=True):
            queue = zw_products(1 - par, xblk[1 - par]) if more else []
            for s in range(SB):
                def product(w, h, ms, ks):
                    for m in ms:
                        for k in ks:
                            ins = nc.tensor.matmul(sums(par, m, s * B, B), w[:, k, m * P:(m + 1) * P], h[:, k, :],
                                                   start=False, stop=False, skip_group_check=True)
                    return ins
                at = n * STEP2 + 2 * s
                nc.tensor.wait_ge(hi_ready, at + 1)
                product(wh_hi, h_hi, HALF[0], HALF[0])
                product(wh_lo, h_hi, HALF[0], HALF[0])
                product(wh_hi, h_hi, HALF[1], HALF[0])
                product(wh_lo, h_hi, HALF[1], HALF[0])
                nc.tensor.wait_ge(lo_ready, at + 1)
                product(wh_hi, h_lo, HALF[0], HALF[0])
                nc.tensor.wait_ge(hi_ready, at + 2)
                product(wh_hi, h_hi, HALF[0], HALF[1])
                product(wh_lo, h_hi, HALF[0], HALF[1])
                nc.tensor.wait_ge(lo_ready, at + 2)
                product(wh_hi, h_lo, HALF[0], HALF[1]).then_inc(pre_ready, 1)
                product(wh_hi, h_lo, HALF[1], HALF[0])
                product(wh_hi, h_hi, HALF[1], HALF[1])
                product(wh_lo, h_hi, HALF[1], HALF[1])
                product(wh_hi, h_lo, HALF[1], HALF[1]).then_inc(pre_ready, 1)
                if more:
                    if s == 0:
                        nc.tensor.wait_ge(xblk_in[1 - par], zw_in_value(n, par))
                    queue.pop(0)()

        def zw_in_value(n, par):
            if isinstance(n, int):
                return 16 * ((n + 1) // 2 + 1)
            return 8 * (n - par) + 16 * (par + 1)

        def zw_products(par, x):
            todo = []
            for m in range(K):
                for k in range(K):
                    def prod(m=m, k=k):
                        if k == 0:
                            nc.tensor.matmul(sums(par, m, 0, SB * B), gb_parts[0:3, m * P:(m + 1) * P],
                                             ones_b[0:3, 0:SB * B], start=(m % 2 == 0), stop=False,
                                             skip_group_check=True)
                        nc.tensor.matmul(sums(par, m, 0, SB * B), wz[:, k, m * P:(m + 1) * P],
                                         x[:, k, :, :].rearrange("p t b -> p (t b)"),
                                         start=False, stop=False, skip_group_check=True)
                    todo.append(prod)
            return todo

        def pe_quant(t):
            nc.tensor.wait_ge(q_ready, t + 1)
            for m in range(K):
                if not (isinstance(t, int) and t == 0 and m < 2):
                    nc.tensor.wait_ge(ffn_ready, t * K + m - 1)
                for k in range(K):
                    ins = nc.tensor.matmul(ACC[m % 2][:, :], qw_sb[:, k, m * P:(m + 1) * P], q_sb[:, k, :],
                                           start=(k == 0), stop=(k == K - 1))
                ins.then_inc(acc_ready, 1)

        def pe_tile(b, half, more=True):
            t = b * 2 + half
            if more:
                pe_quant(t + 1)
            nc.tensor.wait_ge(xp_ready, (t + 1) * K)
            nc.tensor.wait_ge(wb_ready, b + 1)
            x = xt[half]
            for s in range(SUB):
                u, par = t * SUB + s, s % 2
                first = isinstance(t, int) and t == 0 and s < 2
                if not first:
                    nc.tensor.wait_ge(y_ready, u - 1)
                for k in range(K):
                    ins = nc.tensor.matmul(XCB[par][:, :], x[:, k, s * P:(s + 1) * P], wb[:, k, :],
                                           start=(k == 0), stop=(k == K - 1))
                ins.then_inc(xc_ready, 1)
                if not first:
                    nc.tensor.wait_ge(lg_used, u - 1)
                for k in range(K):
                    ins = nc.tensor.matmul(LGB[par][:, 0:P], x[:, k, s * P:(s + 1) * P], route_sb[:, k, :],
                                           start=(k == 0), stop=(k == K - 1))
                ins.then_inc(lg_ready, 1)
                if not first:
                    nc.tensor.wait_ge(orow_ready, u - 1)
                for k in range(K):
                    ins = nc.tensor.transpose(TRB[par][:, k * P:(k + 1) * P], x[:, k, s * P:(s + 1) * P], ident)
                ins.then_inc(tr_ready, 1)

        def pe_xe_t(e):
            nc.tensor.wait_ge(xe_in, (e + 1) * (16 * CT))
            for c in range(CT):
                if not (isinstance(e, int) and e == 0 and c < 2):
                    nc.tensor.wait_ge(xtr_moved, e * CT + c - 1)
                for k in range(K):
                    ins = nc.tensor.transpose(banks[c % 2][:, k * P:(k + 1) * P],
                                              xe_row[:, c, k * P:(k + 1) * P], ident)
                ins.then_inc(xtr_ready, 1)

        def pe_expert(e, more=True):
            nc.tensor.wait_ge(fc1_in, (e + 1) * 16)
            nc.tensor.wait_ge(xtr_moved, (e + 1) * CT)
            for f in range(F):
                for half in range(2):
                    j = 2 * f + half
                    if not (isinstance(e, int) and e == 0 and j < 4):
                        nc.tensor.wait_ge(mid_ready, e * (2 * F) + j - 3)
                    for k in range(K):
                        ins = nc.tensor.matmul(banks[4 + j % 4][:, :], fc1_sb[:, k, f * P:(f + 1) * P],
                                               xe_t[:, k, half * 512:(half + 1) * 512],
                                               start=(k == 0), stop=(k == K - 1))
                    ins.then_inc(mid_pre, 1)
            nc.tensor.wait_ge(mid_pre, (e + 1) * (2 * F))
            pe_sem_inc(fc1_done)
            if more:
                pe_xe_t(e + 1)
            nc.tensor.wait_ge(fc2_in, (e + 1) * 16)
            nc.tensor.wait_ge(mid_ready, (e + 1) * (2 * F))
            for c in range(CT):
                if not (isinstance(e, int) and e == 0 and c < 2):
                    nc.tensor.wait_ge(y_sum, e * CT + c - 1)
                for f in range(F):
                    ins = nc.tensor.matmul(banks[2 + c % 2][:, :], mid[:, f, c * P:(c + 1) * P], fc2_sb[:, f, :],
                                           start=(f == 0), stop=(f == F - 1))
                ins.then_inc(y_pre, 1)
            nc.tensor.wait_ge(y_pre, (e + 1) * CT)
            pe_sem_inc(fc2_done)

        def pe_sem_inc(x):
            nc.tensor.sem_inc(x, 1)

        def pe_prefix(n):
            nc.tensor.wait_ge(flag_ready, n + 1)
            nc.tensor.matmul(banks[2][:, :], tri, flags_row, start=True, stop=True)
            nc.tensor.matmul(banks[3][:, :], ones_b, flags_row, start=True, stop=True).then_inc(rank_done, 1)

        @block.tensor
        def _(pe):
            pe.wait_ge(aux_ready, 1)
            for m in range(K):
                for k in range(K):
                    ins = nc.tensor.matmul(banks[2][:, m * B:(m + 1) * B], mod_sq[:, k, m * P:(m + 1) * P],
                                           ysq[:, k, :], start=(m == 0 and k == 0), stop=(m == K - 1 and k == K - 1),
                                           skip_group_check=True)
            ins.then_inc(aux_done, 1)
            for b in range(B):
                if b >= 2:
                    pe.wait_ge(aux_root, b)
                for k in range(K):
                    ins = nc.tensor.matmul(banks[3 + b % 2][:, :], ysq_wide[:, k, b, :], mod_sq[:, k, :],
                                           start=(k == 0), stop=(k == K - 1))
                ins.then_inc(aux_done, 1)
            pe.wait_ge(aux_ready, 2)
            for ic in range(K):
                for k in range(K):
                    ins = nc.tensor.matmul(banks[5][:, ic * B * E:(ic + 1) * B * E],
                                           mod_t[:, k, ic * P:(ic + 1) * P], g_t[:, k, :, :],
                                           start=(ic == 0 and k == 0), stop=(ic == K - 1 and k == K - 1),
                                           skip_group_check=True)
            ins.then_inc(aux_done, 1)

            pe.wait_ge(split_ready, 1)
            pe.wait_ge(xblk_in[0], 16)
            pe.wait_ge(parts_in, 16 * 3)
            for f in zw_products(0, xblk[0]):
                f()
            for m in range(K):
                for k in range(K):
                    nc.tensor.matmul(sums(0, m, 0, B), wh[:, k, m * P:(m + 1) * P],
                                     h0[:, k, :], start=False, stop=False, skip_group_check=True)
            with pe.Fori(0, NBLK // 2 - 1) as i:
                pe_block(2 * i, 0)
                pe_block(2 * i + 1, 1)
            pe_block(NBLK - 2, 0)
            pe_block(NBLK - 1, 1, more=False)

            pe.wait_ge(gate_ready, 2 * S)
            pe.wait_ge(ident_ready, 1)
            pe_quant(0)
            pe_tile(0, 0)
            pe_tile(0, 1)
            with pe.Fori(1, B - 1) as b:
                pe_tile(b, 0)
                pe_tile(b, 1)
            pe_tile(B - 1, 0)
            pe_tile(B - 1, 1, more=False)

            with pe.Fori(0, BITS) as i:
                pe.wait_ge(cnt_ready, i + 1)
                nc.tensor.matmul(banks[0][:, 0:E], ones_b, cnt, start=True, stop=True).then_inc(count_done, 1)
            pe.wait_ge(cnt_ready, BITS + 1)
            nc.tensor.matmul(banks[0][:, 0:E], ones_b, cnt, start=True, stop=True).then_inc(count_done, 1)
            pe_prefix(0)
            pe_prefix(1)
            with pe.Fori(0, E // 2) as i:
                for par in range(2):
                    pe.wait_ge(hot_ready, 2 * i + par + 1)
                    for t in range(NT):
                        ins = nc.tensor.matmul(banks[4 + par][:, 0:GATHER * CT], onehot[par][:, t, :],
                                               carried[par][:, t, :, :], start=(t == 0), stop=(t == NT - 1))
                    ins.then_inc(hot_used, 1)

            pe_xe_t(0)
            pe_expert(0)
            with pe.Fori(1, E - 1) as e:
                pe_expert(e)
            pe_expert(E - 1, more=False)

        def act_block(n, par, unscale):
            for s in range(SB):
                at = n * STEP2 + 2 * s
                for j in range(2):
                    nc.scalar.wait_ge(pre_ready, at + j + 1)
                    nc.scalar.activation(gate[:, j * HC:(j + 1) * HC, 1].rearrange("p (k b) -> p k b", b=B),
                                         pre(par, j, s), ACT.Sigmoid,
                                         scale=unscale).then_inc(gate_ready, 1)
                for j in range(2):
                    v = hv[:, j * HC:(j + 1) * HC, 1]
                    nc.scalar.wait_ge(v_ready, at + j + 1)
                    nc.scalar.activation(h_hi_flat[:, j * HC:(j + 1) * HC], v, ACT.Tanh).then_inc(hi_ready, 1)
                    if s == 0 and j == 0 and not (isinstance(n, int) and n < 2):
                        nc.scalar.wait_ge(states_moved, n - 1)
                        nc.scalar.wait_ge(max_taken, 2 * (n - 1))
                    nc.scalar.activation(hring_flat[par][:, s, j * HC:(j + 1) * HC], v,
                                         ACT.Tanh).then_inc(h_ready, 1)

        def act_chunks(t):
            for m in range(K):
                nc.scalar.wait_ge(acc_ready, t * K + m + 1)
                if not (isinstance(t, int) and t == 0 and m < 2):
                    nc.scalar.wait_ge(xp_ready, t * K + m - 1)
                nc.scalar.activation(ffn[m % 2], ACC[m % 2][:, :], ACT.Identity, bias=vecs[:, K + m:K + m + 1],
                                     scale=vecs[:, 2 * K + m:2 * K + m + 1]).then_inc(ffn_ready, 1)

        def act_tile(b, half, more=True):
            t = b * 2 + half
            if more:
                act_chunks(t + 1)
            for s in range(SUB):
                u, par = t * SUB + s, s % 2
                nc.scalar.wait_ge(y_ready, u + 1)
                if not (isinstance(t, int) and t == 0 and s < 2):
                    nc.scalar.wait_ge(rstd_ready, u - 1)
                nc.scalar.activation(sq_out, yrow[par], ACT.Square, accum_out=ss[:, par:par + 1]).then_inc(sq_ready, 1)
                nc.scalar.wait_ge(sq_ready, u + 1)
                nc.scalar.activation(ss[:, 2 + par:3 + par], ss[:, par:par + 1], ACT.Sqrt, bias=small[:, 11:12],
                                     scale=1.0 / H).then_inc(root_ready, 1)
                nc.scalar.wait_ge(tr_ready, u + 1)
                if not (isinstance(t, int) and t == 0 and s < 2):
                    nc.scalar.wait_ge(out_stored[par], out_value(b, half, s))
                nc.scalar.activation(orow[par], TRB[par][:, :], ACT.Copy).then_inc(orow_ready, 1)

        def out_value(b, half, s):
            return b * (16 * SUB) + 16 * ((half * SUB + s) // 2)

        def bias_value(e, par):
            return (e - par) * 16 + 32

        @block.scalar
        def _(act):
            act.wait_ge(aux_done, 1)
            act.wait_ge(eps_ready, 1)
            nc.scalar.activation(d_t.rearrange("p k b -> p (k b)"), banks[2][:, 0:K * B], ACT.Sqrt,
                                 bias=small[:, 10:11]).then_inc(aux_root, 1)
            for b in range(B):
                act.wait_ge(aux_done, b + 2)
                nc.scalar.activation(d_rows[:, b, :], banks[3 + b % 2][:, :], ACT.Sqrt,
                                     bias=small[:, 10:11]).then_inc(aux_root, 1)
            act.wait_ge(split_ready, 1)
            unscale = act.alloc_register("unscale")
            act.reg_load(unscale, small[0:1, 1:2].bitcast(i32))
            act_block(0, 0, unscale)
            act_block(1, 1, unscale)
            with act.Fori(1, NBLK // 2) as i:
                act_block(2 * i, 0, unscale)
                act_block(2 * i + 1, 1, unscale)

            act.wait_ge(hmax_ready, 1)
            act_chunks(0)
            act_tile(0, 0)
            act_tile(0, 1)
            with act.Fori(1, B - 1) as b:
                act_tile(b, 0)
                act_tile(b, 1)
            act_tile(B - 1, 0)
            act_tile(B - 1, 1, more=False)

            act.wait_ge(logit_ready, 1)
            nc.scalar.activation(probs, probs, ACT.Exp).then_inc(exp_ready, 1)

            def mid_half(e, par):
                nc.scalar.wait_ge(bias_in[par], bias_value(e, par))
                for f in range(F):
                    for half in range(2):
                        j = 2 * f + half
                        nc.scalar.wait_ge(mid_pre, e * (2 * F) + j + 1)
                        nc.scalar.activation(mid[:, f, half * 512:(half + 1) * 512], banks[4 + j % 4][:, :],
                                             ACT.Gelu, bias=fc1_bias[par][:, f:f + 1]).then_inc(mid_ready, 1)

            with act.Fori(0, E // 2) as i:
                mid_half(2 * i, 0)
                mid_half(2 * i + 1, 1)

        def dve_block(n, par):
            v = nc.vector
            for s in range(SB):
                at = n * STEP2 + 2 * s
                if s == 0:
                    v.wait_ge(zl_ready, n + 1)
                for j in range(2):
                    c = slice(j * HC, (j + 1) * HC)
                    v.wait_ge(gate_ready, at + j + 1)
                    v.wait_ge(lh_ready, at + j + 1)
                    v.tensor_tensor_scan(hv[:, c, :].rearrange("p c w -> p (c w)"),
                                         gate[:, c, :].rearrange("p c w -> p (c w)"),
                                         zl[par][:, s, c, :].rearrange("p c w -> p (c w)"), 0.0,
                                         ALU.mult, ALU.add).then_inc(v_ready, 1)
                for j in range(2):
                    c = slice(j * HC, (j + 1) * HC)
                    hr = hring_flat[par][:, s, c]
                    v.wait_ge(h_ready, at + j + 1)
                    v.tensor_tensor(h_lo_flat[:, c], hr, h_hi_flat[:, c], ALU.subtract).then_inc(lo_ready, 1)
                    nxt = zl[par][:, s + 1, c, 1] if s < SB - 1 else zl[1 - par][:, 0, c, 1]
                    v.tensor_tensor(nxt, hr, leak[:, c], ALU.mult).then_inc(lh_ready, 1)
                if s % (SB // 2) == SB // 2 - 1:
                    q = s // (SB // 2)
                    v.tensor_reduce(hmax[:, bass.ds(2 * n + q, 1)],
                                    hring_flat[par][:, q * (SB // 2):(q + 1) * (SB // 2), :], AX.XY, ALU.max,
                                    apply_absolute_value=True).then_inc(max_taken, 1)

        def dve_quant(b, half, t):
            v = nc.vector
            hb = hs[:, b, :, half * TT:(half + 1) * TT] if isinstance(b, int) else \
                hs[:, bass.ds(b, 1), :, half * TT:(half + 1) * TT].rearrange("p b k t -> p (b k) t")
            if not (isinstance(t, int) and t == 0):
                v.wait_ge(acc_ready, t * K)
            v.tensor_scalar(hb, hb, vecs[:, 3 * K:3 * K + 1], ROUND, ALU.mult, ALU.add).then_inc(q_raw, 1)
            v.wait_ge(q_raw, t + 1)
            v.tensor_scalar(q_sb, hb, ROUND, 127.0, ALU.subtract, ALU.min).then_inc(q_ready, 1)

        def dve_add(b, half, t):
            v = nc.vector
            v.wait_ge(xt_in[half], b * 16 + 16)
            for m in range(K):
                v.wait_ge(ffn_ready, t * K + m + 1)
                v.tensor_tensor(xt[half][:, m, :], xt[half][:, m, :], ffn[m % 2], ALU.add).then_inc(xp_ready, 1)

        def dve_finish(b, u, par):
            v = nc.vector
            v.wait_ge(root_ready, u + 1)
            v.reciprocal(rstd[:, bass.ds(u, 1)], ss[:, 2 + par:3 + par]).then_inc(rstd_ready, 1)
            v.wait_ge(rstd_ready, u + 1)
            v.scalar_tensor_tensor(yrow[par], yrow[par], rstd[:, bass.ds(u, 1)], nw_bc, ALU.mult,
                                   ALU.mult).then_inc(xn_ready, 1)
            v.wait_ge(lg_ready, u + 1)
            v.tensor_scalar(probs[:, bass.ds(u * E, E)], LGB[par][:, bass.ds(b * E, E)], rstd[:, bass.ds(u, 1)],
                            None, ALU.mult).then_inc(lg_used, 1)

        def dve_tile(b, half, quant=True, add=True):
            v = nc.vector
            t = b * 2 + half
            nb, nh = (b, 1) if half == 0 else (b + 1, 0)
            if half == 0:
                if not (isinstance(b, int) and b == 0):
                    v.wait_ge(xc_ready, b * (2 * SUB))
                for k in range(K):
                    ins = v.tensor_scalar(wb[:, k, :], mod_sb[:, k, :], ys_of(k, b), None, ALU.mult)
                ins.then_inc(wb_ready, 1)
            if add:
                dve_add(nb, nh, t + 1)
            if quant:
                dve_quant(b + 1, half, t + 2)
            for s in range(SUB):
                u, par = t * SUB + s, s % 2
                v.wait_ge(xc_ready, u + 1)
                if not (isinstance(t, int) and t == 0 and s < 2):
                    v.wait_ge(xn_stored[par], out_value(b, half, s))
                v.tensor_tensor(yrow[par], XCB[par][:, :], drow(b), ALU.mult).then_inc(y_ready, 1)
                dve_finish(b, u, par)

        def drow(b):
            return d_flat[:, bass.ds(b * H, H)]

        def ys_of(k, b):
            return ys_flat[:, bass.ds(b + k * B, 1)]

        def dve_count(c):
            v = nc.vector

        def dve_prefix(n):
            v = nc.vector
            v.wait_ge(rank_done, n + 1)
            chain(v.tensor_copy(tot.rearrange("p e t -> p (e t)"), banks[3][:, :]))
            for e in range(E):
                ins = v.tensor_tensor_scan(cum[:, e, :], ones64, tot[:, e, :], 0.0, ALU.mult, ALU.add)
            chain(ins)
            chain(v.tensor_tensor(cum, cum, tot, ALU.subtract))
            chain(v.tensor_tensor(rank.rearrange("p e t -> p (e t)"), banks[2][:, :],
                                  cum.rearrange("p e t -> p (e t)"), ALU.add))

        @block.vector
        def _(dve):
            v = nc.vector
            v.memset(ones_f, 1.0)
            v.memset(ones_b, 1.0)
            v.memset(small[:, 10:11], EPS_D)
            chain(v.memset(small[:, 11:12], EPS_N))
            dve.sem_inc(eps_ready, 1)
            v.wait_ge(loaded, 16 * LOADS)
            v.wait_ge(aux_in, 16 * AUX_LOADS)
            chain(v.tensor_scalar(ys_flat, h0.rearrange("p k b -> p (k b)"), float(H) ** -0.5, None, ALU.mult))
            chain(v.tensor_tensor(ysq, ys, ys, ALU.mult))
            v.tensor_copy(ysq_wide, bc(ysq[:, :, :, None], [P, K, B, P]))
            chain(v.tensor_tensor(mod_sq, mod_sb, mod_sb, ALU.mult))
            dve.sem_inc(aux_ready, 1)
            for k in range(K):
                ins = v.tensor_scalar(rnw[:, k, :], rt_t[:, k, :], nw_t[:, k:k + 1], None, ALU.mult)
            chain(ins)
            v.wait_ge(aux_root, 1)
            chain(v.reciprocal(d_t, d_t))
            for k in range(K):
                ins = v.tensor_tensor(g_t[:, k], bc(d_t[:, k, :, None], [P, B, E]),
                                      bc(rnw[:, k, None, :], [P, B, E]), ALU.mult)
            chain(ins)
            dve.sem_inc(aux_ready, 1)
            v.tensor_copy(qw_sb, qw_i8)
            v.memset(route_sb, 0.0)
            v.wait_ge(aux_root, B + 1)
            chain(v.reciprocal(d_flat, d_flat))
            v.wait_ge(aux_done, B + 2)
            for ic in range(K):
                ins = v.tensor_tensor(route_sb[:, ic, 0:B * E].rearrange("p (b e) -> p b e", b=B),
                                      banks[5][:, ic * B * E:(ic + 1) * B * E].rearrange("p (b e) -> p b e", b=B),
                                      bc(ys[:, ic, :, None], [P, B, E]), ALU.mult)
            chain(ins)

            v.tensor_reduce(small[:, 2:3], wh, AX.XY, ALU.max, apply_absolute_value=True)
            chain(v.tensor_reduce(small[:, 3:4], wz, AX.XY, ALU.max, apply_absolute_value=True))
            v.tensor_tensor(small[:, 4:5], small[:, 2:3], small[:, 3:4], ALU.max).then_inc(wmax_in, 1)
            v.wait_ge(wmax_out, 1)
            scale_bits = small[:, 6:7].bitcast(i32)
            chain(v.tensor_scalar(scale_bits, small[:, 5:6].bitcast(i32), 0x7F800000, None, ALU.bitwise_and))
            chain(v.tensor_scalar(scale_bits, scale_bits, float(20 * EXP_ONE), None, ALU.max))
            v.tensor_scalar(small[:, 0:1].bitcast(i32), scale_bits, -1.0, float(267 * EXP_ONE), ALU.mult, ALU.add)
            chain(v.tensor_scalar(small[:, 1:2].bitcast(i32), scale_bits, float(13 * EXP_ONE), None, ALU.subtract))
            v.tensor_scalar(wz, wz, small[:, 0:1], None, ALU.mult)
            chain(v.tensor_scalar(gb_row[0:1, :], gb_row[0:1, :], small[0:1, 0:1], None, ALU.mult))
            for part in gb_part:
                chain(v.tensor_copy(part[0:1, :], gb_row[0:1, :]))
                chain(v.tensor_tensor(gb_row[0:1, :], gb_row[0:1, :], part[0:1, :], ALU.subtract))
            v.sem_inc(parts_ready, 1)
            chain(v.tensor_scalar(wh, wh, small[:, 0:1], None, ALU.mult))
            chain(v.tensor_copy(wh_hi, wh))
            chain(v.tensor_tensor(wh_lo, wh, wh_hi, ALU.subtract))
            chain(v.tensor_scalar(alpha_sb, alpha_sb, -1.0, 1.0, ALU.mult, ALU.add))
            chain(v.tensor_copy(leak.rearrange("p (k b) -> p k b", k=K), bc(alpha_sb[:, :, None], [P, K, B])))
            chain(v.tensor_tensor(zl[0][:, 0, :, 1], leak, h0.rearrange("p k b -> p (k b)"), ALU.mult))
            chain(v.memset(gate, 0.0))
            v.memset(h_lo, 0.0)
            chain(v.memset(h_hi, 0.0))
            for x in (hi_ready, lo_ready, lh_ready):
                dve.sem_inc(x, 2)
            dve.sem_inc(split_ready, 1)
            with dve.Fori(0, NBLK // 2) as i:
                dve_block(2 * i, 0)
                dve_block(2 * i + 1, 1)

            v.wait_ge(max_taken, 2 * NBLK)
            v.tensor_reduce(small[:, 12:13], hmax, AX.X, ALU.max).then_inc(hmax_in, 1)
            v.wait_ge(hmax_out, 1)
            chain(v.tensor_scalar(small[:, 14:15], small[:, 13:14], 1.0 / 127.0, 1e-5, ALU.mult, ALU.max))
            v.reciprocal(vecs[:, 3 * K:3 * K + 1], small[:, 14:15])
            chain(v.tensor_scalar(vecs[:, 2 * K:3 * K], vecs[:, 0:K], small[:, 14:15], None, ALU.mult))
            dve.sem_inc(hmax_ready, 1)
            v.wait_ge(states_moved, NBLK)
            dve_quant(0, 0, 0)
            dve_add(0, 0, 0)
            dve_quant(0, 1, 1)
            dve_tile(0, 0)
            dve_tile(0, 1)
            with dve.Fori(1, B - 1) as b:
                dve_tile(b, 0)
                dve_tile(b, 1)
            dve_tile(B - 1, 0, quant=False)
            dve_tile(B - 1, 1, quant=False, add=False)

            v.wait_ge(iota_ready, 6)
            v.wait_ge(lg_used, NT)
            pr = probs.rearrange("p (t e) -> p t e", t=NT)
            chain(v.tensor_tensor(pr, pr, bc(rb_sb[:, None, :], [P, NT, E]), ALU.add))
            chain(v.tensor_reduce(gsum, pr, AX.X, ALU.max))
            v.tensor_tensor(pr, pr, bc(gsum[:, :, None], [P, NT, E]), ALU.subtract).then_inc(logit_ready, 1)
            v.wait_ge(exp_ready, 1)
            chain(v.tensor_reduce(gsum, pr, AX.X, ALU.add))
            chain(v.reciprocal(gsum, gsum))
            pe_view = p_et.rearrange("p e t -> p t e")
            chain(v.tensor_tensor(pe_view, pr, bc(gsum[:, :, None], [P, NT, E]), ALU.mult))

            v.memset(thr, 0)
            chain(v.memset(bit, 1 << (BITS - 1)))

            def count(flag, n):
                with nc.allow_low_precision(reason="at most 64 flags, which bf16 holds exactly"):
                    nc.vector.tensor_reduce(cnt, flag, AX.X, ALU.add).then_inc(cnt_ready, 1)
                nc.vector.wait_ge(count_done, n + 1)

            STEPS = 6
            base = chain.n

            def link(ins, i, j):
                ins.then_inc(dve_loop, 1)
                nc.vector.wait_ge(dve_loop, i * STEPS + j)

            with dve.Fori(0, BITS) as i:
                link(v.tensor_scalar(cand, thr, bit[:, 0:1], None, ALU.bitwise_or), i, 1)
                link(v.tensor_tensor(flags, p_et, bc(cand.bitcast(f32)[:, :, None], [P, E, NT]), ALU.is_ge), i, 2)
                count(flags, i)
                link(v.tensor_scalar(hit, banks[0][:, 0:E], float(CAP), -1.0, ALU.is_ge, ALU.mult), i, 3)
                link(v.tensor_scalar(hit, hit, bit[:, 0:1], None, ALU.bitwise_and), i, 4)
                link(v.tensor_tensor(thr, thr, hit, ALU.bitwise_or), i, 5)
                link(v.tensor_scalar(bit, bit, 1, None, ALU.logical_shift_right), i, 6)

            thr_b = bc(thr.bitcast(f32)[:, :, None], [P, E, NT])
            chain(v.tensor_tensor(flags, p_et, thr_b, ALU.is_gt))
            count(flags, BITS)
            chain(v.tensor_scalar(need, banks[0][:, 0:E], -1.0, float(CAP), ALU.mult, ALU.add))
            chain(v.tensor_copy(flags2, flags))
            v.tensor_tensor(flags, p_et, thr_b, ALU.is_equal).then_inc(flag_ready, 1)
            dve_prefix(0)
            chain(v.tensor_tensor(rank, rank, bc(need[:, :, None], [P, E, NT]), ALU.is_lt))
            chain(v.tensor_tensor(rank, rank, flags, ALU.mult))
            v.tensor_tensor(flags, flags2, rank, ALU.add).then_inc(flag_ready, 1)
            dve_prefix(1)
            chain(v.tensor_tensor(wsel, flags, p_et, ALU.mult))
            chain(v.tensor_reduce(gsum, wsel.rearrange("p e t -> p t e"), AX.X, ALU.add))
            chain(v.tensor_scalar(gsum, gsum, 1e-9, None, ALU.max))
            chain(v.reciprocal(gsum, gsum))
            chain(v.tensor_tensor(wsel, wsel, bc(gsum[:, None, :], [P, E, NT]), ALU.mult))
            chain(v.tensor_scalar(cum, flags, -float(T), float(T), ALU.mult, ALU.add))
            chain(v.tensor_tensor(slot_i, rank, cum, ALU.add))
            chain(v.tensor_scalar(part_i, slot_i, P - 1, None, ALU.bitwise_and))
            chain(v.tensor_copy(slot_lo, part_i))
            chain(v.tensor_scalar(part_i, slot_i, 7, None, ALU.logical_shift_right))
            chain(v.tensor_copy(slot_hi, part_i))
            v.tensor_copy(vals[:, :, :, 0], bc(row_i[:, None, :], [P, E, NT]))
            v.tensor_copy(vals[:, :, :, 1], bc(tile_i[:, None, :], [P, E, NT]))
            chain(v.tensor_copy(vals[:, :, :, 2], wsel))
            chain(v.tensor_tensor(wres, wsel, vals[:, :, :, 2], ALU.subtract))
            chain(v.tensor_copy(vals[:, :, :, 3], wres))
            chain(v.tensor_tensor(vals[:, :, :, 4], wres, vals[:, :, :, 3], ALU.subtract))
            chain(v.tensor_copy(iota_p, iota_i))
            chain(v.tensor_copy(iota_c, iota_i[:, 0:CT]))

            def lists(e, par):
                lo = slot_lo.rearrange("p e t -> p (e t)")[:, bass.ds(e * NT, NT)]
                hi = slot_hi.rearrange("p e t -> p (e t)")[:, bass.ds(e * NT, NT)]
                va = vals_flat[:, bass.ds(e * (NT * GATHER), NT * GATHER)].rearrange("p (t v) -> p t v", v=GATHER)
                if not (isinstance(e, int) and e < 2):
                    v.wait_ge(hot_used, e - 1)
                v.tensor_tensor(onehot[par], bc(iota_p[:, None, :], [P, NT, P]), bc(lo[:, :, None], [P, NT, P]),
                                ALU.is_equal)
                if not (isinstance(e, int) and e == 0):
                    v.wait_ge(hot_ready, e)
                v.tensor_tensor(hi_hot, bc(iota_c[:, None, :], [P, NT, CT]), bc(hi[:, :, None], [P, NT, CT]),
                                ALU.is_equal).then_inc(hi_hot_ready, 1)
                v.wait_ge(hi_hot_ready, e + 1)
                v.tensor_tensor(carried[par], bc(hi_hot[:, :, None, :], [P, NT, GATHER, CT]),
                                bc(va[:, :, :, None], [P, NT, GATHER, CT]), ALU.mult).then_inc(hot_ready, 1)

            def take_list(e, par):
                v.wait_ge(hot_used, e + 1)
                if not isinstance(e, int):
                    v.wait_ge(idx_ready, e)
                v.tensor_copy(got, banks[4 + par][:, 0:GATHER * CT]).then_inc(got_ready, 1)
                v.wait_ge(got_ready, 3 * e + 1)
                g3 = got.rearrange("p (v c) -> p v c", v=GATHER)
                v.tensor_tensor(g3[:, 2, :], g3[:, 2, :], g3[:, 3, :], ALU.add).then_inc(got_ready, 1)
                v.wait_ge(got_ready, 3 * e + 2)
                v.tensor_tensor(w_flat[:, bass.ds(e * CT, CT)], g3[:, 2, :], g3[:, 4, :], ALU.add)
                v.scalar_tensor_tensor(idx_flat[:, bass.ds(e * CT, CT)], g3[:, 1, :], float(P), g3[:, 0, :],
                                       ALU.mult, ALU.add).then_inc(got_ready, 1)
                v.wait_ge(got_ready, 3 * e + 3)
                v.sem_inc(idx_ready, 1)

            lists(0, 0)
            lists(1, 1)
            take_list(0, 0)
            with dve.Fori(1, E // 2) as i:
                lists(2 * i, 0)
                take_list(2 * i - 1, 1)
                lists(2 * i + 1, 1)
                take_list(2 * i, 0)
            take_list(E - 1, 1)

            def move_xe(e):
                for c in range(CT):
                    v.wait_ge(xtr_ready, e * CT + c + 1)
                    v.tensor_copy(xe_t[:, :, c * P:(c + 1) * P],
                                  banks[c % 2][:, :].rearrange("p (k n) -> p k n", k=K)).then_inc(xtr_moved, 1)

            def current(e, par):
                v.tensor_copy(w_cur[par], w_flat[:, bass.ds(e * CT, CT)])
                v.tensor_copy(idx_cur[par], idx_flat[:, bass.ds(e * CT, CT)]).then_inc(cur_ready, 1)

            def finish_expert(e, par, more=True):
                if more:
                    if not (isinstance(e, int) and e == 0):
                        for c in range(4):
                            v.wait_ge(ye_stored[c], e * 32)
                    current(e + 1, 1 - par)
                    move_xe(e + 1)
                v.wait_ge(bias_in[par], bias_value(e, par))
                for c in range(CT):
                    v.wait_ge(y_pre, e * CT + c + 1)
                    if not (isinstance(e, int) and e == 0 and c < 4):
                        v.wait_ge(ye_stored[c % 4], e * 32 + 16 * (c // 4))
                    v.tensor_tensor(ye[c % 4], banks[2 + c % 2][:, :], fc2_bias[par], ALU.add).then_inc(y_sum, 1)
                    v.wait_ge(y_sum, e * CT + c + 1)
                    v.tensor_scalar(ye[c % 4], ye[c % 4], w_cur[par][:, c:c + 1], None, ALU.mult).then_inc(ye_ready, 1)

            v.wait_ge(idx_ready, E)
            current(0, 0)
            move_xe(0)
            finish_expert(0, 0)
            finish_expert(1, 1)
            with dve.Fori(1, E // 2 - 1) as i:
                finish_expert(2 * i, 0)
                finish_expert(2 * i + 1, 1)
            finish_expert(E - 2, 0)
            finish_expert(E - 1, 1, more=False)

        def pool_spread(n, par):
            g = nc.gpsimd
            g.wait_ge(xblk_in[par], 16 * (n // 2 + 1) if isinstance(n, int) else 8 * (n - par) + 16)
            if not (isinstance(n, int) and n < 2):
                g.wait_ge(v_ready, (n - 1) * STEP2)
            g.sem_inc(pool_turn, 1)
            g.tensor_copy(zl[par][:, :, :, 0].rearrange("p t (k b) -> p t k b", k=K),
                          xblk[par].rearrange("p k t b -> p t k b")).then_inc(zl_ready, 1)

        def pool_block(n, par):
            g = nc.gpsimd
            g.wait_ge(h_ready, (n + 1) * STEP2)
            g.tensor_copy(hs[:, :, :, bass.ds(n * SB, SB)],
                          hring[par].rearrange("p t k b -> p b k t")).then_inc(states_moved, 1)

        @block.gpsimd
        def _(pool):
            g = nc.gpsimd
            pchain(g.memset(ident, 0.0))
            g.affine_select(out=ident, in_=ident, compare_op=ALU.not_equal, fill=1.0, base=0,
                            pattern=[[-1, P]], channel_multiplier=1).then_inc(ident_ready, 1)
            g.wait_ge(wmax_in, 1)
            g.partition_all_reduce(small[:, 5:6], small[:, 4:5], P, ABSMAX).then_inc(wmax_out, 1)
            g.wait_ge(split_ready, 1)
            pool_spread(0, 0)
            pool_spread(1, 1)
            with pool.Fori(0, NBLK // 2 - 1) as i:
                for par in range(2):
                    pool_block(2 * i + par, par)
                    pool_spread(2 * i + 2 + par, par)
            pool_block(NBLK - 2, 0)
            pool_block(NBLK - 1, 1)
            g.wait_ge(hmax_in, 1)
            g.partition_all_reduce(small[:, 13:14], small[:, 12:13], P, ABSMAX).then_inc(hmax_out, 1)

            def load_x(b, half):
                t = b * 2 + half
                g.dma_start(xt[half], x_feat3[:, :, bass.ds(t * TT, TT)]).then_inc(xt_in[half], 16)

            g.wait_ge(hmax_out, 1)
            load_x(0, 0)
            load_x(0, 1)
            with pool.Fori(1, B) as b:
                for half in range(2):
                    g.wait_ge(tr_ready, (b * 2 + half - 1) * SUB)
                    load_x(b, half)

            g.wait_ge(lg_used, NT)
            for par in range(2):
                g.wait_ge(xn_stored[par], 16 * NT // 2)
                g.wait_ge(out_stored[par], 16 * NT // 2)
            g.memset(ones64, 1.0).then_inc(iota_ready, 1)
            pchain(g.memset(tri, 1.0))
            g.affine_select(out=tri, in_=tri, compare_op=ALU.is_gt, fill=0.0, base=0, pattern=[[1, P]],
                            channel_multiplier=-1).then_inc(iota_ready, 1)
            g.iota(iota_i, pattern=[[1, P]], base=0, channel_multiplier=0).then_inc(iota_ready, 1)
            g.iota(row_i, pattern=[[0, NT]], base=0, channel_multiplier=1).then_inc(iota_ready, 1)
            g.iota(tile_i, pattern=[[1, NT]], base=0, channel_multiplier=0).then_inc(iota_ready, 1)
            g.wait_ge(iota_ready, 5)
            g.sem_inc(iota_ready, 1)

            def gather(e, par):
                g.wait_ge(cur_ready, e + 1)
                if not (isinstance(e, int) and e == 0):
                    g.wait_ge(xtr_ready, e * CT)
                g.sem_inc(pool_turn, 1)
                for c in range(CT):
                    g.indirect_dma_start(xe_row[:, c, :], None, xn_rows[:, :],
                                         bass.IndirectOffsetOnAxis(idx_cur[par][:, c:c + 1].bitcast(u32), 0)
                                         ).then_inc(xe_in, 16)

            def scatter(e, par):
                if not (isinstance(e, int) and e == 0):
                    for c in range(4):
                        g.wait_ge(ye_stored[c], e * 32)
                for c in range(CT):
                    g.wait_ge(ye_ready, e * CT + c + 1)
                    g.sem_inc(pool_turn, 1)
                    g.indirect_dma_start(out[:, :],
                                         bass.IndirectOffsetOnAxis(idx_cur[par][:, c:c + 1].bitcast(u32), 0),
                                         ye[c % 4], None, compute_op=ALU.add).then_inc(ye_stored[c % 4], 16)

            for par in range(2):
                g.wait_ge(xn_stored[par], 16 * NT // 2)
                g.wait_ge(out_stored[par], 16 * NT // 2)
            gather(0, 0)
            gather(1, 1)
            scatter(0, 0)
            with pool.Fori(1, E // 2) as i:
                gather(2 * i, 0)
                scatter(2 * i - 1, 1)
                gather(2 * i + 1, 1)
                scatter(2 * i, 0)
            scatter(E - 1, 1)


def kernel(x, cond_1024, L0_cond_W, L0_cond_b, L0_cond_alpha, L0_ffn_weight_int8, L0_ffn_weight_scale,
           L0_ffn_bias, L1_cond_weight, L1_ffn_norm_weight, L1_ffn_router_w, L1_ffn_router_b,
           L1_ffn_fc1_w, L1_ffn_fc1_b, L1_ffn_fc2_w, L1_ffn_fc2_b):
    import numpy as np
    import concourse.bacc as bacc
    from concourse import mybir as _mybir
    from concourse.bass_utils import run_bass_kernel_spmd

    B, S, H = x.shape
    P = 128
    K = H // P
    E, FF, _ = L1_ffn_fc1_w.shape
    x, W = np.asarray(x), np.asarray(L0_cond_W)

    def by_part(m):
        m = np.asarray(m)
        n = m.shape[1]
        return np.ascontiguousarray(m.reshape(-1, P, n).transpose(1, 0, 2).reshape(P, -1))

    def cols(v):
        return np.ascontiguousarray(np.asarray(v).reshape(-1, P).T)

    def row(v):
        return np.ascontiguousarray(np.asarray(v).reshape(1, -1))

    fc1 = np.asarray(L1_ffn_fc1_w).reshape(E, FF, K, P).transpose(0, 3, 2, 1).reshape(E * P, K * FF)
    fc2 = np.asarray(L1_ffn_fc2_w).reshape(E, H, FF // P, P).transpose(0, 3, 2, 1).reshape(E * P, FF // P * H)
    arrays = {
        "x_scan": x.reshape(B, S // 16, 16, K, P).transpose(4, 1, 3, 2, 0).reshape(P, S * K * B),
        "x_feat": x.reshape(B * S, K, P).transpose(2, 1, 0).reshape(P, K * B * S),
        "cond_t": by_part(np.asarray(cond_1024).T),
        "wh_t": by_part(W[:, :H].T),
        "wz_t": by_part(W[:, H:].T),
        "gate_bias": row(L0_cond_b),
        "alpha": cols(L0_cond_alpha),
        "q_weight_t": by_part(np.asarray(L0_ffn_weight_int8).T).view(np.int32),
        "q_vecs": np.concatenate([cols(np.asarray(L0_ffn_weight_scale).reshape(-1)), cols(L0_ffn_bias)], axis=1),
        "mod_w": by_part(L1_cond_weight),
        "mod_w_t": by_part(np.asarray(L1_cond_weight).T),
        "norm_w_t": cols(L1_ffn_norm_weight),
        "norm_w_row": row(L1_ffn_norm_weight),
        "router_t": by_part(np.asarray(L1_ffn_router_w).T),
        "router_b": row(L1_ffn_router_b),
        "fc1_t": fc1,
        "fc1_b": np.asarray(L1_ffn_fc1_b).reshape(E, FF // P, P).transpose(0, 2, 1).reshape(E * P, FF // P),
        "fc2_t": fc2,
        "fc2_b": L1_ffn_fc2_b,
    }
    nc = bacc.Bacc("TRN2", target_bir_lowering=False, num_devices=1)
    arrays = {n: np.ascontiguousarray(a) for n, a in arrays.items()}
    aps = [nc.dram_tensor(f"{n}_dram", a.shape, _mybir.dt.from_np(a.dtype), kind="ExternalInput").ap()
           for n, a in arrays.items()]
    out = nc.dram_tensor("out_dram", (B * S, H), _mybir.dt.float32, kind="ExternalOutput").ap()
    adaln_ffn_kernel(nc, *aps, out)
    r = run_bass_kernel_spmd(nc, [{f"{n}_dram": a for n, a in arrays.items()}], core_ids=[0])
    return r.results[0]["out_dram"].reshape(B, S, H)
```

```python
import concourse.bass as bass
from concourse import mybir
from contextlib import ExitStack


def adaln_ffn_kernel(nc, x_scan, x_feat, cond_t, wh_t, wz_t, gate_bias, alpha, q_weight_t, q_vecs,
                     mod_w, mod_w_t, norm_w_t, norm_w_row, router_t, router_b, fc1_t, fc1_b,
                     fc2_t, fc2_b, out):
    f32, f16, bf16 = mybir.dt.float32, mybir.dt.float16, mybir.dt.bfloat16
    i32, u32 = mybir.dt.int32, mybir.dt.uint32
    ALU = mybir.AluOpType
    ACT = mybir.ActivationFunctionType
    AX = mybir.AxisListType

    P = 128
    B, S, H = 8, 1024, 512
    K = H // P
    T = B * S
    NT = T // P
    E, FF = 8, 2048
    F = FF // P
    CAP = T // E
    CT = CAP // P
    SB = 16
    NBLK = S // SB
    TT = 512
    SUB = TT // P
    ROUND = 1.5 * 2.0 ** 23
    EXP_ONE = 1 << 23
    BITS = 30
    ROUNDS = 5
    GATHER = 5

    ABSMAX = bass.bass_isa.ReduceOp.absmax

    def bc(ap, shape):
        return ap.to_broadcast(shape)

    with ExitStack() as ctx:
        def sem(name):
            return ctx.enter_context(nc.semaphore(name))

        ARENA = 53200
        arena = ctx.enter_context(nc.sbuf_tensor("arena", [P, ARENA], f32))
        banks = [ctx.enter_context(nc.psum_tensor(f"bank{n}", [P, 512], f32)) for n in range(8)]

        class Region:

            def __init__(self, at):
                self.at = at

            def take(self, words, dt=f32):
                lo, self.at = self.at, self.at + words
                assert self.at <= ARENA, self.at
                view = arena[:, lo:self.at]
                return view if dt == f32 else view.bitcast(dt)

        keep = Region(0)
        ident = keep.take(P)
        ident_h = keep.take(P // 2, f16)
        small = keep.take(64)
        ones_f = keep.take(P)
        ones_b = keep.take(P // 2, bf16)
        idx_all = keep.take(E * CT, i32).rearrange("p (e c) -> p e c", e=E)
        w_all = keep.take(E * CT).rearrange("p (e c) -> p e c", e=E)
        EXPERTS_AT = keep.at
        d_rows = keep.take(B * H)
        d_rows = d_rows.rearrange("p (b o) -> p b o", b=B)
        mod_sb = keep.take(K * H).rearrange("p (k o) -> p k o", k=K)
        route_sb = keep.take(K * B * E).rearrange("p (k n) -> p k n", k=K)
        route_hl = keep.take(K * B * E, f16).rearrange("p (h k n) -> p h k n", h=2, k=K)
        qw_sb = keep.take(K * H // 2, bf16).rearrange("p (k o) -> p k o", k=K)
        ys = keep.take(K * B).rearrange("p (k b) -> p k b", k=K)
        probs = keep.take(NT * E)
        rstd = keep.take(NT)
        rb_sb = keep.take(E)
        vecs = keep.take(4 * K)
        keep_nw = keep.take(H)
        AFTER_KEEP = keep.at

        scan = Region(AFTER_KEEP)
        hs = scan.take(B * K * S).rearrange("p (b k t) -> p b k t", b=B, k=K)
        AFTER_HS = scan.at
        wh_hi = scan.take(K * H // 2, f16).rearrange("p (k o) -> p k o", k=K)
        wh_lo = scan.take(K * H // 2, f16).rearrange("p (k o) -> p k o", k=K)
        wz = scan.take(K * H).rearrange("p (k o) -> p k o", k=K)
        xblk = [scan.take(SB * K * B).rearrange("p (k t b) -> p k t b", k=K, t=SB) for _ in range(2)]
        zl = [scan.take(SB * K * B * 2).rearrange("p (t c w) -> p t c w", t=SB, w=2) for _ in range(2)]
        hring = [scan.take(SB * K * B).rearrange("p (t k b) -> p t k b", t=SB, k=K) for _ in range(2)]
        h_hi = scan.take(K * B // 2, f16).rearrange("p (k b) -> p k b", k=K)
        h_lo = scan.take(K * B // 2, f16).rearrange("p (k b) -> p k b", k=K)
        gate = scan.take(K * B * 2).rearrange("p (c w) -> p c w", w=2)
        hv = scan.take(K * B * 2).rearrange("p (c w) -> p c w", w=2)
        leak = scan.take(K * B)
        h0 = scan.take(K * B).rearrange("p (k b) -> p k b", k=K)
        gb_row = scan.take(H)
        gb_part = [scan.take(H // 2, bf16) for _ in range(3)]
        gb_parts = scan.take(H // 2, bf16)
        hmax = scan.take(2 * NBLK)
        xmax = scan.take(K * NBLK)
        nw_bc = keep_nw
        pro = Region(AFTER_KEEP)
        wh = pro.take(K * H).rearrange("p (k o) -> p k o", k=K)
        mod_sq = pro.take(K * H).rearrange("p (k o) -> p k o", k=K)
        mod_t = pro.take(K * H).rearrange("p (k o) -> p k o", k=K)
        ysq = pro.take(K * B).rearrange("p (k b) -> p k b", k=K)
        d_t = pro.take(K * B).rearrange("p (k b) -> p k b", k=K)
        nw_t = pro.take(K)
        rt_t = pro.take(K * E).rearrange("p (k e) -> p k e", k=K)
        rnw = pro.take(K * E).rearrange("p (k e) -> p k e", k=K)
        g_t = pro.take(K * B * E).rearrange("p (k b e) -> p k b e", k=K, b=B)
        qw_words = pro.take(K * H // 4, i32)
        qw_i8 = qw_words.bitcast(mybir.dt.int8).rearrange("p (k o) -> p k o", k=K)
        alpha_sb = pro.take(K)

        dense = Region(AFTER_HS)
        xt = [dense.take(K * TT).rearrange("p (k t) -> p k t", k=K) for _ in range(2)]
        q_sb = dense.take(K * TT // 2, bf16).rearrange("p (k t) -> p k t", k=K)
        ffn = [dense.take(TT) for _ in range(2)]
        mod_hl = dense.take(K * H, f16).rearrange("p (h k o) -> p h k o", h=2, k=K)
        ys_scaled = dense.take(K * B)
        yrow = [dense.take(H) for _ in range(2)]
        orow = [dense.take(H) for _ in range(2)]
        ss = dense.take(8)

        pick = Region(AFTER_KEEP)
        p_et = pick.take(E * NT).rearrange("p (e t) -> p e t", e=E)
        flags = pick.take(E * NT // 2, bf16).rearrange("p (e t) -> p e t", e=E)
        flags2 = pick.take(E * NT // 2, bf16).rearrange("p (e t) -> p e t", e=E)
        above = pick.take(E * NT).rearrange("p (e t) -> p e t", e=E)
        rank = pick.take(E * NT).rearrange("p (e t) -> p e t", e=E)
        cum = pick.take(E * NT).rearrange("p (e t) -> p e t", e=E)
        tot = pick.take(E * NT).rearrange("p (e t) -> p e t", e=E)
        wsel = pick.take(E * NT).rearrange("p (e t) -> p e t", e=E)
        wres = pick.take(E * NT).rearrange("p (e t) -> p e t", e=E)
        slot_i = pick.take(E * NT, i32).rearrange("p (e t) -> p e t", e=E)
        part_i = pick.take(E * NT, i32).rearrange("p (e t) -> p e t", e=E)
        slot_lo = pick.take(E * NT // 2, bf16).rearrange("p (e t) -> p e t", e=E)
        slot_hi = pick.take(E * NT // 2, bf16).rearrange("p (e t) -> p e t", e=E)
        vals = pick.take(E * NT * GATHER // 2 + E, bf16)[:, 0:E * NT * GATHER].rearrange(
            "p (e t v) -> p e t v", e=E, v=GATHER)
        ones64 = pick.take(NT)
        tri = pick.take(P // 2, bf16)
        onehot = [pick.take(NT * P // 2, bf16).rearrange("p (t n) -> p t n", t=NT) for _ in range(2)]
        hi_hot = pick.take(NT * CT // 2, bf16).rearrange("p (t c) -> p t c", t=NT)
        carried = [pick.take(NT * CT * GATHER // 2, bf16).rearrange(
            "p (t v c) -> p t v c", t=NT, v=GATHER) for _ in range(2)]
        iota_p = pick.take(P // 2, bf16)
        iota_c = pick.take(CT // 2, bf16)
        iota_i = pick.take(P, i32)
        row_i = pick.take(NT, i32)
        tile_i = pick.take(NT, i32)
        thr = pick.take(E, i32)
        cand = pick.take(E, i32)
        bit = pick.take(1, i32)
        hit = pick.take(E, i32)
        cnt = pick.take(E // 2, bf16)
        gsum = pick.take(NT)
        need = pick.take(E)
        got = pick.take(GATHER * CT)

        moe = Region(EXPERTS_AT)
        raw = moe.take(F * H).rearrange("p (f n) -> p f n", f=F)
        fc1_hl = moe.take(F * H, f16).rearrange("p (h f k n) -> p h f k n", h=2, f=F, k=K)
        fc2_hl = moe.take(F * H, f16).rearrange("p (h f o) -> p h f o", h=2, f=F)
        mid = moe.take(F * CAP, f16).rearrange("p (h f c) -> p h f c", h=2, f=F)
        mid_f32 = [moe.take(H) for _ in range(4)]
        xe_row = [moe.take(H, f16) for _ in range(4)]
        xe_t = moe.take(K * CAP, f16).rearrange("p (h k c) -> p h k c", h=2, k=K)
        ye = [moe.take(H) for _ in range(4)]
        idx_cur = [moe.take(CT, i32) for _ in range(2)]
        w_cur = [moe.take(CT) for _ in range(2)]
        block_max = moe.take(F)
        scales = moe.take(16)
        fc1_bias = [moe.take(F) for _ in range(2)]
        fc2_bias = [moe.take(H) for _ in range(2)]

        d_dram = nc.dram_tensor("d_dram", [B, H], f32, kind="Internal").ap()
        xn_rows = nc.dram_tensor("xn_rows", [T, 2 * H], f16, kind="Internal").ap()

        loaded = sem("loaded")
        dve_step = sem("dve_step")
        pool_step = sem("pool_step")
        wmax_in = sem("wmax_in")
        wmax_out = sem("wmax_out")
        xblk_in = [sem(f"xblk_in{p}") for p in range(2)]
        pre_ready = sem("pre_ready")
        gate_ready = sem("gate_ready")
        v_ready = sem("v_ready")
        hi_ready = sem("hi_ready")
        h_ready = sem("h_ready")
        lo_ready = sem("lo_ready")
        lh_ready = sem("lh_ready")
        max_taken = sem("max_taken")
        split_ready = sem("split_ready")
        states_moved = sem("states_moved")
        zl_ready = sem("zl_ready")
        parts_ready = sem("parts_ready")
        parts_in = sem("parts_in")

        aux_in = sem("aux_in")
        aux_ready = sem("aux_ready")
        aux_done = sem("aux_done")
        aux_root = sem("aux_root")
        row_rooted = sem("row_rooted")
        d_row_ready = sem("d_row_ready")
        d_row_stored = sem("d_row_stored")
        d_rows_in = sem("d_rows_in")
        hmax_in = sem("hmax_in")
        hmax_out = sem("hmax_out")
        xt_in = [sem(f"xt_in{p}") for p in range(2)]
        q_ready = sem("q_ready")
        acc_ready = sem("acc_ready")
        ffn_ready = sem("ffn_ready")
        xp_ready = sem("xp_ready")
        xmax_taken = sem("xmax_taken")
        x_hi_ready = sem("x_hi_ready")
        x_lo_ready = sem("x_lo_ready")
        ys_ready = sem("ys_ready")
        mod_ready = sem("mod_ready")
        tr_ready = sem("tr_ready")
        orow_ready = sem("orow_ready")
        xc_ready = sem("xc_ready")
        y_ready = sem("y_ready")
        lg_ready = sem("lg_ready")
        lg_used = sem("lg_used")
        root_ready = sem("root_ready")
        rstd_ready = sem("rstd_ready")
        xn_ready = sem("xn_ready")
        out_stored = [sem(f"out_stored{p}") for p in range(2)]
        xn_stored = [sem(f"xn_stored{p}") for p in range(2)]
        logit_ready = sem("logit_ready")
        exp_ready = sem("exp_ready")
        iota_ready = sem("iota_ready")
        cnt_ready = sem("cnt_ready")
        count_done = sem("count_done")
        flag_ready = sem("flag_ready")
        rank_done = sem("rank_done")
        hot_ready = sem("hot_ready")
        hot_used = sem("hot_used")
        idx_ready = sem("idx_ready")
        hi_row_ready = sem("hi_row_ready")
        lo_row_ready = sem("lo_row_ready")
        raw_in = [sem(f"raw_in{q}") for q in range(4)]
        max_in = sem("max_in")
        max_out = sem("max_out")
        max_step = sem("max_step")
        fc1_scale_step = sem("fc1_scale_step")
        fc2_scale_step = sem("fc2_scale_step")
        scale_ready = sem("scale_ready")
        w_hi_ready = sem("w_hi_ready")
        w_lo_ready = sem("w_lo_ready")
        mid_f32_ready = sem("mid_f32_ready")
        mid_hi_ready = sem("mid_hi_ready")
        bias_in = [sem(f"bias_in{p}") for p in range(2)]
        cur_ready = sem("cur_ready")
        xe_in = [sem(f"xe_in{c}") for c in range(4)]
        xtr_ready = sem("xtr_ready")
        xtr_moved = sem("xtr_moved")
        mid_pre = sem("mid_pre")
        mid_ready = sem("mid_ready")
        y_pre = sem("y_pre")
        y_sum = sem("y_sum")
        ye_ready = sem("ye_ready")
        ye_stored = [sem(f"ye_stored{p}") for p in range(4)]
        dve_loop = sem("dve_loop")

        def chain(ins):
            chain.n += 1
            ins.then_inc(dve_step, 1)
            nc.vector.wait_ge(dve_step, chain.n)

        chain.n = 0

        def pchain(ins):
            pchain.n += 1
            ins.then_inc(pool_step, 1)
            nc.gpsimd.wait_ge(pool_step, pchain.n)

        pchain.n = 0

        sq_ready = sem("sq_ready")
        eps_ready = sem("eps_ready")
        load_turn = sem("load_turn")
        act_turn = sem("act_turn")
        pool_turn = sem("pool_turn")
        hmax_ready = sem("hmax_ready")
        q_raw = sem("q_raw")
        hi_hot_ready = sem("hi_hot_ready")
        got_ready = sem("got_ready")
        ident_ready = sem("ident_ready")
        h_hi_flat = h_hi.rearrange("p k b -> p (k b)")
        h_lo_flat = h_lo.rearrange("p k b -> p (k b)")
        hring_flat = [h.rearrange("p t k b -> p t (k b)") for h in hring]
        d_flat = d_rows.rearrange("p b o -> p (b o)")
        ys_flat = ys.rearrange("p k b -> p (k b)")
        vals_flat = vals.rearrange("p e t v -> p (e t v)")
        w_flat = w_all.rearrange("p e c -> p (e c)")
        idx_flat = idx_all.rearrange("p e c -> p (e c)")
        flags_row = flags.rearrange("p e t -> p (e t)")
        x_feat3 = x_feat.rearrange("p (k t) -> p k t", k=K)

        block = ctx.enter_context(nc.Block())

        hs_f32 = hs.rearrange("p b k t -> p (b k t)")
        hs_f16 = hs_f32.bitcast(f16)

        def spent_states(b, half, s):
            return hs_f32[:, bass.ds(b * (K * S) + (s * S + half * TT), H)]

        def xn_part(b, half, s, part):
            return hs_f16[:, bass.ds(b * (2 * K * S) + (2 * (s * S + half * TT) + part * H), H)]

        def xn_both(b, half, s):
            return hs_f16[:, bass.ds(b * (2 * K * S) + 2 * (s * S + half * TT), 2 * H)]

        hs_places = hs_f16.rearrange("p (b s w) -> p b s w", b=B, s=K)

        def x_part(b, half, part, k):
            at = 2 * half * TT + (part * K + k) * P
            return hs_places[:, bass.ds(b, 1), :, at:at + P].rearrange("p b s c -> p (b s) c")

        def x_operand(b, half, s, part, k):
            return hs_f16[:, bass.ds(b * (2 * K * S) + (2 * (s * S + half * TT) + (part * K + k) * P), P)]

        def before(b, half, s):
            if s > 0:
                return b, half, s - 1
            return (b, 0, SUB - 1) if half == 1 else (b - 1, 1, SUB - 1)

        HALF = (range(0, K // 2), range(K // 2, K))
        HC = K * B // 2
        STEP2 = 2 * SB

        def sums(par, m, at, n):
            at += (m % 2) * SB * B
            return banks[2 * par + m // 2][:, at:at + n]

        def pre(par, j, s):
            return banks[2 * par + j][:, 0:2 * SB * B].rearrange("p (m t b) -> p m t b", m=2, t=SB)[:, :, s, :]

        EPS_D, EPS_N = 1e-8, 1e-5
        LOADS = 5
        AUX_LOADS = 8
        ACC = banks[0:2]
        TRB = banks[2:4]
        XCB = banks[4:6]
        LGB = banks[6:8]

        @block.sync
        def _(sp):
            for dst, src in ((wh, wh_t), (wz, wz_t), (gb_row[0:1, :], gate_bias), (h0, cond_t),
                             (alpha_sb, alpha)):
                sp.dma_start(dst, src).then_inc(loaded, 16)
            for dst, src in ((mod_sb, mod_w), (mod_t, mod_w_t), (nw_t, norm_w_t), (rt_t, router_t),
                             (qw_words, q_weight_t), (vecs[:, 0:2 * K], q_vecs),
                             (nw_bc, norm_w_row.broadcast_to([P, H])), (rb_sb, router_b.broadcast_to([P, E]))):
                sp.dma_start(dst, src).then_inc(aux_in, 16)

            def load_block(n, par):
                if not (isinstance(n, int) and n < 2):
                    sp.wait_ge(zl_ready, n - 1)
                    sp.sem_inc(load_turn, 1)
                    sp.wait_ge(xmax_taken, K * (n - 1))
                    sp.sem_inc(load_turn, 1)
                    sp.wait_ge(gate_ready, (n - 2) * STEP2 + 1)
                sp.dma_start(xblk[par].rearrange("p k t b -> p (k t b)"),
                             x_scan[:, bass.ds(n * (SB * K * B), SB * K * B)]).then_inc(xblk_in[par], 16)

            load_block(0, 0)
            load_block(1, 1)
            sp.wait_ge(parts_ready, 1)
            for n, part in enumerate(gb_part):
                sp.dma_start(gb_parts[n:n + 1, :], part[0:1, :]).then_inc(parts_in, 16)
            sp.wait_ge(d_row_ready, 1)
            sp.dma_start(d_dram, d_flat[0:B, 0:H]).then_inc(d_row_stored, 16)
            sp.wait_ge(d_row_stored, 16)
            sp.dma_start(d_flat, d_dram.rearrange("b o -> (b o)").rearrange("(x n) -> x n", x=1).broadcast_to(
                [P, B * H])).then_inc(d_rows_in, 16)
            with sp.Fori(1, NBLK // 2) as i:
                for par in range(2):
                    load_block(2 * i + par, par)

            with sp.Fori(0, B) as b:
                for s in range(2 * SUB):
                    u, par = b * (2 * SUB) + s, s % 2
                    sp.wait_ge(orow_ready, u + 1)
                    sp.dma_start(out[bass.ds(u * P, P), :], orow[par]).then_inc(out_stored[par], 16)
                    sp.wait_ge(lo_row_ready, u + 1)
                    sp.dma_start(xn_rows[bass.ds(u * P, P), :], xn_both(b, s // SUB, s % SUB)).then_inc(xn_stored[par], 16)

            sp.wait_ge(idx_ready, E)

            def load_layer(src, e, rows, layer):
                if not (isinstance(e, int) and e == 0 and layer == 0):
                    sp.wait_ge(w_lo_ready, (2 * e + layer) * F)
                for q in range(4):
                    n = F * H // 4
                    sp.dma_start(raw.rearrange("p f n -> p (f n)")[:, q * n:(q + 1) * n],
                                 src[bass.ds(rows, P), q * n:(q + 1) * n]).then_inc(raw_in[q], 16)

            def load_expert(e, par):
                rows = e * P if isinstance(e, int) else sp.snap(e * P)
                if not isinstance(e, int):
                    sp.wait_ge(mid_f32_ready, (e - 1) * (2 * F))
                    sp.sem_inc(load_turn, 1)
                    sp.wait_ge(y_sum, (e - 1) * CT)
                    sp.sem_inc(load_turn, 1)
                sp.dma_start(fc1_bias[par], fc1_b[bass.ds(rows, P), :]).then_inc(bias_in[par], 16)
                sp.dma_start(fc2_bias[par], fc2_b[bass.ds(e, 1), :].broadcast_to([P, H])).then_inc(bias_in[par], 16)
                load_layer(fc1_t, e, rows, 0)
                load_layer(fc2_t, e, rows, 1)

            load_expert(0, 0)
            load_expert(1, 1)
            with sp.Fori(1, E // 2) as i:
                load_expert(2 * i, 0)
                load_expert(2 * i + 1, 1)
            sp.wait_ge(out_stored[0], 16 * NT // 2)
            sp.wait_ge(out_stored[1], 16 * NT // 2)
            for c in range(4):
                sp.wait_ge(ye_stored[c], 16 * E * CT // 4)

        def pe_block(n, par, more=True):
            queue = zw_products(1 - par, xblk[1 - par]) if more else []
            for s in range(SB):
                def product(w, h, ms, ks):
                    for m in ms:
                        for k in ks:
                            ins = nc.tensor.matmul(sums(par, m, s * B, B), w[:, k, m * P:(m + 1) * P], h[:, k, :],
                                                   start=False, stop=False, skip_group_check=True)
                    return ins
                at = n * STEP2 + 2 * s
                nc.tensor.wait_ge(hi_ready, at + 1)
                product(wh_hi, h_hi, HALF[0], HALF[0])
                product(wh_lo, h_hi, HALF[0], HALF[0])
                product(wh_hi, h_hi, HALF[1], HALF[0])
                product(wh_lo, h_hi, HALF[1], HALF[0])
                nc.tensor.wait_ge(lo_ready, at + 1)
                product(wh_hi, h_lo, HALF[0], HALF[0])
                nc.tensor.wait_ge(hi_ready, at + 2)
                product(wh_hi, h_hi, HALF[0], HALF[1])
                product(wh_lo, h_hi, HALF[0], HALF[1])
                nc.tensor.wait_ge(lo_ready, at + 2)
                product(wh_hi, h_lo, HALF[0], HALF[1]).then_inc(pre_ready, 1)
                product(wh_hi, h_lo, HALF[1], HALF[0])
                product(wh_hi, h_hi, HALF[1], HALF[1])
                product(wh_lo, h_hi, HALF[1], HALF[1])
                product(wh_hi, h_lo, HALF[1], HALF[1]).then_inc(pre_ready, 1)
                if more:
                    if s == 0:
                        nc.tensor.wait_ge(xblk_in[1 - par], zw_in_value(n, par))
                    queue.pop(0)()

        def zw_in_value(n, par):
            if isinstance(n, int):
                return 16 * ((n + 1) // 2 + 1)
            return 8 * (n - par) + 16 * (par + 1)

        def zw_products(par, x):
            todo = []
            for m in range(K):
                for k in range(K):
                    def prod(m=m, k=k):
                        if k == 0:
                            nc.tensor.matmul(sums(par, m, 0, SB * B), gb_parts[0:3, m * P:(m + 1) * P],
                                             ones_b[0:3, 0:SB * B], start=(m % 2 == 0), stop=False,
                                             skip_group_check=True)
                        nc.tensor.matmul(sums(par, m, 0, SB * B), wz[:, k, m * P:(m + 1) * P],
                                         x[:, k, :, :].rearrange("p t b -> p (t b)"),
                                         start=False, stop=False, skip_group_check=True)
                    todo.append(prod)
            return todo

        CHUNK_AT = {0: (0, 1), 1: (2,), 2: (3,)}
        HI_AT = {0: (0,), 1: (1,), 2: (2,), 3: (3,)}
        LO_AT = {1: (0, 1), 2: (2,), 3: (3,)}

        def pe_quant(t, chunks):
            for m in chunks:
                if m == 0:
                    nc.tensor.wait_ge(q_ready, t + 1)
                if not (isinstance(t, int) and t == 0 and m < 2):
                    nc.tensor.wait_ge(ffn_ready, t * K + m - 1)
                for k in range(K):
                    ins = nc.tensor.matmul(ACC[m % 2][:, :], qw_sb[:, k, m * P:(m + 1) * P], q_sb[:, k, :],
                                           start=(k == 0), stop=(k == K - 1))
                ins.then_inc(acc_ready, 1)

        PARTS = ((0, 0), (0, 1), (1, 0))

        def pe_tile(b, half, more=True):
            t = b * 2 + half
            if more:
                pe_quant(t + 1, CHUNK_AT[0])
            nc.tensor.wait_ge(x_lo_ready, (t + 1) * K)
            if isinstance(t, int) and t == 0:
                nc.tensor.wait_ge(mod_ready, 1)
            x = xt[half]
            for s in range(SUB):
                u, par = t * SUB + s, s % 2
                first = isinstance(t, int) and t == 0 and s < 2
                if more and s > 0:
                    pe_quant(t + 1, CHUNK_AT.get(s, ()))
                if not first:
                    nc.tensor.wait_ge(y_ready, u - 1)
                def product(dst, weights):
                    for k in range(K):
                        for hx, hw in PARTS:
                            ins = nc.tensor.matmul(dst, x_operand(b, half, s, hx, k), weights[:, hw, k, :],
                                                   start=(k == 0 and (hx, hw) == PARTS[0]),
                                                   stop=(k == K - 1 and (hx, hw) == PARTS[-1]))
                    return ins

                ins = product(XCB[par][:, :], mod_hl)
                ins.then_inc(xc_ready, 1)
                if not first:
                    nc.tensor.wait_ge(lg_used, u - 1)
                product(LGB[par][:, 0:B * E], route_hl).then_inc(lg_ready, 1)
                if not first:
                    nc.tensor.wait_ge(orow_ready, u - 1)
                for k in range(K):
                    ins = nc.tensor.transpose(TRB[par][:, k * P:(k + 1) * P], x[:, k, s * P:(s + 1) * P], ident)
                ins.then_inc(tr_ready, 1)

        def pe_xe_t(e, c):
            nc.tensor.wait_ge(xe_in[c % 4], e * 32 + 16 * (c // 4 + 1))
            if not (isinstance(e, int) and e == 0 and c < 2):
                nc.tensor.wait_ge(xtr_moved, e * CT + c - 1)
            for n in range(2 * K):
                ins = nc.tensor.transpose(banks[c % 2][:, :].bitcast(f16)[:, n * P:(n + 1) * P],
                                          xe_row[c % 4][:, n * P:(n + 1) * P], ident_h)
            ins.then_inc(xtr_ready, 1)

        def pe_expert(e, more=True):
            nc.tensor.wait_ge(w_lo_ready, (2 * e + 1) * F)
            for f in range(F):
                for half in range(2):
                    j = 2 * f + half
                    if j < 2:
                        nc.tensor.wait_ge(xtr_moved, e * CT + (half + 1) * (CT // 2))
                    if not (isinstance(e, int) and e == 0 and j < 4):
                        nc.tensor.wait_ge(mid_f32_ready, e * (2 * F) + j - 3)
                    for k in range(K):
                        for a, b in PARTS:
                            ins = nc.tensor.matmul(banks[4 + j % 4][:, :], fc1_hl[:, a, f, k, :],
                                                   xe_t[:, b, k, half * 512:(half + 1) * 512],
                                                   start=(k == 0 and (a, b) == (0, 0)),
                                                   stop=(k == K - 1 and (a, b) == (1, 0)))
                    ins.then_inc(mid_pre, 1)
            nc.tensor.wait_ge(mid_ready, (e + 1) * (2 * F))
            nc.tensor.wait_ge(w_lo_ready, (2 * e + 2) * F)
            for c in range(CT):
                if more:
                    pe_xe_t(e + 1, c)
                if not (isinstance(e, int) and e == 0 and c < 2):
                    nc.tensor.wait_ge(y_sum, e * CT + c - 1)
                for f in range(F):
                    for a, b in PARTS:
                        ins = nc.tensor.matmul(banks[2 + c % 2][:, :], mid[:, a, f, c * P:(c + 1) * P],
                                               fc2_hl[:, b, f, :], start=(f == 0 and (a, b) == (0, 0)),
                                               stop=(f == F - 1 and (a, b) == (1, 0)))
                ins.then_inc(y_pre, 1)

        def pe_prefix(n):
            nc.tensor.wait_ge(flag_ready, n + 1)
            nc.tensor.matmul(banks[2][:, :], tri, flags_row, start=True, stop=True)
            nc.tensor.matmul(banks[3][:, :], ones_b, flags_row, start=True, stop=True).then_inc(rank_done, 1)

        @block.tensor
        def _(pe):
            pe.wait_ge(aux_ready, 1)
            for m in range(K):
                for k in range(K):
                    ins = nc.tensor.matmul(banks[5][:, m * B:(m + 1) * B], mod_sq[:, k, m * P:(m + 1) * P],
                                           ysq[:, k, :], start=(m == 0 and k == 0), stop=(m == K - 1 and k == K - 1),
                                           skip_group_check=True)
            ins.then_inc(aux_done, 1)
            for k in range(K):
                ins = nc.tensor.matmul(banks[4][0:B, :], ysq[:, k, :], mod_sq[:, k, :],
                                       start=(k == 0), stop=(k == K - 1))
            ins.then_inc(aux_done, 1)

            pe.wait_ge(split_ready, 1)
            pe.wait_ge(xblk_in[0], 16)
            pe.wait_ge(parts_in, 16 * 3)
            for f in zw_products(0, xblk[0]):
                f()
            pe.wait_ge(aux_ready, 2)
            for ic in range(K):
                for k in range(K):
                    ins = nc.tensor.matmul(banks[6][:, ic * B * E:(ic + 1) * B * E],
                                           mod_t[:, k, ic * P:(ic + 1) * P], g_t[:, k, :, :],
                                           start=(ic == 0 and k == 0), stop=(ic == K - 1 and k == K - 1),
                                           skip_group_check=True)
            ins.then_inc(aux_done, 1)
            for m in range(K):
                for k in range(K):
                    nc.tensor.matmul(sums(0, m, 0, B), wh[:, k, m * P:(m + 1) * P],
                                     h0[:, k, :], start=False, stop=False, skip_group_check=True)
            with pe.Fori(0, NBLK // 2 - 1) as i:
                pe_block(2 * i, 0)
                pe_block(2 * i + 1, 1)
            pe_block(NBLK - 2, 0)
            pe_block(NBLK - 1, 1, more=False)

            pe.wait_ge(gate_ready, 2 * S)
            pe.wait_ge(ident_ready, 2)
            pe_quant(0, range(K))
            pe_tile(0, 0)
            pe_tile(0, 1)
            with pe.Fori(1, B - 1) as b:
                pe_tile(b, 0)
                pe_tile(b, 1)
            pe_tile(B - 1, 0)
            pe_tile(B - 1, 1, more=False)

            with pe.Fori(0, BITS // ROUNDS) as i:
                for n in range(ROUNDS):
                    pe.wait_ge(cnt_ready, i * ROUNDS + n + 1)
                    nc.tensor.matmul(banks[0][:, 0:E], ones_b, cnt, start=True, stop=True).then_inc(count_done, 1)
            pe.wait_ge(cnt_ready, BITS + 1)
            nc.tensor.matmul(banks[0][:, 0:E], ones_b, cnt, start=True, stop=True).then_inc(count_done, 1)
            pe_prefix(0)
            pe_prefix(1)
            with pe.Fori(0, E // 2) as i:
                for par in range(2):
                    pe.wait_ge(hot_ready, 2 * i + par + 1)
                    for t in range(NT):
                        ins = nc.tensor.matmul(banks[4 + par][:, 0:GATHER * CT], onehot[par][:, t, :],
                                               carried[par][:, t, :, :], start=(t == 0), stop=(t == NT - 1))
                    ins.then_inc(hot_used, 1)

            for c in range(CT):
                pe_xe_t(0, c)
            pe_expert(0)
            with pe.Fori(1, E - 1) as e:
                pe_expert(e)
            pe_expert(E - 1, more=False)

        def act_block(n, par, unscale):
            for s in range(SB):
                at = n * STEP2 + 2 * s
                for j in range(2):
                    nc.scalar.wait_ge(pre_ready, at + j + 1)
                    nc.scalar.activation(gate[:, j * HC:(j + 1) * HC, 1].rearrange("p (k b) -> p k b", b=B),
                                         pre(par, j, s), ACT.Sigmoid,
                                         scale=unscale).then_inc(gate_ready, 1)
                for j in range(2):
                    v = hv[:, j * HC:(j + 1) * HC, 1]
                    nc.scalar.wait_ge(v_ready, at + j + 1)
                    nc.scalar.activation(h_hi_flat[:, j * HC:(j + 1) * HC], v, ACT.Tanh).then_inc(hi_ready, 1)
                    if s == 0 and j == 0 and not (isinstance(n, int) and n < 2):
                        nc.scalar.wait_ge(states_moved, n - 1)
                        nc.scalar.wait_ge(max_taken, 2 * (n - 1))
                    nc.scalar.activation(hring_flat[par][:, s, j * HC:(j + 1) * HC], v,
                                         ACT.Tanh).then_inc(h_ready, 1)

        def act_chunks(t, chunks):
            for m in chunks:
                nc.scalar.wait_ge(acc_ready, t * K + m + 1)
                if not (isinstance(t, int) and t == 0 and m < 2):
                    nc.scalar.wait_ge(xp_ready, t * K + m - 1)
                nc.scalar.activation(ffn[m % 2], ACC[m % 2][:, :], ACT.Identity, bias=vecs[:, K + m:K + m + 1],
                                     scale=vecs[:, 2 * K + m:2 * K + m + 1]).then_inc(ffn_ready, 1)

        def after(b, half):
            return (b, 1) if half == 0 else (b + 1, 0)

        def act_x_hi(b, half, t, chunks):
            for k in chunks:
                nc.scalar.wait_ge(xp_ready, t * K + k + 1)
                nc.scalar.sem_inc(act_turn, 1)
                nc.scalar.activation(x_part(b, half, 0, k), xt[half][:, k, :].rearrange("p (s c) -> p s c", c=P),
                                     ACT.Copy, scale=ys_scaled[:, bass.ds(b + k * B, 1)]).then_inc(x_hi_ready, 1)

        def act_hi(b, half, s, u, par):
            nc.scalar.wait_ge(xn_ready, u + 1)
            nc.scalar.sem_inc(act_turn, 1)
            nc.scalar.activation(xn_part(b, half, s, 0), yrow[par], ACT.Copy).then_inc(hi_row_ready, 1)

        def act_tile(b, half, more=True):
            t = b * 2 + half
            for s in range(SUB):
                u, par = t * SUB + s, s % 2
                if more:
                    act_chunks(t + 1, CHUNK_AT.get(s, ()))
                nc.scalar.wait_ge(y_ready, u + 1)
                if not (isinstance(t, int) and t == 0 and s < 2):
                    nc.scalar.wait_ge(rstd_ready, u - 1)
                nc.scalar.wait_ge(lg_ready, u + 1)
                nc.scalar.sem_inc(act_turn, 1)
                nc.scalar.activation(spent_states(b, half, s), yrow[par], ACT.Square, accum_out=ss[:, par:par + 1]).then_inc(sq_ready, 1)
                nc.scalar.wait_ge(sq_ready, u + 1)
                nc.scalar.activation(ss[:, 2 + par:3 + par], ss[:, par:par + 1], ACT.Sqrt, bias=small[:, 11:12],
                                     scale=1.0 / H).then_inc(root_ready, 1)
                if not (isinstance(t, int) and t == 0 and s == 0):
                    act_hi(*before(b, half, s), u - 1, 1 - par)
                if more:
                    act_x_hi(*after(b, half), t + 1, HI_AT.get(s, ()))
                nc.scalar.wait_ge(tr_ready, u + 1)
                if not (isinstance(t, int) and t == 0 and s < 2):
                    nc.scalar.wait_ge(out_stored[par], out_value(b, half, s))
                nc.scalar.activation(orow[par], TRB[par][:, :], ACT.Copy).then_inc(orow_ready, 1)

        def out_value(b, half, s):
            return b * (16 * SUB) + 16 * ((half * SUB + s) // 2)

        FC2_MAX_AT = {j: (j - 2,) for j in range(2, 2 + F)}
        FC2_RED_AT, FC2_SCALE_AT = 2 + F, 5 + F
        FC2_SPLIT_AT = {22 + n: (2 * n, 2 * n + 1) for n in range(F // 2)}
        FC1_MAX_AT = {c: range(4 * c, 4 * c + 4) for c in range(4)}
        FC1_RED_AT, FC1_SCALE_AT = 3, 4
        FC1_SPLIT_AT = {4: range(0, 5), 5: range(5, 11), 6: range(11, F)}

        def bias_value(e, par):
            return (e - par) * 16 + 32

        @block.scalar
        def _(act):
            act.wait_ge(aux_done, 1)
            act.wait_ge(eps_ready, 1)
            nc.scalar.activation(d_t.rearrange("p k b -> p (k b)"), banks[5][:, 0:K * B], ACT.Sqrt,
                                 bias=small[:, 10:11]).then_inc(aux_root, 1)
            act.wait_ge(aux_done, 2)
            nc.scalar.activation(d_flat[0:B, 0:H], banks[4][0:B, :], ACT.Sqrt,
                                 bias=small[0:B, 10:11]).then_inc(row_rooted, 1)
            act.wait_ge(split_ready, 1)
            unscale = act.alloc_register("unscale")
            act.reg_load(unscale, small[0:1, 1:2].bitcast(i32))
            act_block(0, 0, unscale)
            act_block(1, 1, unscale)
            with act.Fori(1, NBLK // 2) as i:
                act_block(2 * i, 0, unscale)
                act_block(2 * i + 1, 1, unscale)

            act.wait_ge(hmax_ready, 1)
            act_chunks(0, range(K))
            act.wait_ge(ys_ready, 1)
            act_x_hi(0, 0, 0, range(K))
            act_tile(0, 0)
            act_tile(0, 1)
            with act.Fori(1, B - 1) as b:
                act_tile(b, 0)
                act_tile(b, 1)
            act_tile(B - 1, 0)
            act_tile(B - 1, 1, more=False)
            act_hi(B - 1, 1, SUB - 1, NT - 1, (NT - 1) % 2)

            act.wait_ge(logit_ready, 1)
            nc.scalar.activation(probs, probs, ACT.Exp).then_inc(exp_ready, 1)

            def w_hi(r, f, layer):
                dst = (fc1_hl[:, 0, f].rearrange("p k n -> p (k n)"), fc2_hl[:, 0, f])[layer]
                nc.scalar.activation(dst, raw[:, f, :], ACT.Copy,
                                     scale=scales[:, 2 * layer:2 * layer + 1]).then_inc(w_hi_ready, 1)

            def move_xe(e, c):
                nc.scalar.wait_ge(xtr_ready, e * CT + c + 1)
                nc.scalar.activation(xe_t.rearrange("p h k c -> p (h k) c")[:, :, c * P:(c + 1) * P],
                                     banks[c % 2][:, :].bitcast(f16).rearrange("p (n c) -> p n c", c=P),
                                     ACT.Copy).then_inc(xtr_moved, 1)

            def act_expert(e, par, more=True):
                nc.scalar.wait_ge(bias_in[par], bias_value(e, par))
                for j in range(2 * F):
                    nc.scalar.wait_ge(mid_pre, e * (2 * F) + j + 1)
                    if not (isinstance(e, int) and e == 0 and j < 4):
                        nc.scalar.wait_ge(mid_ready, e * (2 * F) + j - 3)
                    nc.scalar.activation(mid_f32[j % 4], banks[4 + j % 4][:, :],
                                         ACT.Gelu, bias=fc1_bias[par][:, j // 2:j // 2 + 1],
                                         scale=scales[:, 4:5]).then_inc(mid_f32_ready, 1)
                    for f in FC2_SPLIT_AT.get(j, ()):
                        if f == 0:
                            nc.scalar.wait_ge(scale_ready, 2 * e + 2)
                            if not (isinstance(e, int) and e == 0):
                                nc.scalar.wait_ge(y_pre, e * CT)
                        w_hi(2 * e + 1, f, 1)
                if more:
                    for c in range(CT):
                        move_xe(e + 1, c)
                        for f in FC1_SPLIT_AT.get(c, ()):
                            if f == 0:
                                nc.scalar.wait_ge(scale_ready, 2 * e + 3)
                            w_hi(2 * e + 2, f, 0)

            act.wait_ge(scale_ready, 1)
            for f in range(F):
                w_hi(0, f, 0)
            for c in range(CT):
                move_xe(0, c)
            act_expert(0, 0)
            act_expert(1, 1)
            with act.Fori(1, E // 2 - 1) as i:
                act_expert(2 * i, 0)
                act_expert(2 * i + 1, 1)
            act_expert(E - 2, 0)
            act_expert(E - 1, 1, more=False)

        def dve_block(n, par):
            v = nc.vector
            for s in range(SB):
                at = n * STEP2 + 2 * s
                if s == 0:
                    v.wait_ge(zl_ready, n + 1)
                for j in range(2):
                    c = slice(j * HC, (j + 1) * HC)
                    v.wait_ge(gate_ready, at + j + 1)
                    v.wait_ge(lh_ready, at + j + 1)
                    v.tensor_tensor_scan(hv[:, c, :].rearrange("p c w -> p (c w)"),
                                         gate[:, c, :].rearrange("p c w -> p (c w)"),
                                         zl[par][:, s, c, :].rearrange("p c w -> p (c w)"), 0.0,
                                         ALU.mult, ALU.add).then_inc(v_ready, 1)
                for j in range(2):
                    c = slice(j * HC, (j + 1) * HC)
                    hr = hring_flat[par][:, s, c]
                    v.wait_ge(h_ready, at + j + 1)
                    v.tensor_tensor(h_lo_flat[:, c], hr, h_hi_flat[:, c], ALU.subtract).then_inc(lo_ready, 1)
                    nxt = zl[par][:, s + 1, c, 1] if s < SB - 1 else zl[1 - par][:, 0, c, 1]
                    v.tensor_tensor(nxt, hr, leak[:, c], ALU.mult).then_inc(lh_ready, 1)
                if s < K:
                    v.tensor_reduce(xmax[:, bass.ds(K * n + s, 1)], xblk[par][:, s, :, :], AX.XY, ALU.max,
                                    apply_absolute_value=True).then_inc(xmax_taken, 1)
                if s % (SB // 2) == SB // 2 - 1:
                    q = s // (SB // 2)
                    v.tensor_reduce(hmax[:, bass.ds(2 * n + q, 1)],
                                    hring_flat[par][:, q * (SB // 2):(q + 1) * (SB // 2), :], AX.XY, ALU.max,
                                    apply_absolute_value=True).then_inc(max_taken, 1)

        def dve_quant(b, half, t, parts=(0, 1)):
            v = nc.vector
            hb = hs[:, b, :, half * TT:(half + 1) * TT] if isinstance(b, int) else \
                hs[:, bass.ds(b, 1), :, half * TT:(half + 1) * TT].rearrange("p b k t -> p (b k) t")
            if 0 in parts:
                v.tensor_scalar(hb, hb, vecs[:, 3 * K:3 * K + 1], ROUND, ALU.mult, ALU.add).then_inc(q_raw, 1)
            if 1 in parts:
                v.wait_ge(q_raw, t + 1)
                if not (isinstance(t, int) and t == 0):
                    v.wait_ge(acc_ready, t * K)
                v.tensor_scalar(q_sb, hb, ROUND, 127.0, ALU.subtract, ALU.min).then_inc(q_ready, 1)

        def dve_add(b, half, t, chunks):
            v = nc.vector
            for m in chunks:
                if m == 0:
                    v.wait_ge(xt_in[half], b * 16 + 16)
                v.wait_ge(ffn_ready, t * K + m + 1)
                v.tensor_tensor(xt[half][:, m, :], xt[half][:, m, :], ffn[m % 2], ALU.add).then_inc(xp_ready, 1)

        def dve_x_lo(b, half, t, chunks):
            v = nc.vector
            for k in chunks:
                v.wait_ge(x_hi_ready, t * K + k + 1)
                v.scalar_tensor_tensor(x_part(b, half, 1, k), xt[half][:, k, :].rearrange("p (s c) -> p s c", c=P),
                                       ys_scaled[:, bass.ds(b + k * B, 1)], x_part(b, half, 0, k),
                                       ALU.mult, ALU.subtract).then_inc(x_lo_ready, 1)

        def dve_finish(b, half, s, u, par):
            v = nc.vector
            v.wait_ge(root_ready, u + 1)
            v.reciprocal(rstd[:, bass.ds(u, 1)], ss[:, 2 + par:3 + par]).then_inc(rstd_ready, 1)
            v.wait_ge(rstd_ready, u + 1)
            v.scalar_tensor_tensor(yrow[par], yrow[par], rstd[:, bass.ds(u, 1)], nw_bc, ALU.mult,
                                   ALU.mult).then_inc(xn_ready, 1)

        def dve_low(b, half, s, u, par):
            v = nc.vector
            v.wait_ge(hi_row_ready, u + 1)
            v.tensor_tensor(xn_part(b, half, s, 1), yrow[par], xn_part(b, half, s, 0),
                            ALU.subtract).then_inc(lo_row_ready, 1)
            v.wait_ge(lg_ready, u + 1)
            v.tensor_scalar(probs[:, bass.ds(u * E, E)], LGB[par][:, bass.ds(b * E, E)], rstd[:, bass.ds(u, 1)],
                            small[:, 49:50], ALU.mult, ALU.mult).then_inc(lg_used, 1)

        def dve_tile(b, half, quant=True, add=True):
            v = nc.vector
            t = b * 2 + half
            nb, nh = (b, 1) if half == 0 else (b + 1, 0)
            for s in range(SUB):
                u, par = t * SUB + s, s % 2
                v.wait_ge(xc_ready, u + 1)
                if not (isinstance(t, int) and t == 0 and s < 2):
                    v.wait_ge(lo_row_ready, u - 1)
                v.tensor_tensor(yrow[par], XCB[par][:, :], drow(b), ALU.mult).then_inc(y_ready, 1)
                if not (isinstance(t, int) and t == 0 and s == 0):
                    dve_finish(*before(b, half, s), u - 1, 1 - par)
                if add:
                    dve_add(nb, nh, t + 1, CHUNK_AT.get(s, ()))
                if quant and s >= 2:
                    dve_quant(b + 1, half, t + 2, (s - 2,))
                if add and s < SUB - 1:
                    dve_x_lo(nb, nh, t + 1, LO_AT.get(s, ()))
                if not (isinstance(t, int) and t == 0 and s == 0):
                    dve_low(*before(b, half, s), u - 1, 1 - par)
                if add and s == SUB - 1:
                    dve_x_lo(nb, nh, t + 1, LO_AT[s])

        def drow(b):
            return d_flat[:, bass.ds(b * H, H)]

        def pow2(largest, scale, inverse, tmp):
            v, tmp = nc.vector, tmp.bitcast(i32)
            yield lambda: v.tensor_scalar(tmp, largest.bitcast(i32), 0x7F800000, None, ALU.bitwise_and)
            yield lambda: v.tensor_scalar(tmp, tmp, float(20 * EXP_ONE), None, ALU.max)
            yield lambda: v.tensor_scalar(scale.bitcast(i32), tmp, -1.0, float(267 * EXP_ONE), ALU.mult, ALU.add)
            yield lambda: v.tensor_scalar(inverse.bitcast(i32), tmp, float(13 * EXP_ONE), None, ALU.subtract)

        def dve_prefix(n):
            v = nc.vector
            v.wait_ge(rank_done, n + 1)
            chain(v.tensor_copy(tot.rearrange("p e t -> p (e t)"), banks[3][:, :]))
            for e in range(E):
                ins = v.tensor_tensor_scan(cum[:, e, :], ones64, tot[:, e, :], 0.0, ALU.mult, ALU.add)
            chain(ins)
            chain(v.tensor_tensor(cum, cum, tot, ALU.subtract))
            chain(v.tensor_tensor(rank.rearrange("p e t -> p (e t)"), banks[2][:, :],
                                  cum.rearrange("p e t -> p (e t)"), ALU.add))

        @block.vector
        def _(dve):
            v = nc.vector
            v.memset(ones_f, 1.0)
            v.memset(ones_b, 1.0)
            v.memset(small[:, 10:11], EPS_D)
            chain(v.memset(small[:, 11:12], EPS_N))
            dve.sem_inc(eps_ready, 1)
            v.wait_ge(loaded, 16 * LOADS)
            v.tensor_reduce(small[:, 2:3], wh, AX.XY, ALU.max, apply_absolute_value=True)
            chain(v.tensor_reduce(small[:, 3:4], wz, AX.XY, ALU.max, apply_absolute_value=True))
            v.tensor_tensor(small[:, 4:5], small[:, 2:3], small[:, 3:4], ALU.max).then_inc(wmax_in, 1)
            v.wait_ge(aux_in, 16 * AUX_LOADS)
            chain(v.tensor_scalar(ys_flat, h0.rearrange("p k b -> p (k b)"), float(H) ** -0.5, None, ALU.mult))
            chain(v.tensor_tensor(ysq, ys, ys, ALU.mult))
            chain(v.tensor_tensor(mod_sq, mod_sb, mod_sb, ALU.mult))
            dve.sem_inc(aux_ready, 1)
            v.wait_ge(wmax_out, 1)
            for ins in pow2(small[:, 5:6], small[:, 0:1], small[:, 1:2], small[:, 6:7]):
                chain(ins())
            v.tensor_scalar(wz, wz, small[:, 0:1], None, ALU.mult)
            chain(v.tensor_scalar(gb_row[0:1, :], gb_row[0:1, :], small[0:1, 0:1], None, ALU.mult))
            for part in gb_part:
                chain(v.tensor_copy(part[0:1, :], gb_row[0:1, :]))
                chain(v.tensor_tensor(gb_row[0:1, :], gb_row[0:1, :], part[0:1, :], ALU.subtract))
            v.sem_inc(parts_ready, 1)
            chain(v.tensor_scalar(wh, wh, small[:, 0:1], None, ALU.mult))
            chain(v.tensor_copy(wh_hi, wh))
            chain(v.tensor_tensor(wh_lo, wh, wh_hi, ALU.subtract))
            chain(v.tensor_scalar(alpha_sb, alpha_sb, -1.0, 1.0, ALU.mult, ALU.add))
            chain(v.tensor_copy(leak.rearrange("p (k b) -> p k b", k=K), bc(alpha_sb[:, :, None], [P, K, B])))
            chain(v.tensor_tensor(zl[0][:, 0, :, 1], leak, h0.rearrange("p k b -> p (k b)"), ALU.mult))
            chain(v.memset(gate, 0.0))
            v.memset(h_lo, 0.0)
            chain(v.memset(h_hi, 0.0))
            for x in (hi_ready, lo_ready, lh_ready):
                dve.sem_inc(x, 2)
            dve.sem_inc(split_ready, 1)
            for k in range(K):
                ins = v.tensor_scalar(rnw[:, k, :], rt_t[:, k, :], nw_t[:, k:k + 1], None, ALU.mult)
            chain(ins)
            v.wait_ge(aux_root, 1)
            chain(v.reciprocal(d_t, d_t))
            for k in range(K):
                ins = v.tensor_tensor(g_t[:, k], bc(d_t[:, k, :, None], [P, B, E]),
                                      bc(rnw[:, k, None, :], [P, B, E]), ALU.mult)
            chain(ins)
            dve.sem_inc(aux_ready, 1)
            v.wait_ge(row_rooted, 1)
            v.reciprocal(d_flat[0:B, 0:H], d_flat[0:B, 0:H]).then_inc(d_row_ready, 1)
            v.tensor_copy(qw_sb, qw_i8)
            v.wait_ge(aux_done, 3)
            for ic in range(K):
                ins = v.tensor_copy(route_sb[:, ic, :], banks[6][:, ic * B * E:(ic + 1) * B * E])
            chain(ins)
            with dve.Fori(0, NBLK // 2) as i:
                dve_block(2 * i, 0)
                dve_block(2 * i + 1, 1)

            chain(v.tensor_reduce(small[:, 16:17], nw_bc, AX.X, ALU.max, apply_absolute_value=True))
            chain(v.tensor_scalar(small[:, 17:18], small[:, 16:17], float(H) ** 0.5, None, ALU.mult))
            for ins in pow2(small[:, 17:18], small[:, 18:19], small[:, 19:20], small[:, 20:21]):
                chain(ins())
            chain(v.tensor_scalar(small[:, 21:22], small[:, 16:17], float(H), None, ALU.mult))
            chain(v.tensor_scalar(nw_bc, nw_bc, small[:, 18:19], None, ALU.mult))

            v.wait_ge(max_taken, 2 * NBLK)
            v.wait_ge(xmax_taken, K * NBLK)
            for n, (part, axes) in enumerate(((xmax, AX.X), (ys_flat, AX.X), (vecs[:, 0:K], AX.X),
                                              (vecs[:, K:2 * K], AX.X), (mod_sb, AX.XY), (route_sb, AX.XY),
                                              (hmax, AX.X))):
                ins = v.tensor_reduce(small[:, 22 + n:23 + n], part, axes, ALU.max, apply_absolute_value=True)
            ins.then_inc(hmax_in, 1)
            v.wait_ge(hmax_out, 1)
            x_top, y_top, qs_top, qb_top, mod_top, route_top, h_top = (small[:, 32 + n:33 + n] for n in range(7))
            chain(v.tensor_scalar(small[:, 14:15], h_top, 1.0 / 127.0, 1e-5, ALU.mult, ALU.max))
            v.reciprocal(vecs[:, 3 * K:3 * K + 1], small[:, 14:15])
            chain(v.tensor_scalar(vecs[:, 2 * K:3 * K], vecs[:, 0:K], small[:, 14:15], None, ALU.mult))
            dve.sem_inc(hmax_ready, 1)
            v.wait_ge(states_moved, NBLK)
            v.wait_ge(d_rows_in, 16)
            dve_quant(0, 0, 0)
            dve_quant(0, 1, 1)
            top = small[:, 47:48]
            chain(v.tensor_tensor(top, small[:, 14:15], qs_top, ALU.mult))
            chain(v.scalar_tensor_tensor(top, top, 127.0 * 127.0 * H, qb_top, ALU.mult, ALU.add))
            chain(v.tensor_scalar(top, top, x_top, 1e-20, ALU.add, ALU.max))
            chain(v.tensor_tensor(top, top, y_top, ALU.mult))
            for largest, at in ((top, 40), (mod_top, 43), (route_top, 50)):
                for ins in pow2(largest, small[:, at:at + 1], small[:, at + 1:at + 2], small[:, at + 2:at + 3]):
                    chain(ins())
            v.tensor_tensor(small[:, 48:49], small[:, 41:42], small[:, 44:45], ALU.mult)
            v.tensor_tensor(small[:, 49:50], small[:, 41:42], small[:, 51:52], ALU.mult)
            v.tensor_scalar(ys_scaled, ys_flat, small[:, 40:41], None, ALU.mult).then_inc(ys_ready, 1)
            dve_add(0, 0, 0, range(K))
            v.tensor_scalar(route_sb, route_sb, small[:, 50:51], None, ALU.mult)
            chain(v.tensor_scalar(mod_sb, mod_sb, small[:, 43:44], None, ALU.mult))
            v.tensor_copy(route_hl[:, 0], route_sb)
            chain(v.tensor_copy(mod_hl[:, 0], mod_sb))
            v.tensor_tensor(route_hl[:, 1], route_sb, route_hl[:, 0], ALU.subtract)
            chain(v.tensor_tensor(mod_hl[:, 1], mod_sb, mod_hl[:, 0], ALU.subtract))
            v.sem_inc(mod_ready, 1)
            dve_x_lo(0, 0, 0, range(K))
            chain(v.tensor_scalar(d_flat, d_flat, small[:, 48:49], None, ALU.mult))
            dve_tile(0, 0)
            dve_tile(0, 1)
            with dve.Fori(1, B - 1) as b:
                dve_tile(b, 0)
                dve_tile(b, 1)
            dve_tile(B - 1, 0, quant=False)
            dve_tile(B - 1, 1, quant=False, add=False)
            dve_finish(B - 1, 1, SUB - 1, NT - 1, (NT - 1) % 2)
            dve_low(B - 1, 1, SUB - 1, NT - 1, (NT - 1) % 2)

            v.wait_ge(iota_ready, 6)
            v.wait_ge(lg_used, NT)
            pr = probs.rearrange("p (t e) -> p t e", t=NT)
            chain(v.tensor_tensor(pr, pr, bc(rb_sb[:, None, :], [P, NT, E]), ALU.add))
            chain(v.tensor_reduce(gsum, pr, AX.X, ALU.max))
            v.tensor_tensor(pr, pr, bc(gsum[:, :, None], [P, NT, E]), ALU.subtract).then_inc(logit_ready, 1)
            v.wait_ge(exp_ready, 1)
            chain(v.tensor_reduce(gsum, pr, AX.X, ALU.add))
            chain(v.reciprocal(gsum, gsum))
            pe_view = p_et.rearrange("p e t -> p t e")
            chain(v.tensor_tensor(pe_view, pr, bc(gsum[:, :, None], [P, NT, E]), ALU.mult))

            v.memset(thr, 0)
            chain(v.memset(bit, 1 << (BITS - 1)))

            def count(flag, n):
                with nc.allow_low_precision(reason="at most 64 flags, which bf16 holds exactly"):
                    nc.vector.tensor_reduce(cnt, flag, AX.X, ALU.add).then_inc(cnt_ready, 1)
                nc.vector.wait_ge(count_done, n + 1)

            STEPS = 6

            def link(ins, i, j):
                ins.then_inc(dve_loop, 1)
                nc.vector.wait_ge(dve_loop, i * STEPS + j)

            with dve.Fori(0, BITS // ROUNDS) as turn:
                for n in range(ROUNDS):
                    i = turn * ROUNDS + n
                    link(v.tensor_scalar(cand, thr, bit[:, 0:1], None, ALU.bitwise_or), i, 1)
                    link(v.tensor_tensor(flags, p_et, bc(cand.bitcast(f32)[:, :, None], [P, E, NT]), ALU.is_ge), i, 2)
                    count(flags, i)
                    link(v.tensor_scalar(hit, banks[0][:, 0:E], float(CAP), -1.0, ALU.is_ge, ALU.mult), i, 3)
                    link(v.tensor_scalar(hit, hit, bit[:, 0:1], None, ALU.bitwise_and), i, 4)
                    link(v.tensor_tensor(thr, thr, hit, ALU.bitwise_or), i, 5)
                    link(v.tensor_scalar(bit, bit, 1, None, ALU.logical_shift_right), i, 6)

            thr_b = bc(thr.bitcast(f32)[:, :, None], [P, E, NT])
            chain(v.tensor_tensor(flags, p_et, thr_b, ALU.is_gt))
            count(flags, BITS)
            chain(v.tensor_scalar(need, banks[0][:, 0:E], -1.0, float(CAP), ALU.mult, ALU.add))
            chain(v.tensor_copy(flags2, flags))
            v.tensor_tensor(flags, p_et, thr_b, ALU.is_equal).then_inc(flag_ready, 1)
            dve_prefix(0)
            chain(v.tensor_tensor(rank, rank, bc(need[:, :, None], [P, E, NT]), ALU.is_lt))
            chain(v.tensor_tensor(rank, rank, flags, ALU.mult))
            v.tensor_tensor(flags, flags2, rank, ALU.add).then_inc(flag_ready, 1)
            dve_prefix(1)
            chain(v.tensor_tensor(wsel, flags, p_et, ALU.mult))
            chain(v.tensor_reduce(gsum, wsel.rearrange("p e t -> p t e"), AX.X, ALU.add))
            chain(v.tensor_scalar(gsum, gsum, 1e-9, None, ALU.max))
            chain(v.reciprocal(gsum, gsum))
            chain(v.tensor_tensor(wsel, wsel, bc(gsum[:, None, :], [P, E, NT]), ALU.mult))
            chain(v.tensor_scalar(cum, flags, -float(T), float(T), ALU.mult, ALU.add))
            chain(v.tensor_tensor(slot_i, rank, cum, ALU.add))
            chain(v.tensor_scalar(part_i, slot_i, P - 1, None, ALU.bitwise_and))
            chain(v.tensor_copy(slot_lo, part_i))
            chain(v.tensor_scalar(part_i, slot_i, 7, None, ALU.logical_shift_right))
            chain(v.tensor_copy(slot_hi, part_i))
            v.tensor_copy(vals[:, :, :, 0], bc(row_i[:, None, :], [P, E, NT]))
            v.tensor_copy(vals[:, :, :, 1], bc(tile_i[:, None, :], [P, E, NT]))
            chain(v.tensor_copy(vals[:, :, :, 2], wsel))
            chain(v.tensor_tensor(wres, wsel, vals[:, :, :, 2], ALU.subtract))
            chain(v.tensor_copy(vals[:, :, :, 3], wres))
            chain(v.tensor_tensor(vals[:, :, :, 4], wres, vals[:, :, :, 3], ALU.subtract))
            chain(v.tensor_copy(iota_p, iota_i))
            chain(v.tensor_copy(iota_c, iota_i[:, 0:CT]))

            def lists(e, par):
                lo = slot_lo.rearrange("p e t -> p (e t)")[:, bass.ds(e * NT, NT)]
                hi = slot_hi.rearrange("p e t -> p (e t)")[:, bass.ds(e * NT, NT)]
                va = vals_flat[:, bass.ds(e * (NT * GATHER), NT * GATHER)].rearrange("p (t v) -> p t v", v=GATHER)
                if not (isinstance(e, int) and e < 2):
                    v.wait_ge(hot_used, e - 1)
                v.tensor_tensor(onehot[par], bc(iota_p[:, None, :], [P, NT, P]), bc(lo[:, :, None], [P, NT, P]),
                                ALU.is_equal)
                if not (isinstance(e, int) and e == 0):
                    v.wait_ge(hot_ready, e)
                v.tensor_tensor(hi_hot, bc(iota_c[:, None, :], [P, NT, CT]), bc(hi[:, :, None], [P, NT, CT]),
                                ALU.is_equal).then_inc(hi_hot_ready, 1)
                v.wait_ge(hi_hot_ready, e + 1)
                v.tensor_tensor(carried[par], bc(hi_hot[:, :, None, :], [P, NT, GATHER, CT]),
                                bc(va[:, :, :, None], [P, NT, GATHER, CT]), ALU.mult).then_inc(hot_ready, 1)

            def take_list(e, par):
                v.wait_ge(hot_used, e + 1)
                if not isinstance(e, int):
                    v.wait_ge(idx_ready, e)
                v.tensor_copy(got, banks[4 + par][:, 0:GATHER * CT]).then_inc(got_ready, 1)
                v.wait_ge(got_ready, 3 * e + 1)
                g3 = got.rearrange("p (v c) -> p v c", v=GATHER)
                v.tensor_tensor(g3[:, 2, :], g3[:, 2, :], g3[:, 3, :], ALU.add).then_inc(got_ready, 1)
                v.wait_ge(got_ready, 3 * e + 2)
                v.tensor_tensor(w_flat[:, bass.ds(e * CT, CT)], g3[:, 2, :], g3[:, 4, :], ALU.add)
                v.scalar_tensor_tensor(idx_flat[:, bass.ds(e * CT, CT)], g3[:, 1, :], float(P), g3[:, 0, :],
                                       ALU.mult, ALU.add).then_inc(got_ready, 1)
                v.wait_ge(got_ready, 3 * e + 3)
                v.sem_inc(idx_ready, 1)

            lists(0, 0)
            lists(1, 1)
            take_list(0, 0)
            with dve.Fori(1, E // 2) as i:
                lists(2 * i, 0)
                take_list(2 * i - 1, 1)
                lists(2 * i + 1, 1)
                take_list(2 * i, 0)
            take_list(E - 1, 1)

            def current(e, par):
                v.tensor_copy(w_cur[par], w_flat[:, bass.ds(e * CT, CT)])
                v.tensor_copy(idx_cur[par], idx_flat[:, bass.ds(e * CT, CT)]).then_inc(cur_ready, 1)

            sc = [scales[:, n:n + 1] for n in range(16)]
            SCALE_STEPS = 12

            def w_max(e, layer, f):
                r = 2 * e + layer
                if f % 4 == 0:
                    v.wait_ge(raw_in[f // 4], 16 * (r + 1))
                v.tensor_reduce(block_max[:, f:f + 1], raw[:, f, :], AX.X, ALU.max,
                                apply_absolute_value=True).then_inc(max_step, 1)

            def w_reduce(e, layer, par):
                r = 2 * e + layer
                v.wait_ge(max_step, r * (F + 1) + F)
                if layer == 0:
                    v.wait_ge(bias_in[par], bias_value(e, par))
                    v.tensor_reduce(sc[9], fc1_bias[par], AX.X, ALU.max, apply_absolute_value=True)
                v.tensor_reduce(sc[8], block_max, AX.X, ALU.max).then_inc(max_step, 1)
                v.wait_ge(max_step, (r + 1) * (F + 1))
                v.sem_inc(max_in, 1)

            def w_scale(e, layer):
                step, done = (fc1_scale_step, fc2_scale_step)[layer], [0]

                def link(ins):
                    done[0] += 1
                    ins.then_inc(step, 1)
                    v.wait_ge(step, e * SCALE_STEPS + done[0])

                v.wait_ge(max_out, 2 * e + layer + 1)
                for ins in pow2(sc[10], sc[2 * layer], sc[2 * layer + 1], sc[12]):
                    link(ins())
                if layer == 0:
                    link(v.tensor_tensor(sc[4], sc[1], small[:, 19:20], ALU.mult))
                    link(v.scalar_tensor_tensor(sc[13], sc[10], small[:, 21:22], sc[11], ALU.mult, ALU.add))
                    for ins in pow2(sc[13], sc[6], sc[7], sc[12]):
                        link(ins())
                else:
                    link(v.tensor_tensor(sc[5], sc[3], sc[7], ALU.mult))
                while done[0] < SCALE_STEPS:
                    link(v.tensor_copy(sc[14], sc[12]))
                v.sem_inc(scale_ready, 1)

            def w_lo(e, layer, f):
                hl = (fc1_hl, fc2_hl)[layer]
                hi, lo = ((hl[:, n, f].rearrange("p k n -> p (k n)") if layer == 0 else hl[:, n, f])
                          for n in range(2))
                v.wait_ge(w_hi_ready, (2 * e + layer) * F + f + 1)
                v.scalar_tensor_tensor(lo, raw[:, f, :], sc[2 * layer], hi, ALU.mult,
                                       ALU.subtract).then_inc(w_lo_ready, 1)

            def dve_expert(e, par, more=True):
                if more:
                    if not (isinstance(e, int) and e == 0):
                        for c in range(4):
                            v.wait_ge(ye_stored[c], e * 32)
                    current(e + 1, 1 - par)
                for j in range(2 * F):
                    f, cols = j // 2, slice((j % 2) * 512, (j % 2 + 1) * 512)
                    v.wait_ge(mid_f32_ready, e * (2 * F) + j + 1)
                    v.tensor_scalar(mid[:, 0, f, cols], mid_f32[j % 4], sc[6], None,
                                    ALU.mult).then_inc(mid_hi_ready, 1)
                    v.wait_ge(mid_hi_ready, e * (2 * F) + j + 1)
                    v.scalar_tensor_tensor(mid[:, 1, f, cols], mid_f32[j % 4], sc[6], mid[:, 0, f, cols],
                                           ALU.mult, ALU.subtract).then_inc(mid_ready, 1)
                    for f in FC2_MAX_AT.get(j, ()):
                        w_max(e, 1, f)
                    if j == FC2_RED_AT:
                        w_reduce(e, 1, par)
                    if j == FC2_SCALE_AT:
                        w_scale(e, 1)
                    for f in FC2_SPLIT_AT.get(j, ()):
                        w_lo(e, 1, f)
                for c in range(CT):
                    v.wait_ge(y_pre, e * CT + c + 1)
                    if not (isinstance(e, int) and e == 0 and c < 4):
                        v.wait_ge(ye_stored[c % 4], e * 32 + 16 * (c // 4))
                    v.scalar_tensor_tensor(ye[c % 4], banks[2 + c % 2][:, :], sc[5], fc2_bias[par], ALU.mult,
                                           ALU.add).then_inc(y_sum, 1)
                    v.wait_ge(y_sum, e * CT + c + 1)
                    v.tensor_scalar(ye[c % 4], ye[c % 4], w_cur[par][:, c:c + 1], None, ALU.mult).then_inc(ye_ready, 1)
                    if more:
                        for f in FC1_MAX_AT.get(c, ()):
                            w_max(e + 1, 0, f)
                        if c == FC1_RED_AT:
                            w_reduce(e + 1, 0, 1 - par)
                        if c == FC1_SCALE_AT:
                            w_scale(e + 1, 0)
                        for f in FC1_SPLIT_AT.get(c, ()):
                            w_lo(e + 1, 0, f)

            v.wait_ge(idx_ready, E)
            current(0, 0)
            for f in range(F):
                w_max(0, 0, f)
            w_reduce(0, 0, 0)
            w_scale(0, 0)
            for f in range(F):
                w_lo(0, 0, f)
            dve_expert(0, 0)
            dve_expert(1, 1)
            with dve.Fori(1, E // 2 - 1) as i:
                dve_expert(2 * i, 0)
                dve_expert(2 * i + 1, 1)
            dve_expert(E - 2, 0)
            dve_expert(E - 1, 1, more=False)

        def pool_spread(n, par):
            g = nc.gpsimd
            g.wait_ge(xblk_in[par], 16 * (n // 2 + 1) if isinstance(n, int) else 8 * (n - par) + 16)
            if not (isinstance(n, int) and n < 2):
                g.wait_ge(v_ready, (n - 1) * STEP2)
            g.sem_inc(pool_turn, 1)
            g.tensor_copy(zl[par][:, :, :, 0].rearrange("p t (k b) -> p t k b", k=K),
                          xblk[par].rearrange("p k t b -> p t k b")).then_inc(zl_ready, 1)

        def pool_block(n, par):
            g = nc.gpsimd
            g.wait_ge(h_ready, (n + 1) * STEP2)
            g.tensor_copy(hs[:, :, :, bass.ds(n * SB, SB)],
                          hring[par].rearrange("p t k b -> p b k t")).then_inc(states_moved, 1)

        @block.gpsimd
        def _(pool):
            g = nc.gpsimd
            pchain(g.memset(ident, 0.0))
            g.affine_select(out=ident, in_=ident, compare_op=ALU.not_equal, fill=1.0, base=0,
                            pattern=[[-1, P]], channel_multiplier=1).then_inc(ident_ready, 1)
            g.wait_ge(ident_ready, 1)
            g.tensor_copy(ident_h, ident).then_inc(ident_ready, 1)
            g.wait_ge(wmax_in, 1)
            g.partition_all_reduce(small[:, 5:6], small[:, 4:5], P, ABSMAX).then_inc(wmax_out, 1)
            g.wait_ge(split_ready, 1)
            pool_spread(0, 0)
            pool_spread(1, 1)
            with pool.Fori(0, NBLK // 2 - 1) as i:
                for par in range(2):
                    pool_block(2 * i + par, par)
                    pool_spread(2 * i + 2 + par, par)
            pool_block(NBLK - 2, 0)
            pool_block(NBLK - 1, 1)
            g.wait_ge(hmax_in, 1)
            g.partition_all_reduce(small[:, 32:39], small[:, 22:29], P, ABSMAX).then_inc(hmax_out, 1)

            def load_x(b, half):
                t = b * 2 + half
                g.dma_start(xt[half], x_feat3[:, :, bass.ds(t * TT, TT)]).then_inc(xt_in[half], 16)

            g.wait_ge(hmax_out, 1)
            load_x(0, 0)
            load_x(0, 1)
            with pool.Fori(1, B) as b:
                for half in range(2):
                    g.wait_ge(tr_ready, (b * 2 + half - 1) * SUB)
                    load_x(b, half)

            g.wait_ge(lg_used, NT)
            for par in range(2):
                g.wait_ge(xn_stored[par], 16 * NT // 2)
                g.wait_ge(out_stored[par], 16 * NT // 2)
            g.memset(ones64, 1.0).then_inc(iota_ready, 1)
            pchain(g.memset(tri, 1.0))
            g.affine_select(out=tri, in_=tri, compare_op=ALU.is_gt, fill=0.0, base=0, pattern=[[1, P]],
                            channel_multiplier=-1).then_inc(iota_ready, 1)
            g.iota(iota_i, pattern=[[1, P]], base=0, channel_multiplier=0).then_inc(iota_ready, 1)
            g.iota(row_i, pattern=[[0, NT]], base=0, channel_multiplier=1).then_inc(iota_ready, 1)
            g.iota(tile_i, pattern=[[1, NT]], base=0, channel_multiplier=0).then_inc(iota_ready, 1)
            g.wait_ge(iota_ready, 5)
            g.sem_inc(iota_ready, 1)

            def gather(e, par, c):
                if c == 0:
                    g.wait_ge(cur_ready, e + 1)
                if not (isinstance(e, int) and e == 0 and c < 4):
                    g.wait_ge(xtr_ready, e * CT + c - 3)
                g.sem_inc(pool_turn, 1)
                g.indirect_dma_start(xe_row[c % 4], None, xn_rows[:, :],
                                     bass.IndirectOffsetOnAxis(idx_cur[par][:, c:c + 1].bitcast(u32), 0)
                                     ).then_inc(xe_in[c % 4], 16)

            def scatter(e, par, c):
                if c == 0 and not (isinstance(e, int) and e == 0):
                    for n in range(4):
                        g.wait_ge(ye_stored[n], e * 32)
                g.wait_ge(ye_ready, e * CT + c + 1)
                g.sem_inc(pool_turn, 1)
                g.indirect_dma_start(out[:, :],
                                     bass.IndirectOffsetOnAxis(idx_cur[par][:, c:c + 1].bitcast(u32), 0),
                                     ye[c % 4], None, compute_op=ALU.add).then_inc(ye_stored[c % 4], 16)

            def layer_max(r):
                g.wait_ge(max_in, r + 1)
                g.sem_inc(pool_turn, 1)
                g.partition_all_reduce(scales[:, 10:12], scales[:, 8:10], P, ABSMAX).then_inc(max_out, 1)

            def pool_expert(e, par, more=True):
                if more:
                    for c in range(4):
                        gather(e + 1, 1 - par, c)
                layer_max(2 * e + 1)
                for c in range(CT):
                    if more and c < 4:
                        gather(e + 1, 1 - par, c + 4)
                    scatter(e, par, c)
                    if more and c == FC1_RED_AT:
                        layer_max(2 * e + 2)

            for par in range(2):
                g.wait_ge(xn_stored[par], 16 * NT // 2)
                g.wait_ge(out_stored[par], 16 * NT // 2)
            for c in range(4):
                gather(0, 0, c)
            layer_max(0)
            for c in range(4, CT):
                gather(0, 0, c)
            pool_expert(0, 0)
            pool_expert(1, 1)
            with pool.Fori(1, E // 2 - 1) as i:
                pool_expert(2 * i, 0)
                pool_expert(2 * i + 1, 1)
            pool_expert(E - 2, 0)
            pool_expert(E - 1, 1, more=False)


def kernel(x, cond_1024, L0_cond_W, L0_cond_b, L0_cond_alpha, L0_ffn_weight_int8, L0_ffn_weight_scale,
           L0_ffn_bias, L1_cond_weight, L1_ffn_norm_weight, L1_ffn_router_w, L1_ffn_router_b,
           L1_ffn_fc1_w, L1_ffn_fc1_b, L1_ffn_fc2_w, L1_ffn_fc2_b):
    import numpy as np
    import concourse.bacc as bacc
    from concourse import mybir as _mybir
    from concourse.bass_utils import run_bass_kernel_spmd

    B, S, H = x.shape
    P = 128
    K = H // P
    E, FF, _ = L1_ffn_fc1_w.shape
    x, W = np.asarray(x), np.asarray(L0_cond_W)

    def by_part(m):
        m = np.asarray(m)
        n = m.shape[1]
        return np.ascontiguousarray(m.reshape(-1, P, n).transpose(1, 0, 2).reshape(P, -1))

    def cols(v):
        return np.ascontiguousarray(np.asarray(v).reshape(-1, P).T)

    def row(v):
        return np.ascontiguousarray(np.asarray(v).reshape(1, -1))

    fc1 = np.asarray(L1_ffn_fc1_w).reshape(E, FF // P, P, K, P).transpose(0, 4, 1, 3, 2).reshape(E * P, K * FF)
    fc2 = np.asarray(L1_ffn_fc2_w).reshape(E, H, FF // P, P).transpose(0, 3, 2, 1).reshape(E * P, FF // P * H)
    arrays = {
        "x_scan": x.reshape(B, S // 16, 16, K, P).transpose(4, 1, 3, 2, 0).reshape(P, S * K * B),
        "x_feat": x.reshape(B * S, K, P).transpose(2, 1, 0).reshape(P, K * B * S),
        "cond_t": by_part(np.asarray(cond_1024).T),
        "wh_t": by_part(W[:, :H].T),
        "wz_t": by_part(W[:, H:].T),
        "gate_bias": row(L0_cond_b),
        "alpha": cols(L0_cond_alpha),
        "q_weight_t": by_part(np.asarray(L0_ffn_weight_int8).T).view(np.int32),
        "q_vecs": np.concatenate([cols(np.asarray(L0_ffn_weight_scale).reshape(-1)), cols(L0_ffn_bias)], axis=1),
        "mod_w": by_part(L1_cond_weight),
        "mod_w_t": by_part(np.asarray(L1_cond_weight).T),
        "norm_w_t": cols(L1_ffn_norm_weight),
        "norm_w_row": row(L1_ffn_norm_weight),
        "router_t": by_part(np.asarray(L1_ffn_router_w).T),
        "router_b": row(L1_ffn_router_b),
        "fc1_t": fc1,
        "fc1_b": np.asarray(L1_ffn_fc1_b).reshape(E, FF // P, P).transpose(0, 2, 1).reshape(E * P, FF // P),
        "fc2_t": fc2,
        "fc2_b": L1_ffn_fc2_b,
    }
    nc = bacc.Bacc("TRN2", target_bir_lowering=False, num_devices=1)
    arrays = {n: np.ascontiguousarray(a) for n, a in arrays.items()}
    aps = [nc.dram_tensor(f"{n}_dram", a.shape, _mybir.dt.from_np(a.dtype), kind="ExternalInput").ap()
           for n, a in arrays.items()]
    out = nc.dram_tensor("out_dram", (B * S, H), _mybir.dt.float32, kind="ExternalOutput").ap()
    adaln_ffn_kernel(nc, *aps, out)
    r = run_bass_kernel_spmd(nc, [{f"{n}_dram": a for n, a in arrays.items()}], core_ids=[0])
    return r.results[0]["out_dram"].reshape(B, S, H)
```
